# Optimizing a Trainium2 kernel written in Bass

```python
import numpy as np
import jax
import jax.numpy as jnp

def _softmax(x, axis=-1):
    return jax.nn.softmax(x, axis=axis)

def _gelu(x):
    return jax.nn.gelu(x, approximate=True)

def _silu(x):
    return jax.nn.silu(x)

def _sigmoid(x):
    return jax.nn.sigmoid(x)

def _layernorm(x, axis=-1, eps=1e-05):
    m = jnp.mean(x, axis=axis, keepdims=True)
    v = jnp.var(x, axis=axis, keepdims=True)
    return (x - m) / jnp.sqrt(v + eps)

def _scatter_add(tgt, idx, src, axis=0):
    return tgt.at[idx].add(src)

def _segment_sum(src, seg, n):
    return jax.ops.segment_sum(src, seg, n)
kernel_name = 'mk_adaln_d2_jaxref_r8_8c3f34'

def setup_inputs(seed: int=0):
    np.random.seed(seed)
    _w = jnp.asarray

    def _L0_attn_setup():
        import jax, jax.numpy as jnp
        import numpy as np
        import math
        B, S, D_IN, D_KQ, D_OUT = (4, 256, 128, 128, 128)
        key = jax.random.key(seed)
        ks = jax.random.split(key, 7)
        sc = 0.02
        return {'x': jax.random.normal(ks[0], (B, S, D_IN), jnp.float32), 'Wq': jax.random.normal(ks[1], (D_KQ, D_IN), jnp.float32) * sc, 'bq': jax.random.normal(ks[2], (D_KQ,), jnp.float32) * sc, 'Wk': jax.random.normal(ks[3], (D_KQ, D_IN), jnp.float32) * sc, 'bk': jax.random.normal(ks[4], (D_KQ,), jnp.float32) * sc, 'Wv': jax.random.normal(ks[5], (D_OUT, D_IN), jnp.float32) * sc, 'bv': jax.random.normal(ks[6], (D_OUT,), jnp.float32) * sc}
    _L0_attn_in = _L0_attn_setup()

    def _L0_ffn_setup():
        import jax, jax.numpy as jnp
        import numpy as np
        B, S, DIM = (4, 512, 128)
        BASE_COUPLING = 0.1
        NUM_CYCLES = 3

        def _gelu(x):
            return jax.nn.gelu(x, approximate=False)

        def _coupling_net(h, w1, b1, w2, b2, w3, b3, w4, b4):
            h = _gelu(h @ w1 + b1)
            h = _gelu(h @ w2 + b2)
            h = _gelu(h @ w3 + b3)
            return jax.nn.sigmoid(h @ w4 + b4)

        def _global_net(h, w1, b1, w2, b2, w3, b3):
            h = _gelu(h @ w1 + b1)
            h = _gelu(h @ w2 + b2)
            return jax.nn.sigmoid(h @ w3 + b3)

        def _twist(x):
            o_r, o_i, p_r, p_i = jnp.split(x, 4, axis=-1)
            return jnp.concatenate([p_r, -p_i, -o_r, o_i], axis=-1)
        key = jax.random.key(seed)
        ks = jax.random.split(key, 9)
        d = DIM

        def w(k, fan_in, fan_out):
            return jax.random.normal(k, (fan_in, fan_out), dtype=jnp.float32) / np.sqrt(fan_in).astype(np.float32)
        inp = {'x': jax.random.normal(ks[0], (B, S, d), dtype=jnp.float32)}
        cn_dims = [(d, d), (d, d // 2), (d // 2, d // 4), (d // 4, 1)]
        for i, (a, b) in enumerate(cn_dims):
            inp[f'cn_w{i + 1}'] = w(ks[1 + i], a, b)
            inp[f'cn_b{i + 1}'] = jnp.zeros((b,), dtype=jnp.float32)
        gc_dims = [(d, d // 2), (d // 2, d // 4), (d // 4, 1)]
        for i, (a, b) in enumerate(gc_dims):
            inp[f'gc_w{i + 1}'] = w(ks[5 + i], a, b)
            inp[f'gc_b{i + 1}'] = jnp.zeros((b,), dtype=jnp.float32)
        inp['adaptive_range'] = jnp.full((1,), 0.2, dtype=jnp.float32)
        return inp
    _L0_ffn_in = _L0_ffn_setup()
    _L0_c = _w((lambda *s: np.random.randn(*s).astype(np.float32) * 0.05)(1, 128))
    _L0_wmod = _w((lambda *s: np.random.randn(*s).astype(np.float32) * 0.05)(128, 6 * 128) * 128 ** (-0.5))

    def _L1_attn_setup():
        import jax, jax.numpy as jnp
        import numpy as np
        SPS_AMPLIFY = 1.5
        SPS_DAMPEN = 0.3
        SPS_DEEP_QUESTION = 0.1
        SPS_EXCLAIM = 0.85
        SPS_QUESTION = 0.25
        SPS_SUPER_EXCLAIM = 0.95
        B, S, D = (4, 256, 128)
        NUM_HEADS = 16
        HEAD_DIM = D // NUM_HEADS
        SCALE = HEAD_DIM ** (-0.5)

        def sps_pro(x):
            xn = jax.nn.sigmoid(x)
            mult = jnp.where(xn > SPS_SUPER_EXCLAIM, 2.0, jnp.where(xn > SPS_EXCLAIM, SPS_AMPLIFY, jnp.where(xn < SPS_DEEP_QUESTION, 0.1, jnp.where(xn < SPS_QUESTION, SPS_DAMPEN, 1.0))))
            return x * mult
        key = jax.random.key(seed)
        k0, k1, k2, k3, k4 = jax.random.split(key, 5)
        s = 1.0 / np.sqrt(D)
        return {'x': jax.random.normal(k0, (B, S, D), dtype=jnp.float32), 'W_qkv': jax.random.uniform(k1, (D, 3 * D), dtype=jnp.float32, minval=-s, maxval=s), 'b_qkv': jax.random.uniform(k2, (3 * D,), dtype=jnp.float32, minval=-s, maxval=s), 'W_proj': jax.random.uniform(k3, (D, D), dtype=jnp.float32, minval=-s, maxval=s), 'b_proj': jax.random.uniform(k4, (D,), dtype=jnp.float32, minval=-s, maxval=s)}
    _L1_attn_in = _L1_attn_setup()

    def _L1_ffn_setup():
        import jax, jax.numpy as jnp
        import numpy as np
        DIM = 128
        MLP_MULT = 4
        NUM_EXPERTS = 8
        EXPERT_HIDDEN = MLP_MULT * DIM // NUM_EXPERTS
        key = jax.random.key(seed)
        k_x, k_r, k_fc, k_pj = jax.random.split(key, 4)
        x = jax.random.normal(k_x, (4, 512, DIM), dtype=jnp.float32)
        w_router = jax.random.normal(k_r, (NUM_EXPERTS, DIM), dtype=jnp.float32) * (1.0 / np.sqrt(DIM))
        w_fc = jax.random.normal(k_fc, (NUM_EXPERTS, EXPERT_HIDDEN, DIM), dtype=jnp.float32) * (1.0 / np.sqrt(DIM))
        w_proj = jax.random.normal(k_pj, (NUM_EXPERTS, DIM, EXPERT_HIDDEN), dtype=jnp.float32) * (1.0 / np.sqrt(EXPERT_HIDDEN))
        return {'x': x, 'w_router': w_router, 'w_fc': w_fc, 'w_proj': w_proj}
    _L1_ffn_in = _L1_ffn_setup()
    _L1_c = _w((lambda *s: np.random.randn(*s).astype(np.float32) * 0.05)(1, 128))
    _L1_wmod = _w((lambda *s: np.random.randn(*s).astype(np.float32) * 0.05)(128, 6 * 128) * 128 ** (-0.5))
    _d = {'L0_attn_x': _L0_attn_in['x'], 'L0_attn_Wq': _L0_attn_in['Wq'], 'L0_attn_bq': _L0_attn_in['bq'], 'L0_attn_Wk': _L0_attn_in['Wk'], 'L0_attn_bk': _L0_attn_in['bk'], 'L0_attn_Wv': _L0_attn_in['Wv'], 'L0_attn_bv': _L0_attn_in['bv'], 'L0_ffn_cn_w1': _L0_ffn_in['cn_w1'], 'L0_ffn_cn_b1': _L0_ffn_in['cn_b1'], 'L0_ffn_cn_w2': _L0_ffn_in['cn_w2'], 'L0_ffn_cn_b2': _L0_ffn_in['cn_b2'], 'L0_ffn_cn_w3': _L0_ffn_in['cn_w3'], 'L0_ffn_cn_b3': _L0_ffn_in['cn_b3'], 'L0_ffn_cn_w4': _L0_ffn_in['cn_w4'], 'L0_ffn_cn_b4': _L0_ffn_in['cn_b4'], 'L0_ffn_gc_w1': _L0_ffn_in['gc_w1'], 'L0_ffn_gc_b1': _L0_ffn_in['gc_b1'], 'L0_ffn_gc_w2': _L0_ffn_in['gc_w2'], 'L0_ffn_gc_b2': _L0_ffn_in['gc_b2'], 'L0_ffn_gc_w3': _L0_ffn_in['gc_w3'], 'L0_ffn_gc_b3': _L0_ffn_in['gc_b3'], 'L0_ffn_adaptive_range': _L0_ffn_in['adaptive_range'], 'L0_c': _L0_c, 'L0_wmod': _L0_wmod, 'L1_attn_W_qkv': _L1_attn_in['W_qkv'], 'L1_attn_b_qkv': _L1_attn_in['b_qkv'], 'L1_attn_W_proj': _L1_attn_in['W_proj'], 'L1_attn_b_proj': _L1_attn_in['b_proj'], 'L1_ffn_w_router': _L1_ffn_in['w_router'], 'L1_ffn_w_fc': _L1_ffn_in['w_fc'], 'L1_ffn_w_proj': _L1_ffn_in['w_proj'], 'L1_c': _L1_c, 'L1_wmod': _L1_wmod}
    _x0 = _d['L0_attn_x']
    _d['L0_attn_x'] = jax.random.normal(jax.random.fold_in(jax.random.key(seed), 1), (1, 2048, 128), dtype=_x0.dtype)
    del _x0
    return _d

def reference(L0_attn_x, L0_attn_Wq, L0_attn_bq, L0_attn_Wk, L0_attn_bk, L0_attn_Wv, L0_attn_bv, L0_ffn_cn_w1, L0_ffn_cn_b1, L0_ffn_cn_w2, L0_ffn_cn_b2, L0_ffn_cn_w3, L0_ffn_cn_b3, L0_ffn_cn_w4, L0_ffn_cn_b4, L0_ffn_gc_w1, L0_ffn_gc_b1, L0_ffn_gc_w2, L0_ffn_gc_b2, L0_ffn_gc_w3, L0_ffn_gc_b3, L0_ffn_adaptive_range, L0_c, L0_wmod, L1_attn_W_qkv, L1_attn_b_qkv, L1_attn_W_proj, L1_attn_b_proj, L1_ffn_w_router, L1_ffn_w_fc, L1_ffn_w_proj, L1_c, L1_wmod):

    def _L0_attn_ref(x, Wq, bq, Wk, bk, Wv, bv):
        import jax, jax.numpy as jnp
        import numpy as np
        import math
        B, S, D_IN, D_KQ, D_OUT = (4, 256, 128, 128, 128)
        Q = jnp.einsum('bsd,kd->bsk', x, Wq) + bq
        K = jnp.einsum('bsd,kd->bsk', x, Wk) + bk
        V = jnp.einsum('bsd,od->bso', x, Wv) + bv
        scale = 1.0 / math.sqrt(D_KQ)
        attn = jnp.einsum('bqk,bsk->bqs', Q, K) * scale
        s = attn.shape[-1]
        causal = jnp.tril(jnp.ones((s, s), dtype=bool))
        attn = jnp.where(causal[None, :, :], attn, -jnp.inf)
        attn = jax.nn.softmax(attn, axis=-1)
        Z = jnp.einsum('bqs,bso->bqo', attn, V)
        return Z

    def _L0_ffn_ref(x, cn_w1, cn_b1, cn_w2, cn_b2, cn_w3, cn_b3, cn_w4, cn_b4, gc_w1, gc_b1, gc_w2, gc_b2, gc_w3, gc_b3, adaptive_range):
        import jax, jax.numpy as jnp
        import numpy as np
        B, S, DIM = (4, 512, 128)
        BASE_COUPLING = 0.1
        NUM_CYCLES = 3

        def _gelu(x):
            return jax.nn.gelu(x, approximate=False)

        def _coupling_net(h, w1, b1, w2, b2, w3, b3, w4, b4):
            h = _gelu(h @ w1 + b1)
            h = _gelu(h @ w2 + b2)
            h = _gelu(h @ w3 + b3)
            return jax.nn.sigmoid(h @ w4 + b4)

        def _global_net(h, w1, b1, w2, b2, w3, b3):
            h = _gelu(h @ w1 + b1)
            h = _gelu(h @ w2 + b2)
            return jax.nn.sigmoid(h @ w3 + b3)

        def _twist(x):
            o_r, o_i, p_r, p_i = jnp.split(x, 4, axis=-1)
            return jnp.concatenate([p_r, -p_i, -o_r, o_i], axis=-1)
        global_context = x.mean(axis=1, keepdims=True)
        gf = _global_net(global_context, gc_w1, gc_b1, gc_w2, gc_b2, gc_w3, gc_b3)
        out = x
        for _ in range(NUM_CYCLES):
            tf = _coupling_net(out, cn_w1, cn_b1, cn_w2, cn_b2, cn_w3, cn_b3, cn_w4, cn_b4)
            combined = 0.7 * gf + 0.3 * tf
            coupling = BASE_COUPLING + adaptive_range * (combined - 0.5) * 2.0
            out = out + coupling * _twist(out)
        return out

    def _L1_attn_ref(x, W_qkv, b_qkv, W_proj, b_proj):
        import jax, jax.numpy as jnp
        import numpy as np
        SPS_AMPLIFY = 1.5
        SPS_DAMPEN = 0.3
        SPS_DEEP_QUESTION = 0.1
        SPS_EXCLAIM = 0.85
        SPS_QUESTION = 0.25
        SPS_SUPER_EXCLAIM = 0.95
        B, S, D = (4, 256, 128)
        NUM_HEADS = 16
        HEAD_DIM = D // NUM_HEADS
        SCALE = HEAD_DIM ** (-0.5)

        def sps_pro(x):
            xn = jax.nn.sigmoid(x)
            mult = jnp.where(xn > SPS_SUPER_EXCLAIM, 2.0, jnp.where(xn > SPS_EXCLAIM, SPS_AMPLIFY, jnp.where(xn < SPS_DEEP_QUESTION, 0.1, jnp.where(xn < SPS_QUESTION, SPS_DAMPEN, 1.0))))
            return x * mult
        qkv = jnp.einsum('bsd,de->bse', x, W_qkv) + b_qkv
        q, k, v = jnp.split(qkv, 3, axis=-1)
        attn = jnp.einsum('bsd,btd->bst', q, k) * SCALE
        attn = sps_pro(attn)
        attn = jax.nn.softmax(attn, axis=-1)
        out = jnp.einsum('bst,btd->bsd', attn, v)
        out = jnp.einsum('bsd,de->bse', out, W_proj) + b_proj
        return out

    def _L1_ffn_ref(x, w_router, w_fc, w_proj):
        import jax, jax.numpy as jnp
        import numpy as np
        DIM = 128
        MLP_MULT = 4
        NUM_EXPERTS = 8
        EXPERT_HIDDEN = MLP_MULT * DIM // NUM_EXPERTS
        logits = jnp.einsum('bsd,ed->bse', jax.lax.stop_gradient(x), w_router)
        weights = jax.nn.softmax(logits, axis=-1)
        indices = jnp.argmax(weights, axis=-1)
        onehot = jax.nn.one_hot(indices, NUM_EXPERTS, dtype=x.dtype)
        h = jnp.einsum('bsd,ehd->bseh', x, w_fc)
        h = jnp.where(h >= 0, h, 0.5 * h)
        h = h * h
        out = jnp.einsum('bseh,edh,bse->bsd', h, w_proj, onehot)
        return out
    x = L0_attn_x
    mod = (_silu(L0_c) @ L0_wmod).reshape(L0_c.shape[0], 6, 1, -1)
    sa, ca, ga, sb, cb, gb = (mod[:, 0], mod[:, 1], mod[:, 2], mod[:, 3], mod[:, 4], mod[:, 5])
    ga = (2 * (ga >= 0) - 1) * jnp.maximum(jnp.abs(ga), 0.25)
    gb = (2 * (gb >= 0) - 1) * jnp.maximum(jnp.abs(gb), 0.25)
    h = _layernorm(x, axis=-1) * (1 + ca) + sa
    x = x + ga * _L0_attn_ref(h, L0_attn_Wq, L0_attn_bq, L0_attn_Wk, L0_attn_bk, L0_attn_Wv, L0_attn_bv)
    h = _layernorm(x, axis=-1) * (1 + cb) + sb
    x = x + gb * _L0_ffn_ref(h, L0_ffn_cn_w1, L0_ffn_cn_b1, L0_ffn_cn_w2, L0_ffn_cn_b2, L0_ffn_cn_w3, L0_ffn_cn_b3, L0_ffn_cn_w4, L0_ffn_cn_b4, L0_ffn_gc_w1, L0_ffn_gc_b1, L0_ffn_gc_w2, L0_ffn_gc_b2, L0_ffn_gc_w3, L0_ffn_gc_b3, L0_ffn_adaptive_range)
    mod = (_silu(L1_c) @ L1_wmod).reshape(L1_c.shape[0], 6, 1, -1)
    sa, ca, ga, sb, cb, gb = (mod[:, 0], mod[:, 1], mod[:, 2], mod[:, 3], mod[:, 4], mod[:, 5])
    ga = (2 * (ga >= 0) - 1) * jnp.maximum(jnp.abs(ga), 0.25)
    gb = (2 * (gb >= 0) - 1) * jnp.maximum(jnp.abs(gb), 0.25)
    h = _layernorm(x, axis=-1) * (1 + ca) + sa
    x = x + ga * _L1_attn_ref(h, L1_attn_W_qkv, L1_attn_b_qkv, L1_attn_W_proj, L1_attn_b_proj)
    h = _layernorm(x, axis=-1) * (1 + cb) + sb
    x = x + gb * _L1_ffn_ref(h, L1_ffn_w_router, L1_ffn_w_fc, L1_ffn_w_proj)
    return x

_drawn_inputs = setup_inputs


def setup_inputs(seed=0):
    import zlib

    import numpy as np

    out = dict(_drawn_inputs(seed))
    spreads = {'L0_ffn_cn_b1': (0.0, 0.8),
     'L0_ffn_cn_b2': (0.0, 2.0),
     'L0_ffn_cn_b3': (0.0, 2.0),
     'L0_ffn_gc_b1': (0.0, 0.8),
     'L0_ffn_gc_b2': (0.0, 2.0)}
    factors = {'L0_attn_Wq': 8.0,
     'L0_attn_bq': 8.0,
     'L0_attn_Wk': 8.0,
     'L0_attn_bk': 64.0,
     'L0_attn_Wv': 3.702,
     'L0_ffn_cn_w1': 3.975,
     'L0_ffn_cn_w2': 3.262,
     'L0_ffn_cn_w3': 3.646,
     'L0_ffn_gc_w1': 64.0,
     'L0_ffn_gc_w2': 28.716,
     'L0_ffn_gc_w3': 5.642,
     'L0_attn_bv': 2.687}
    for name, (base, spread) in spreads.items():
        noise = np.random.default_rng([zlib.crc32(name.encode()), seed]).standard_normal(out[name].shape)
        drawn = base * np.exp(spread * noise) if base else spread * noise
        out[name] = jnp.asarray(drawn.astype(out[name].dtype))
    for name, factor in factors.items():
        out[name] = (out[name] * factor).astype(out[name].dtype)
    return out
```

```python
from contextlib import ExitStack

import concourse.bass as bass
from concourse import mybir

P = 128
C = 512
TPC = C // P

ALU = mybir.AluOpType
ACT = mybir.ActivationFunctionType
AX = mybir.AxisListType
F32 = mybir.dt.float32
BF16 = mybir.dt.bfloat16

LN_EPS = 1e-5
GATE_FLOOR = 0.25
MASKED = -1e30
CYCLES = 3
HEAD_DIM_L1 = 8
EXPERTS = 8

BAND_EDGES = (-2.1972245773362196, -1.0986122886681098, 1.7346010553881064, 2.9444389791664403)
BAND_STEPS = (1.0, 3.5, 2.5, 2.5)
BAND_BASE = 0.5
BAND_UNIT = 0.2


def build(nc, x, Wq, bq, Wk, bk, Wv, bv, cn_w1, cn_b1, cn_w2, cn_b2, cn_w3, cn_b3, cn_w4, cn_b4,
          gc_w1, gc_b1, gc_w2, gc_b2, gc_w3, gc_b3, adaptive_range, c0, wmod0,
          W_qkv, b_qkv, W_proj, b_proj, w_router, w_fc, w_proj, c1, wmod1, out):
    _, S, D = x.shape
    T = S // P
    G = S // C
    H2, H3 = cn_w2.shape[1], cn_w3.shape[1]
    assert D == P and H2 == 64 and H3 == 32 and T == 16
    SCALE0 = float(D) ** -0.5
    SCALE1 = float(HEAD_DIM_L1) ** -0.5

    with ExitStack() as ctx:
        def sb(name, shape, dt=F32):
            return ctx.enter_context(nc.sbuf_tensor(name, shape, dt))

        def sem(name):
            return ctx.enter_context(nc.semaphore(name))

        xres = sb("xres", [P, T, D])
        yT = sb("yT", [P, S])
        hT = sb("hT", [P, S])
        qT = sb("qT", [P, S])
        kT = sb("kT", [P, S])
        v = sb("v", [P, T, D])
        ident = sb("ident", [P, P])
        identb = sb("identb", [P, P], BF16)
        causal = sb("causal", [P, P])
        twist = sb("twist", [P, P])
        ones = sb("ones", [P, P])
        neghalf = sb("neghalf", [P, TPC])
        expert_sel = sb("expert_sel", [EXPERTS, TPC, 2, 64], BF16)
        tie_rank = sb("tie_rank", [P, TPC, EXPERTS])
        wqkv0_raw = sb("wqkv0_raw", [P, 3, P])
        wqkvT0 = sb("wqkvT0", [P, 3, P])
        bqk0 = sb("bqk0", [P, 2])
        bv_row = sb("bv_row", [P, P])
        c_col = sb("c_col", [P, 2])
        tanh_c = sb("tanh_c", [P, 2])
        silu_col = sb("silu_col", [P, 2])
        silu_b = sb("silu_b", [P, 2, P])
        wmod = sb("wmod", [P, 2, 6 * P])
        modc = sb("modc", [P, 2, 6])
        modp = sb("modp", [P, 2, 6])
        gate_sign = sb("gate_sign", [P, 3, P])
        gate_abs = sb("gate_abs", [P, 3, P])
        gcol_abs = sb("gcol_abs", [P, 1])
        gate_mag = sb("gate_mag", [P, 3, P])
        gate_row = sb("gate_row", [P, 3, P])
        gcol_sign = sb("gcol_sign", [P, 1])
        gcol_mag = sb("gcol_mag", [P, 1])
        gb0_col = sb("gb0_col", [P, 1])
        w1s = sb("w1s", [P, P])
        w2s = sb("w2s", [P, H2])
        w3s = sb("w3s", [P, 2 * H3])
        w4s = sb("w4s", [2 * H3, 1])
        w4b = sb("w4b", [2 * H3, P])
        g1s = sb("g1s", [P, H2])
        g2s = sb("g2s", [H2, H3])
        g3s = sb("g3s", [H3, 1])
        g3b = sb("g3b", [H3, P])
        cb1 = sb("cb1", [P, 1])
        cb2 = sb("cb2", [P, 1])
        cb3 = sb("cb3", [2 * H3, 1])
        cb4 = sb("cb4", [P, 1])
        cb4h = sb("cb4h", [P, 1])
        gb1s = sb("gb1s", [H2, 1])
        gb2s = sb("gb2s", [H3, 1])
        gb3s = sb("gb3s", [P, 1])
        gb3h = sb("gb3h", [P, 1])
        arange = sb("arange", [P, 1])
        ctx_parts = sb("ctx_parts", [P, G])
        ctx_sum = sb("ctx_sum", [P, 1])
        ctx_mean = sb("ctx_mean", [P, 1])
        g_a1 = sb("g_a1", [H2, 1])
        g_a2 = sb("g_a2", [H3, 1])
        g_th = sb("g_th", [P, 1])
        cpl_a0 = sb("cpl_a0", [P, 1])
        cpl_a1 = sb("cpl_a1", [P, 1])
        cpl_a = sb("cpl_a", [P, 1])
        cpl_b = sb("cpl_b", [P, 1])
        wqkv1 = sb("wqkv1", [P, 3, P])
        bqkv1 = sb("bqkv1", [P, 3])
        bv1_b = sb("bv1_b", [P, P])
        wproj1 = sb("wproj1", [P, P])
        bproj_row = sb("bproj_row", [P, P])
        wvT1 = sb("wvT1", [P, P])
        wvp1 = sb("wvp1", [P, P])
        add0_row = sb("add0_row", [P, P])
        add1_pre = sb("add1_pre", [P, P])
        add1_row = sb("add1_row", [P, P])
        wr_raw = sb("wr_raw", [EXPERTS, P])
        wrT = sb("wrT", [P, EXPERTS])
        wfc_raw = sb("wfc_raw", [P, TPC, P])
        wfcT = sb("wfcT", [P, TPC, P])
        wpr_raw = sb("wpr_raw", [P, EXPERTS, 64])
        wpr = sb("wpr", [P, TPC, P])
        st = sb("st", [P, 4 * T, 6])
        mv = sb("mv", [P, 4 * T, 2])
        veps = sb("veps", [P, 4 * T])
        rstd = sb("rstd", [P, 4 * T])
        nrm = sb("nrm", [P, G, TPC, P])
        probs = sb("probs", [P, 2, S])
        pT = sb("pT", [P, 2, TPC, P])
        mx = sb("mx", [P, T, G])
        mrow = sb("mrow", [P, T])
        negmax = sb("negmax", [P, T])
        rs = sb("rs", [P, T, G])
        rsum = sb("rsum", [P, T])
        rinv = sb("rinv", [P, T])
        scores = sb("scores", [P, 2, S])
        band = sb("band", [P, 4, S], BF16)
        band_sum = sb("band_sum", [P, 2, S], BF16)
        mult = sb("mult", [P, S], BF16)
        qbuf = sb("qbuf", [P, 2, P])
        max1 = sb("max1", [P, 2])
        negmax1 = sb("negmax1", [P, 2])
        rsum1 = sb("rsum1", [P, 2])
        rinv1 = sb("rinv1", [P, 2])
        a1 = scores[:, 0, :].rearrange("p (r u t) -> p r u t", r=2, u=2)
        th = scores[:, 1, :].rearrange("p (r u t) -> p r u t", r=2, u=2)
        cpl = band[:, 0:2, :].rearrange("p b t -> p (b t)").bitcast(F32).rearrange("p (r u t) -> p r u t", r=2, u=2)
        step = band[:, 2:4, :].rearrange("p b t -> p (b t)").bitcast(F32).rearrange("p (r u t) -> p r u t", r=2, u=2)
        a2 = sb("a2", [P, 2, C])
        a3 = sb("a3", [2 * H3, 2, C])
        wait_holder = sb("wait_holder", [P, 1])
        lg = sb("lg", [P, T, EXPERTS])
        lgmax = sb("lgmax", [P, T])
        ranked = sb("ranked", [P, T, EXPERTS])
        best = sb("best", [P, T])
        onehot = sb("onehot", [P, T, EXPERTS], BF16)
        ohT = sb("ohT", [EXPERTS, 2, C], BF16)
        relu_h = sb("relu_h", [P, 2, C])
        lrelu2 = sb("lrelu2", [P, 2, C])
        picked = sb("picked", [P, 2, C])
        act2 = probs[:, :, :].rearrange("p b (c t) -> p b c t", c=TPC)

        sc4 = ctx.enter_context(nc.psum_tensor("sc4", [P, 4, C], F32))
        b4 = ctx.enter_context(nc.psum_tensor("b4", [P, C], F32))
        b5 = ctx.enter_context(nc.psum_tensor("b5", [P, C], F32))
        b6 = ctx.enter_context(nc.psum_tensor("b6", [P, C], F32))
        b7 = ctx.enter_context(nc.psum_tensor("b7", [P, C], F32))
        bank = [sc4[:, i, :] for i in range(4)] + [b[:, :] for b in (b4, b5, b6, b7)]
        ohT_ps = b7[:, :].bitcast(BF16)

        ld_x = [sem(f"ld_x{g}") for g in range(G)]
        ld_attn0 = sem("ld_attn0")
        ld_mod = sem("ld_mod")
        ld_ffn0 = sem("ld_ffn0")
        ld_l1 = sem("ld_l1")
        ld_moe = sem("ld_moe")
        pool_chain = sem("pool_chain")
        consts_ready = sem("consts_ready")
        tanh_c_ready = sem("tanh_c_ready")
        silu_ready = sem("silu_ready")
        w0T_psum = sem("w0T_psum")
        w0T_ready = sem("w0T_ready")
        mod_psum = sem("mod_psum")
        mod_ready = sem("mod_ready")
        w1T_psum = sem("w1T_psum")
        wv1T_ready = sem("wv1T_ready")
        wmoe_ready = sem("wmoe_ready")
        wvp_psum = sem("wvp_psum")
        wvp_ready = sem("wvp_ready")
        dve_chain = sem("dve_chain")
        act_chain = sem("act_chain")
        ffn_w_ready = sem("ffn_w_ready")
        bias_row_ready = sem("bias_row_ready")
        stats_ready = sem("stats_ready")
        rstd_ready = sem("rstd_ready")
        norm_ready = sem("norm_ready")
        lnT_psum = sem("lnT_psum")
        lnT_ready = sem("lnT_ready")
        qkv_psum = sem("qkv_psum")
        qk_ready = sem("qk_ready")
        v_ready = sem("v_ready")
        res_biased = sem("res_biased")
        score_psum = sem("score_psum")
        negmax_ready = sem("negmax_ready")
        exp_done = sem("exp_done")
        pT_psum = sem("pT_psum")
        pT_ready = sem("pT_ready")
        attn_psum = sem("attn_psum")
        attn_added = sem("attn_added")
        h1_psum = sem("h1_psum")
        h1_ready = sem("h1_ready")
        h2_psum = sem("h2_psum")
        h2_ready = sem("h2_ready")
        h3_psum = sem("h3_psum")
        h3_ready = sem("h3_ready")
        z_psum = sem("z_psum")
        th_ready = sem("th_ready")
        tw_psum = sem("tw_psum")
        y_ready = sem("y_ready")
        ctx_ready = sem("ctx_ready")
        gc_psum = sem("gc_psum")
        gc_ready = sem("gc_ready")
        cpl_ready = sem("cpl_ready")
        ffn_out_ready = sem("ffn_out_ready")
        ffnT_psum = sem("ffnT_psum")
        ffn_added = sem("ffn_added")
        q1_psum = sem("q1_psum")
        q1_ready = sem("q1_ready")
        s1_psum = sem("s1_psum")
        s1_ready = sem("s1_ready")
        bands_done = sem("bands_done")
        exp1_done = sem("exp1_done")
        p1T_psum = sem("p1T_psum")
        p1T_ready = sem("p1T_ready")
        attn1_psum = sem("attn1_psum")
        attn1_added = sem("attn1_added")
        lg_psum = sem("lg_psum")
        onehot_ready = sem("onehot_ready")
        ohT_psum = sem("ohT_psum")
        ohT_ready = sem("ohT_ready")
        fc_psum = sem("fc_psum")
        mask_psum = sem("mask_psum")
        relu_ready = sem("relu_ready")
        picked_ready = sem("picked_ready")
        act_ready = sem("act_ready")
        moe_psum = sem("moe_psum")
        out_ready = sem("out_ready")
        stored = sem("stored")

        def nchunks(i):
            return (i + TPC) // TPC

        def first_chunk(i):
            return sum(nchunks(j) for j in range(i))

        def width(i, c):
            return min(C, (i + 1) * P - c * C)

        SRING = 5
        x_t = x.rearrange("a (t p) d -> p (a t) d", p=P)
        out_t = out.rearrange("a (t p) d -> p (a t) d", p=P)

        def col(w):
            return w.rearrange("(p a) -> p a", a=1)

        block = ctx.enter_context(nc.Block())

        @block.sync
        def _(sp):
            for n, w in enumerate((Wq, Wk, Wv)):
                sp.dma_start(wqkv0_raw[:, n, :], w).then_inc(ld_attn0, 16)
            sp.dma_start(xres[:, 0:TPC, :], x_t[:, 0:TPC, :]).then_inc(ld_x[0], 16)
            sp.dma_start(wmod[:, 0, :], wmod0).then_inc(ld_mod, 16)
            sp.dma_start(wmod[:, 1, :], wmod1).then_inc(ld_mod, 16)
            for g in range(1, G):
                sp.dma_start(xres[:, g * TPC:(g + 1) * TPC, :],
                             x_t[:, g * TPC:(g + 1) * TPC, :]).then_inc(ld_x[g], 16)
            sp.dma_start(wqkv1[:, :, :], W_qkv.rearrange("d (n e) -> d n e", n=3)).then_inc(ld_l1, 16)
            sp.dma_start(wproj1[:, :], W_proj).then_inc(ld_l1, 16)
            sp.dma_start(bproj_row[:, :], b_proj.partition_broadcast(P)).then_inc(ld_l1, 16)
            for n in range(3):
                sp.dma_start(bqkv1[:, n:n + 1], col(b_qkv[n * P:(n + 1) * P])).then_inc(ld_l1, 16)
            sp.dma_start(wr_raw[:, :], w_router).then_inc(ld_moe, 16)
            for c in range(TPC):
                sp.dma_start(wfc_raw[:, c, :],
                             w_fc[2 * c:2 * c + 2, :, :].rearrange("u h d -> (u h) d")).then_inc(ld_moe, 16)
            sp.dma_start(wpr_raw[:, :, :], w_proj.rearrange("e d h -> d e h")).then_inc(ld_moe, 16)
            for dst, src in ((w1s[:, :], cn_w1), (w2s[:, :], cn_w2), (g1s[:, :], gc_w1), (g2s[:, :], gc_w2),
                             (g3s[:, :], gc_w3), (w4s[0:H3, :], cn_w4), (w4s[H3:2 * H3, :], cn_w4),
                             (cb1[:, :], col(cn_b1)), (cb2[0:H2, :], col(cn_b2)), (cb2[H2:P, :], col(cn_b2)),
                             (cb3[0:H3, :], col(cn_b3)), (cb3[H3:2 * H3, :], col(cn_b3)),
                             (cb4[:, :], cn_b4.partition_broadcast(P)), (gb1s[:, :], col(gc_b1)),
                             (gb2s[:, :], col(gc_b2)), (gb3s[:, :], gc_b3.partition_broadcast(P)),
                             (arange[:, :], adaptive_range.partition_broadcast(P))):
                sp.dma_start(dst, src).then_inc(ld_ffn0, 16)
            sp.wait_ge(consts_ready, 1)
            for u in range(2):
                sp.dma_start(w3s[u * H2:(u + 1) * H2, u * H3:(u + 1) * H3], cn_w3).then_inc(ld_ffn0, 16)
            for g in range(G):
                sp.wait_ge(out_ready, g + 1)
                sp.dma_start(out_t[:, g * TPC:(g + 1) * TPC, :],
                             xres[:, g * TPC:(g + 1) * TPC, :]).then_inc(stored, 16)
            sp.wait_ge(stored, 16 * G)
        FFN_LOADS = 19

        @block.gpsimd
        def _(pool):
            pool.memset(w3s[:, :], 0.0)
            pool.memset(ident[:, :], 0.0)
            pool.memset(identb[:, :], 0.0)
            pool.memset(twist[:, :], 0.0)
            pool.memset(causal[:, :], 0.0)
            pool.memset(ones[:, :], 1.0)
            pool.memset(neghalf[:, :], -0.5)
            for e in range(EXPERTS):
                pool.memset(tie_rank[:, :, e:e + 1], float(EXPERTS - e))
            pool.memset(expert_sel[:, :, :, :], 0.0).then_inc(pool_chain, 1)
            pool.wait_ge(pool_chain, 1)
            pool.affine_select(out=ident[:, :], in_=ident[:, :], compare_op=ALU.not_equal, fill=1.0,
                               base=0, pattern=[[-1, P]], channel_multiplier=1)
            pool.affine_select(out=identb[:, :], in_=identb[:, :], compare_op=ALU.not_equal, fill=1.0,
                               base=0, pattern=[[-1, P]], channel_multiplier=1)
            pool.affine_select(out=causal[:, :], in_=causal[:, :], compare_op=ALU.is_ge, fill=MASKED,
                               base=0, pattern=[[-1, P]], channel_multiplier=1)
            for j0, src, sign in ((0, 64, 1.0), (32, 96, -1.0), (64, 0, -1.0), (96, 32, 1.0)):
                pool.affine_select(out=twist[:, j0:j0 + 32], in_=twist[:, j0:j0 + 32],
                                   compare_op=ALU.not_equal, fill=sign, base=-src,
                                   pattern=[[-1, 32]], channel_multiplier=1)
            pool.affine_select(out=expert_sel[:, :, :, :], in_=expert_sel[:, :, :, :],
                               compare_op=ALU.not_equal, fill=1.0, base=0,
                               pattern=[[-2, TPC], [-1, 2], [0, 64]],
                               channel_multiplier=1).then_inc(consts_ready, 1)

            def ln_rstd(ph, g):
                n = ph * G + g
                s = slice(n * TPC, (n + 1) * TPC)
                pool.wait_ge(stats_ready, n + 1)
                pool.tensor_scalar(veps[:, s], mv[:, s, 1], LN_EPS, None, ALU.add).then_inc(pool_chain, 1)
                pool.wait_ge(pool_chain, n + 2)
                pool.tensor_tensor(rstd[:, s], veps[:, s], neghalf[:, :], ALU.pow).then_inc(rstd_ready, 1)

            for g in range(G):
                ln_rstd(0, g)
            pool.wait_ge(bias_row_ready, 1)
            for g in range(G):
                pool.wait_ge(norm_ready, g + 1)
                pool.tensor_tensor(xres[:, g * TPC:(g + 1) * TPC, :], xres[:, g * TPC:(g + 1) * TPC, :],
                                   add0_row[:, :].unsqueeze(1).to_broadcast([P, TPC, P]),
                                   ALU.add).then_inc(res_biased, 1)
            for g in range(G):
                ln_rstd(1, g)
            for g in range(G):
                ln_rstd(2, g)
            pool.wait_ge(wvp_ready, 1)
            for g in range(G):
                pool.wait_ge(norm_ready, 2 * G + g + 1)
                pool.tensor_tensor(xres[:, g * TPC:(g + 1) * TPC, :], xres[:, g * TPC:(g + 1) * TPC, :],
                                   add1_row[:, :].unsqueeze(1).to_broadcast([P, TPC, P]),
                                   ALU.add).then_inc(res_biased, 1)
            for g in range(G):
                ln_rstd(3, g)

        @block.scalar
        def _(act):
            act.dma_start(c_col[:, 0:1], c0.rearrange("a p -> p a")).then_inc(ld_mod, 16)
            act.dma_start(c_col[:, 1:2], c1.rearrange("a p -> p a")).then_inc(ld_mod, 16)
            act.dma_start(bqk0[:, 0:1], col(bq)).then_inc(ld_attn0, 16)
            act.dma_start(bqk0[:, 1:2], col(bk)).then_inc(ld_attn0, 16)
            act.dma_start(bv_row[:, :], bv.partition_broadcast(P)).then_inc(ld_attn0, 16)

            act.wait_ge(ld_mod, 64)
            nc.scalar.activation(tanh_c[:, :], c_col[:, :], ACT.Tanh, scale=0.5).then_inc(tanh_c_ready, 1)
            act.wait_ge(w0T_psum, 1)
            nc.scalar.activation(wqkvT0[:, 0:2, :], bank[0].rearrange("p (n e) -> p n e", n=4)[:, 0:2, :],
                                 ACT.Copy).then_inc(w0T_ready, 1)

            def ln_affine(ph, g, dst, layer, shift, scale):
                n = ph * G + g
                act.wait_ge(lnT_psum, n + 1)
                nc.scalar.activation(dst[:, g * C:(g + 1) * C], bank[6 + n % 2], ACT.Identity,
                                     bias=modc[:, layer, shift:shift + 1],
                                     scale=modp[:, layer, scale:scale + 1]).then_inc(lnT_ready, 1)

            act.wait_ge(mod_ready, 1)
            for g in range(G):
                ln_affine(0, g, hT, 0, 0, 1)
                for n, dst in ((0, qT), (1, kT)):
                    act.wait_ge(qkv_psum, 3 * g + n + 1)
                    nc.scalar.activation(dst[:, g * C:(g + 1) * C], bank[3 * (g % 2) + n], ACT.Identity,
                                         bias=bqk0[:, n:n + 1]).then_inc(qk_ready, 1)

            for i in range(T):
                act.wait_ge(negmax_ready, i + 1)
                if i >= 2:
                    act.wait_ge(attn_psum, i - 1)
                for c in range(nchunks(i)):
                    w = width(i, c)
                    nc.scalar.activation(probs[:, i % 2, c * C:c * C + w],
                                         bank[(first_chunk(i) + c) % SRING][:, 0:w], ACT.Exp,
                                         bias=negmax[:, i:i + 1], scale=SCALE0,
                                         accum_out=rs[:, i, c:c + 1]).then_inc(exp_done, 1)

            for g in range(G):
                ln_affine(1, g, yT, 0, 3, 4)
            act.wait_ge(gc_psum, 1)
            nc.scalar.activation(g_a1[:, :], bank[7][0:H2, 0:1], ACT.Gelu, bias=gb1s[:, :]).then_inc(gc_ready, 1)
            act.wait_ge(gc_psum, 2)
            nc.scalar.activation(g_a2[:, :], bank[7][0:H3, 0:1], ACT.Gelu, bias=gb2s[:, :]).then_inc(gc_ready, 1)
            act.wait_ge(gc_psum, 3)
            nc.scalar.activation(g_th[:, :], bank[7][:, 0:1], ACT.Tanh, bias=gb3h[:, :], scale=0.5)\
              .then_inc(gc_ready, 1)

            with act.Fori(0, CYCLES) as cyc:
                for pr in range(2):
                    for u in range(2):
                        act.wait_ge(h1_psum, cyc * 4 + (2 * pr + u + 1))
                        nc.scalar.activation(a1[:, pr, u, :], bank[u], ACT.Gelu, bias=cb1[:, :])\
                          .then_inc(h1_ready, 1)
                for pr in range(2):
                    act.wait_ge(h2_psum, cyc * 2 + (pr + 1))
                    nc.scalar.activation(a2[:, pr, :], bank[2], ACT.Gelu, bias=cb2[:, :]).then_inc(h2_ready, 1)
                for pr in range(2):
                    act.wait_ge(h3_psum, cyc * 2 + (pr + 1))
                    nc.scalar.activation(a3[:, pr, :], bank[3][0:2 * H3, :], ACT.Gelu, bias=cb3[:, :])\
                      .then_inc(h3_ready, 1)
                for pr in range(2):
                    for u in range(2):
                        act.wait_ge(z_psum, cyc * 4 + (2 * pr + u + 1))
                        nc.scalar.activation(th[:, pr, u, :], bank[4 + u], ACT.Tanh, bias=cb4h[:, :], scale=0.5)\
                          .then_inc(th_ready, 1)

            for g in range(G):
                ln_affine(2, g, hT, 1, 0, 1)
                act.wait_ge(qkv_psum, 3 * G + 2 * g + 1)
                nc.scalar.activation(kT[:, g * C:(g + 1) * C], bank[2 * (g % 2)], ACT.Identity,
                                     bias=bqkv1[:, 1:2]).then_inc(qk_ready, 1)

            def fetch_scores(j, u):
                act.wait_ge(q1_psum, j + 1)
                nc.scalar.activation(qbuf[:, u, :], bank[7][:, 0:P], ACT.Identity,
                                     bias=bqkv1[:, 0:1]).then_inc(q1_ready, 1)
                for c in range(G):
                    act.wait_ge(s1_psum, j * G + (c + 1))
                    nc.scalar.activation(scores[:, u, c * C:(c + 1) * C], bank[c], ACT.Copy).then_inc(s1_ready, 1)

            def exp_and_transposes(j, u):
                act.wait_ge(bands_done, j + 1)
                nc.scalar.activation(probs[:, u, :], scores[:, u, :], ACT.Exp, bias=negmax1[:, u:u + 1],
                                     scale=BAND_UNIT * SCALE1, accum_out=rsum1[:, u:u + 1]).then_inc(exp1_done, 1)
                for c in range(G):
                    act.wait_ge(p1T_psum, j * G + (c + 1))
                    nc.scalar.activation(pT[:, c % 2, :, :], bank[4 + c % 2].rearrange("p (t q) -> p t q", t=TPC),
                                         ACT.Copy).then_inc(p1T_ready, 1)

            fetch_scores(0, 0)
            fetch_scores(1, 1)
            with act.Fori(0, T // 2 - 1) as pair:
                for u in range(2):
                    exp_and_transposes(pair * 2 + u, u)
                    fetch_scores(pair * 2 + (u + 2), u)
            for u in range(2):
                exp_and_transposes(T - 2 + u, u)

            for g in range(G):
                ln_affine(3, g, hT, 1, 3, 4)
                act.wait_ge(ohT_psum, g + 1)
                nc.scalar.activation(ohT[:, g % 2, :], ohT_ps[0:EXPERTS, 0:C], ACT.Copy).then_inc(ohT_ready, 1)
                for c in range(TPC):
                    n = g * TPC + c
                    act.wait_ge(fc_psum, n + 1)
                    nc.scalar.activation(relu_h[:, n % 2, :], bank[n % 2], ACT.Relu).then_inc(relu_ready, 1)
                    act.wait_ge(picked_ready, n + 1)
                    if g >= 2 and c == 0:
                        act.wait_ge(moe_psum, g - 1)
                    nc.scalar.activation(act2[:, g % 2, c, :], picked[:, n % 2, :], ACT.Square, scale=0.5)\
                      .then_inc(act_ready, 1)

        @block.vector
        def _(dve):
            links = [0]

            def link(ins):
                links[0] += 1
                ins.then_inc(dve_chain, 1)
                dve.wait_ge(dve_chain, links[0])

            def ln_stats(ph, g):
                n = ph * G + g
                for t in range(TPC):
                    last = nc.vector.bn_stats(st[:, n * TPC + t, :], xres[:, g * TPC + t, :])
                link(last)
                for t in range(TPC):
                    last = nc.vector.bn_aggr(mv[:, n * TPC + t, :], st[:, n * TPC + t, :])
                last.then_inc(stats_ready, 1)

            def ln_norm(ph, g):
                n = ph * G + g
                dve.wait_ge(rstd_ready, n + 1)
                if n >= G:
                    dve.wait_ge(lnT_psum, n - G + 1)
                for t in range(TPC):
                    k = n * TPC + t
                    last = nc.vector.tensor_scalar(nrm[:, g, t, :], xres[:, g * TPC + t, :],
                                                   mv[:, k, 0:1], rstd[:, k:k + 1], ALU.subtract, ALU.mult)
                last.then_inc(norm_ready, 1)

            for g in range(G):
                if g == 1:
                    dve.wait_ge(tanh_c_ready, 1)
                    dve.wait_ge(ld_mod, 64)
                    link(nc.vector.scalar_tensor_tensor(out=silu_col[:, :], in0=tanh_c[:, :], scalar=1.0,
                                                        in1=c_col[:, :], op0=ALU.add, op1=ALU.mult))
                    dve.wait_ge(consts_ready, 1)
                    for n in range(2):
                        last = nc.vector.tensor_scalar(silu_b[:, n, :], ones[:, :], silu_col[:, n:n + 1], 0.5,
                                                       ALU.mult, ALU.mult)
                    last.then_inc(silu_ready, 1)
                    dve.wait_ge(w0T_ready, 1)
                    nc.vector.tensor_copy(wqkvT0[:, 2, :], bank[0][:, 2 * P:3 * P]).then_inc(w0T_ready, 1)
                dve.wait_ge(ld_x[g], 16)
                ln_stats(0, g)
            dve.wait_ge(mod_psum, 1)
            nc.vector.tensor_copy(modc[:, :, :], bank[1][:, 0:12].rearrange("p (n j) -> p n j", n=2))
            nc.vector.tensor_scalar(modp[:, :, :], bank[1][:, 0:12].rearrange("p (n j) -> p n j", n=2), 1.0, None,
                                    ALU.add)
            gcol = bank[1][:, 5:6]
            rows = bank[2][:, 0:3 * P].rearrange("p (n e) -> p n e", n=3)
            nc.vector.tensor_scalar(gcol_sign[:, :], gcol, 0.0, 2.0, ALU.is_ge, ALU.mult)
            link(nc.vector.tensor_scalar(gate_sign[:, :, :], rows, 0.0, 2.0, ALU.is_ge, ALU.mult))
            nc.vector.scalar_tensor_tensor(out=gcol_abs[:, :], in0=gcol_sign[:, :], scalar=-1.0, in1=gcol,
                                           op0=ALU.add, op1=ALU.mult)
            link(nc.vector.scalar_tensor_tensor(out=gate_abs[:, :, :], in0=gate_sign[:, :, :], scalar=-1.0,
                                                in1=rows, op0=ALU.add, op1=ALU.mult))
            nc.vector.tensor_scalar(gcol_mag[:, :], gcol_abs[:, :], GATE_FLOOR, None, ALU.max)
            link(nc.vector.tensor_scalar(gate_mag[:, :, :], gate_abs[:, :, :], GATE_FLOOR, None, ALU.max))
            nc.vector.scalar_tensor_tensor(out=gb0_col[:, :], in0=gcol_sign[:, :], scalar=-1.0, in1=gcol_mag[:, :],
                                           op0=ALU.add, op1=ALU.mult)
            link(nc.vector.scalar_tensor_tensor(out=gate_row[:, :, :], in0=gate_sign[:, :, :], scalar=-1.0,
                                                in1=gate_mag[:, :, :], op0=ALU.add, op1=ALU.mult))
            dve.wait_ge(w0T_ready, 2)
            nc.vector.tensor_tensor(wqkvT0[:, 2, :], wqkvT0[:, 2, :], gate_row[:, 0, :], ALU.mult)\
              .then_inc(mod_ready, 1)
            dve.wait_ge(ld_attn0, 96)
            nc.vector.tensor_tensor(add0_row[:, :], bv_row[:, :], gate_row[:, 0, :], ALU.mult)\
              .then_inc(bias_row_ready, 1)
            for g in range(G):
                ln_norm(0, g)

            dve.wait_ge(ld_ffn0, 16 * FFN_LOADS)
            nc.vector.tensor_scalar(w4b[:, :], ones[0:2 * H3, :], w4s[:, :], None, ALU.mult)
            nc.vector.tensor_scalar(g3b[:, :], ones[0:H3, :], g3s[:, :], None, ALU.mult)
            nc.vector.tensor_scalar(cb4h[:, :], cb4[:, :], 0.5, None, ALU.mult)
            nc.vector.tensor_scalar(gb3h[:, :], gb3s[:, :], 0.5, None, ALU.mult)
            nc.vector.tensor_scalar(cpl_b[:, :], arange[:, :], 0.3, None, ALU.mult).then_inc(ffn_w_ready, 1)
            dve.wait_ge(ld_l1, 96)
            nc.vector.tensor_scalar(bv1_b[:, :], ones[:, :], bqkv1[:, 2:3], None, ALU.mult)
            dve.wait_ge(w1T_psum, 1)
            nc.vector.tensor_copy(wvT1[:, :], bank[5][:, 0:P]).then_inc(wv1T_ready, 1)
            nc.vector.tensor_copy(wrT[:, :], bank[5][:, P:P + EXPERTS])
            nc.vector.tensor_copy(wfcT[:, :, :], bank[3].rearrange("p (c e) -> p c e", c=TPC))
            nc.vector.tensor_tensor(wpr[:, :, :], bank[4].rearrange("p (c e) -> p c e", c=TPC),
                                    gate_row[:, 2, :].unsqueeze(1).to_broadcast([P, TPC, P]), ALU.mult)\
              .then_inc(wmoe_ready, 1)
            dve.wait_ge(wvp_psum, 1)
            nc.vector.tensor_tensor(wvp1[:, :], bank[5][:, 0:P], gate_row[:, 1, :], ALU.mult)
            link(nc.vector.tensor_tensor(add1_pre[:, :], bank[5][:, P:2 * P], bproj_row[:, :], ALU.add))
            nc.vector.tensor_tensor(add1_row[:, :], add1_pre[:, :], gate_row[:, 1, :], ALU.mult)\
              .then_inc(wvp_ready, 1)
            for g in range(G):
                dve.wait_ge(qkv_psum, 3 * g + 3)
                nc.vector.tensor_copy(v[:, g * TPC:(g + 1) * TPC, :],
                                      bank[3 * (g % 2) + 2].rearrange("p (t e) -> p t e", t=TPC)).then_inc(v_ready, 1)

            def row_max(i):
                n = nchunks(i)
                for c in range(n):
                    q = first_chunk(i) + c
                    w = width(i, c)
                    dve.wait_ge(score_psum, q + 1)
                    s = bank[q % SRING]
                    if c == n - 1:
                        link(nc.vector.tensor_tensor(s[:, w - P:w], s[:, w - P:w], causal[:, :], ALU.add))
                    last = nc.vector.reduce_max(mx[:, i, c:c + 1], s[:, 0:w], AX.X)
                link(last)
                link(nc.vector.reduce_max(mrow[:, i:i + 1], mx[:, i, 0:n], AX.X))
                nc.vector.tensor_scalar(negmax[:, i:i + 1], mrow[:, i:i + 1], -SCALE0, None, ALU.mult)\
                  .then_inc(negmax_ready, 1)

            def fetch_pT(i, c):
                q = first_chunk(i) + c
                n = width(i, c) // P
                dve.wait_ge(pT_psum, q + 1)
                nc.vector.tensor_copy(pT[:, q % 2, 0:n, :],
                                      bank[5 + q % 2][:, 0:n * P].rearrange("p (t q) -> p t q", t=n))\
                  .then_inc(pT_ready, 1)

            dve.wait_ge(consts_ready, 1)
            row_max(0)
            for i in range(T):
                n = nchunks(i)
                for c in range(min(2, n)):
                    fetch_pT(i, c)
                if i + 1 < T:
                    row_max(i + 1)
                for c in range(2, n):
                    fetch_pT(i, c)
                dve.wait_ge(exp_done, first_chunk(i + 1))
                link(nc.vector.reduce_sum(rsum[:, i:i + 1], rs[:, i, 0:n], AX.X))
                link(nc.vector.reciprocal(rinv[:, i:i + 1], rsum[:, i:i + 1]))
                dve.wait_ge(attn_psum, i + 1)
                dve.wait_ge(res_biased, i // TPC + 1)
                ins = nc.vector.scalar_tensor_tensor(out=xres[:, i, :], in0=bank[7][:, 0:P], scalar=rinv[:, i:i + 1],
                                                     in1=xres[:, i, :], op0=ALU.mult, op1=ALU.add)
                ins.then_inc(attn_added, 1)

            dve.wait_ge(attn_added, T)
            for g in range(G):
                ln_stats(1, g)
            for g in range(G):
                ln_norm(1, g)
            for g in range(G):
                dve.wait_ge(lnT_ready, G + g + 1)
                nc.vector.reduce_sum(ctx_parts[:, g:g + 1], yT[:, g * C:(g + 1) * C], AX.X).then_inc(y_ready, 1)
            dve.wait_ge(y_ready, G)
            link(nc.vector.reduce_sum(ctx_sum[:, :], ctx_parts[:, :], AX.X))
            nc.vector.tensor_scalar(ctx_mean[:, :], ctx_sum[:, :], 1.0 / S, None, ALU.mult).then_inc(ctx_ready, 1)
            dve.wait_ge(gc_ready, 3)
            link(nc.vector.tensor_scalar(cpl_a0[:, :], g_th[:, :], 0.7, None, ALU.mult))
            link(nc.vector.tensor_scalar(cpl_a1[:, :], cpl_a0[:, :], arange[:, :], None, ALU.mult))
            link(nc.vector.tensor_scalar(cpl_a[:, :], cpl_a1[:, :], 0.1, None, ALU.add))
            base = links[0]
            with dve.Fori(0, CYCLES) as cyc:
                for pr in range(2):
                    for u in range(2):
                        k = 2 * pr + u
                        dve.wait_ge(th_ready, cyc * 4 + (k + 1))
                        nc.vector.tensor_scalar(cpl[:, pr, u, :], th[:, pr, u, :], cpl_b[:, :], cpl_a[:, :],
                                                ALU.mult, ALU.add).then_inc(dve_chain, 1)
                        dve.wait_ge(dve_chain, cyc * 8 + (base + 2 * k + 1))
                        dve.wait_ge(tw_psum, cyc * 4 + (k + 1))
                        nc.vector.tensor_tensor(step[:, pr, u, :], cpl[:, pr, u, :], bank[6 + u], ALU.mult)\
                          .then_inc(dve_chain, 1)
                        dve.wait_ge(dve_chain, cyc * 8 + (base + 2 * k + 2))
                        ys = yT[:, k * C:(k + 1) * C]
                        nc.vector.tensor_tensor(ys, ys, step[:, pr, u, :], ALU.add).then_inc(y_ready, 1)
            links[0] = base + 8 * CYCLES
            dve.wait_ge(y_ready, G * (CYCLES + 1))
            for g in range(G):
                nc.vector.tensor_scalar(yT[:, g * C:(g + 1) * C], yT[:, g * C:(g + 1) * C], gb0_col[:, :], None,
                                        ALU.mult).then_inc(ffn_out_ready, 1)
            for g in range(G):
                dve.wait_ge(ffnT_psum, g + 1)
                xs = xres[:, g * TPC:(g + 1) * TPC, :]
                link(nc.vector.tensor_tensor(xs, xs, bank[4 + g % 2].rearrange("p (t e) -> p t e", t=TPC), ALU.add))
                ln_stats(2, g)
                ln_norm(2, g)

            for g in range(G):
                dve.wait_ge(qkv_psum, 3 * G + 2 * g + 2)
                nc.vector.tensor_copy(v[:, g * TPC:(g + 1) * TPC, :],
                                      bank[2 * (g % 2) + 1].rearrange("p (t e) -> p t e", t=TPC)).then_inc(v_ready, 1)

            BLINKS = 5

            def bands(j, u, base):
                s = scores[:, u, :]
                edge = [e / SCALE1 for e in BAND_EDGES]
                dve.wait_ge(s1_ready, j * G + G)
                nc.vector.tensor_scalar(band[:, 0, :], s, edge[0], BAND_BASE, ALU.is_ge, ALU.add)
                nc.vector.tensor_scalar(band[:, 1, :], s, edge[1], BAND_STEPS[1], ALU.is_ge, ALU.mult)
                nc.vector.tensor_scalar(band[:, 2, :], s, edge[2], BAND_STEPS[2], ALU.is_gt, ALU.mult)
                nc.vector.tensor_scalar(band[:, 3, :], s, edge[3], BAND_STEPS[3], ALU.is_gt, ALU.mult)\
                  .then_inc(dve_chain, 1)
                dve.wait_ge(dve_chain, j * BLINKS + (base + 1))
                nc.vector.tensor_tensor(band_sum[:, 0, :], band[:, 0, :], band[:, 1, :], ALU.add)
                nc.vector.tensor_tensor(band_sum[:, 1, :], band[:, 2, :], band[:, 3, :], ALU.add)\
                  .then_inc(dve_chain, 1)
                dve.wait_ge(dve_chain, j * BLINKS + (base + 2))
                nc.vector.tensor_tensor(mult[:, :], band_sum[:, 0, :], band_sum[:, 1, :], ALU.add)\
                  .then_inc(dve_chain, 1)
                dve.wait_ge(dve_chain, j * BLINKS + (base + 3))
                nc.vector.memset(wait_holder[:, :], 0.0)
                nc.vector.tensor_tensor_reduce(out=s, in0=mult[:, :], in1=s, scale=1.0, scalar=-3.0e38,
                                               op0=ALU.mult, op1=ALU.max, accum_out=max1[:, u:u + 1])\
                  .then_inc(dve_chain, 1)
                dve.wait_ge(dve_chain, j * BLINKS + (base + 4))
                nc.vector.tensor_scalar(negmax1[:, u:u + 1], max1[:, u:u + 1], -BAND_UNIT * SCALE1, None, ALU.mult)\
                  .then_inc(bands_done, 1)

            def add_attention(j, u, base):
                dve.wait_ge(exp1_done, j + 1)
                nc.vector.reciprocal(rinv1[:, u:u + 1], rsum1[:, u:u + 1]).then_inc(dve_chain, 1)
                dve.wait_ge(dve_chain, j * BLINKS + (base + BLINKS + 4 + 1))
                dve.wait_ge(attn1_psum, j + 1)
                xs = xres[:, bass.ds(j, 1), :].rearrange("p a d -> p (a d)")
                nc.vector.scalar_tensor_tensor(out=xs, in0=bank[6][:, 0:P], scalar=rinv1[:, u:u + 1], in1=xs,
                                               op0=ALU.mult, op1=ALU.add).then_inc(attn1_added, 1)

            dve.wait_ge(res_biased, 2 * G)
            base = links[0]
            bands(0, 0, base)
            with dve.Fori(0, T // 2 - 1) as pair:
                for u in range(2):
                    bands(pair * 2 + (u + 1), (u + 1) % 2, base - 1)
                    add_attention(pair * 2 + u, u, base - 1)
            bands(T - 1, 1, base - 1)
            add_attention(T - 2, 0, base - 1)
            dve.wait_ge(exp1_done, T)
            nc.vector.reciprocal(rinv1[:, 1:2], rsum1[:, 1:2]).then_inc(dve_chain, 1)
            links[0] = base + 4 * T + T
            dve.wait_ge(dve_chain, links[0])
            dve.wait_ge(attn1_psum, T)
            nc.vector.scalar_tensor_tensor(out=xres[:, T - 1, :], in0=bank[6][:, 0:P], scalar=rinv1[:, 1:2],
                                           in1=xres[:, T - 1, :], op0=ALU.mult, op1=ALU.add).then_inc(attn1_added, 1)

            dve.wait_ge(attn1_added, T)
            for g in range(G):
                ln_stats(3, g)
            for g in range(G):
                ln_norm(3, g)
            for g in range(G):
                ts = slice(g * TPC, (g + 1) * TPC)
                dve.wait_ge(lg_psum, g + 1)
                lgp = bank[5][:, 0:TPC * EXPERTS].rearrange("p (t e) -> p t e", t=TPC)
                link(nc.vector.tensor_copy(lg[:, ts, :], lgp))
                link(nc.vector.reduce_max(lgmax[:, ts], lg[:, ts, :], AX.X))
                link(nc.vector.tensor_tensor(ranked[:, ts, :], lg[:, ts, :],
                                             lgmax[:, ts].unsqueeze(2).to_broadcast([P, TPC, EXPERTS]), ALU.is_ge))
                link(nc.vector.tensor_tensor(ranked[:, ts, :], ranked[:, ts, :], tie_rank[:, :, :], ALU.mult))
                link(nc.vector.reduce_max(best[:, ts], ranked[:, ts, :], AX.X))
                nc.vector.tensor_tensor(onehot[:, ts, :], ranked[:, ts, :],
                                        best[:, ts].unsqueeze(2).to_broadcast([P, TPC, EXPERTS]), ALU.is_equal)\
                  .then_inc(onehot_ready, 1)
                for c in range(TPC):
                    n = g * TPC + c
                    dve.wait_ge(relu_ready, n + 1)
                    link(nc.vector.tensor_tensor(lrelu2[:, n % 2, :], bank[n % 2], relu_h[:, n % 2, :], ALU.add))
                    dve.wait_ge(mask_psum, n + 1)
                    if n >= 2:
                        dve.wait_ge(act_ready, n - 1)
                    nc.vector.tensor_tensor(picked[:, n % 2, :], lrelu2[:, n % 2, :], bank[2 + n % 2], ALU.mult)\
                      .then_inc(picked_ready, 1)
                dve.wait_ge(moe_psum, g + 1)
                xs = xres[:, ts, :]
                nc.vector.tensor_tensor(xs, xs, bank[4].rearrange("p (t e) -> p t e", t=TPC), ALU.add)\
                  .then_inc(out_ready, 1)

        @block.tensor
        def _(pe):
            mm = nc.tensor.matmul
            tr = nc.tensor.transpose

            pe.wait_ge(consts_ready, 1)
            pe.wait_ge(ld_attn0, 96)
            for n in range(3):
                last = tr(bank[0][:, n * P:(n + 1) * P], wqkv0_raw[:, n, :], ident[:, :])
            last.then_inc(w0T_psum, 1)
            pe.wait_ge(silu_ready, 1)
            for n in range(2):
                for j in range(6):
                    mm(bank[1][:, 6 * n + j:6 * n + j + 1], wmod[:, n, j * P:(j + 1) * P], silu_b[:, n, 0:1],
                       start=True, stop=True)
            for r, (n, j) in enumerate(((0, 2), (1, 2), (1, 5))):
                last = mm(bank[2][:, r * P:(r + 1) * P], silu_b[:, n, :], wmod[:, n, j * P:(j + 1) * P],
                          start=True, stop=True)
            last.then_inc(mod_psum, 1)

            def ln_transpose(ph, g):
                n = ph * G + g
                pe.wait_ge(norm_ready, n + 1)
                if n >= 2:
                    pe.wait_ge(lnT_ready, n - 1)
                for t in range(TPC):
                    last = tr(bank[6 + n % 2][:, t * P:(t + 1) * P], nrm[:, g, t, :], ident[:, :])
                last.then_inc(lnT_psum, 1)

            pe.wait_ge(mod_ready, 1)
            for g in range(G):
                hc = hT[:, g * C:(g + 1) * C]
                if g == 0:
                    ln_transpose(0, 0)
                if g + 1 < G:
                    ln_transpose(0, g + 1)
                if g >= 2:
                    pe.wait_ge(qk_ready, 2 * (g - 1))
                    pe.wait_ge(v_ready, g - 1)
                elif g == 1:
                    pe.wait_ge(wvp_ready, 1)
                pe.wait_ge(lnT_ready, g + 1)
                for n in range(2):
                    mm(bank[3 * (g % 2) + n], wqkvT0[:, n, :], hc, start=True, stop=True).then_inc(qkv_psum, 1)
                for t in range(TPC):
                    last = mm(bank[3 * (g % 2) + 2][:, t * P:(t + 1) * P], hT[:, g * C + t * P:g * C + (t + 1) * P],
                              wqkvT0[:, 2, :], start=True, stop=True)
                last.then_inc(qkv_psum, 1)
                if g == 0:
                    pe.wait_ge(ld_l1, 96)
                    pe.wait_ge(ld_moe, 96)
                    for c in range(TPC):
                        tr(bank[3][:, c * P:(c + 1) * P], wfc_raw[:, c, :], ident[:, :])
                        tr(bank[4][:, c * P:(c + 1) * P],
                           wpr_raw[:, 2 * c:2 * c + 2, :].rearrange("p u h -> p (u h)"), ident[:, :])
                    tr(bank[5][:, 0:P], wqkv1[:, 2, :], ident[:, :])
                    tr(bank[5][:, P:P + EXPERTS], wr_raw[:, :], ident[0:EXPERTS, 0:EXPERTS]).then_inc(w1T_psum, 1)
                    pe.wait_ge(wv1T_ready, 1)
                    pe.wait_ge(wmoe_ready, 1)
                    mm(bank[5][:, 0:P], wvT1[:, :], wproj1[:, :], start=True, stop=True)
                    mm(bank[5][:, P:2 * P], bv1_b[:, :], wproj1[:, :], start=True, stop=True).then_inc(wvp_psum, 1)

            def score_chunks(i):
                for c in range(nchunks(i)):
                    q = first_chunk(i) + c
                    w = width(i, c)
                    if q >= SRING:
                        pe.wait_ge(exp_done, q - SRING + 1)
                    mm(bank[q % SRING][:, 0:w], qT[:, i * P:(i + 1) * P], kT[:, c * C:c * C + w],
                       start=True, stop=True).then_inc(score_psum, 1)

            def transpose_probs(i, c):
                q = first_chunk(i) + c
                pe.wait_ge(exp_done, q + 1)
                if q >= 2:
                    pe.wait_ge(pT_ready, q - 1)
                for b in range(width(i, c) // P):
                    last = tr(bank[5 + q % 2][:, b * P:(b + 1) * P],
                              probs[:, i % 2, c * C + b * P:c * C + (b + 1) * P], ident[:, :])
                last.then_inc(pT_psum, 1)

            def weigh_values(i, c):
                q = first_chunk(i) + c
                pe.wait_ge(pT_ready, q + 1)
                if c == 0 and i >= 1:
                    pe.wait_ge(attn_added, i)
                for b in range(width(i, c) // P):
                    k = c * TPC + b
                    last = mm(bank[7][:, 0:P], pT[:, q % 2, b, :], v[:, k, :], start=(k == 0), stop=(k == i))
                if c == nchunks(i) - 1:
                    last.then_inc(attn_psum, 1)

            pe.wait_ge(lnT_ready, G)
            pe.wait_ge(qk_ready, 2 * G)
            pe.wait_ge(v_ready, G)
            score_chunks(0)
            for i in range(T):
                n = nchunks(i)
                for c in range(min(2, n)):
                    transpose_probs(i, c)
                if i + 1 < T:
                    score_chunks(i + 1)
                for c in range(n):
                    weigh_values(i, c)
                    if c + 2 < n:
                        transpose_probs(i, c + 2)

            pe.wait_ge(attn_added, T)
            for g in range(G):
                ln_transpose(1, g)
            pe.wait_ge(ffn_w_ready, 1)
            pe.wait_ge(ctx_ready, 1)
            pe.wait_ge(lnT_ready, 2 * G)
            mm(bank[7][0:H2, 0:1], g1s[:, :], ctx_mean[:, :], start=True, stop=True).then_inc(gc_psum, 1)
            pe.wait_ge(gc_ready, 1)
            mm(bank[7][0:H3, 0:1], g2s[:, :], g_a1[:, :], start=True, stop=True).then_inc(gc_psum, 1)
            pe.wait_ge(gc_ready, 2)
            mm(bank[7][:, 0:1], g3b[:, :], g_a2[:, :], start=True, stop=True).then_inc(gc_psum, 1)
            pe.wait_ge(gc_ready, 3)
            with pe.Fori(0, CYCLES) as cyc:
                for pr in range(2):
                    for u in range(2):
                        k = 2 * pr + u
                        pe.wait_ge(y_ready, cyc * 4 + (k + 1))
                        if pr == 1:
                            pe.wait_ge(h1_ready, cyc * 4 + (u + 1))
                        mm(bank[u], w1s[:, :], yT[:, k * C:(k + 1) * C], start=True, stop=True).then_inc(h1_psum, 1)
                for pr in range(2):
                    if pr == 1:
                        pe.wait_ge(h2_ready, cyc * 2 + 1)
                    for u in range(2):
                        pe.wait_ge(h1_ready, cyc * 4 + (2 * pr + u + 1))
                        last = mm(bank[2][u * H2:(u + 1) * H2, :], w2s[:, :], a1[:, pr, u, :], start=True, stop=True)
                    last.then_inc(h2_psum, 1)
                for pr in range(2):
                    pe.wait_ge(h2_ready, cyc * 2 + (pr + 1))
                    if pr == 1:
                        pe.wait_ge(h3_ready, cyc * 2 + 1)
                    mm(bank[3][0:2 * H3, :], w3s[:, :], a2[:, pr, :], start=True, stop=True).then_inc(h3_psum, 1)
                for pr in range(2):
                    pe.wait_ge(h3_ready, cyc * 2 + (pr + 1))
                    for u in range(2):
                        k = 2 * pr + u
                        pe.wait_ge(y_ready, cyc * 4 + (4 * pr + 2 * (1 - pr) + u + 1))
                        mm(bank[4 + u], w4b[u * H3:(u + 1) * H3, :], a3[u * H3:(u + 1) * H3, pr, :],
                           start=True, stop=True).then_inc(z_psum, 1)
                        mm(bank[6 + u], twist[:, :], yT[:, k * C:(k + 1) * C], start=True, stop=True)\
                          .then_inc(tw_psum, 1)
            for g in range(G):
                pe.wait_ge(ffn_out_ready, g + 1)
                if g == 0:
                    pe.wait_ge(y_ready, G * (CYCLES + 1))
                if g >= 2:
                    pe.wait_ge(stats_ready, 2 * G + g - 1)
                for t in range(TPC):
                    last = tr(bank[4 + g % 2][:, t * P:(t + 1) * P],
                              yT[:, g * C + t * P:g * C + (t + 1) * P], ident[:, :])
                last.then_inc(ffnT_psum, 1)

            pe.wait_ge(wvp_ready, 1)
            for g in range(G):
                ln_transpose(2, g)
                if g >= 2:
                    pe.wait_ge(qk_ready, 2 * G + g - 1)
                    pe.wait_ge(v_ready, G + g - 1)
                pe.wait_ge(lnT_ready, 2 * G + g + 1)
                mm(bank[2 * (g % 2)], wqkv1[:, 1, :], hT[:, g * C:(g + 1) * C], start=True, stop=True)\
                  .then_inc(qkv_psum, 1)
                for t in range(TPC):
                    last = mm(bank[2 * (g % 2) + 1][:, t * P:(t + 1) * P],
                              hT[:, g * C + t * P:g * C + (t + 1) * P], wvp1[:, :], start=True, stop=True)
                last.then_inc(qkv_psum, 1)

            def score_tile(j, u, first):
                if not first:
                    pe.wait_ge(q1_ready, j)
                mm(bank[7][:, 0:P], wqkv1[:, 0, :], hT[:, bass.ds(j * P, P)], start=True, stop=True)\
                  .then_inc(q1_psum, 1)
                pe.wait_ge(q1_ready, j + 1)
                for c in range(G):
                    if not first:
                        pe.wait_ge(s1_ready, (j - 1) * G + (c + 1))
                    mm(bank[c], qbuf[:, u, :], kT[:, c * C:(c + 1) * C], start=True, stop=True).then_inc(s1_psum, 1)

            def attend(j, u, first=False):
                pe.wait_ge(exp1_done, j + 1)

                def turn(c):
                    if not (first and c < 2):
                        pe.wait_ge(p1T_ready, j * G + (c - 1))
                    for b in range(TPC):
                        last = tr(bank[4 + c % 2][:, b * P:(b + 1) * P],
                                  probs[:, u, c * C + b * P:c * C + (b + 1) * P], ident[:, :])
                    last.then_inc(p1T_psum, 1)

                turn(0)
                turn(1)
                for c in range(G):
                    pe.wait_ge(p1T_ready, j * G + (c + 1))
                    if c == 0 and not first:
                        pe.wait_ge(attn1_added, j)
                    for b in range(TPC):
                        k = c * TPC + b
                        last = mm(bank[6][:, 0:P], pT[:, c % 2, b, :], v[:, k, :], start=(k == 0), stop=(k == T - 1))
                    if c == G - 1:
                        last.then_inc(attn1_psum, 1)
                    elif c + 2 < G:
                        turn(c + 2)

            pe.wait_ge(lnT_ready, 3 * G)
            pe.wait_ge(qk_ready, 3 * G)
            pe.wait_ge(v_ready, 2 * G)
            score_tile(0, 0, True)
            score_tile(1, 1, False)
            for u in range(2):
                attend(u, u, first=(u == 0))
                score_tile(2 + u, u, False)
            with pe.Fori(1, T // 2 - 1) as pair:
                for u in range(2):
                    attend(pair * 2 + u, u)
                    score_tile(pair * 2 + (u + 2), u, False)
            for u in range(2):
                attend(T - 2 + u, u)

            pe.wait_ge(wmoe_ready, 1)
            pe.wait_ge(attn1_added, T)
            pe.wait_ge(s1_ready, G * T)
            pe.wait_ge(p1T_ready, G * T)
            pe.wait_ge(q1_ready, T)
            for g in range(G):
                ln_transpose(3, g)
                pe.wait_ge(lnT_ready, 3 * G + g + 1)
                if g >= 1:
                    pe.wait_ge(onehot_ready, g)
                for t in range(TPC):
                    last = mm(bank[5][:, t * EXPERTS:(t + 1) * EXPERTS], hT[:, g * C + t * P:g * C + (t + 1) * P],
                              wrT[:, :], start=True, stop=True)
                last.then_inc(lg_psum, 1)
                pe.wait_ge(onehot_ready, g + 1)
                for t in range(TPC):
                    last = tr(ohT_ps[0:EXPERTS, t * P:(t + 1) * P], onehot[:, g * TPC + t, :], identb[:, :])
                last.then_inc(ohT_psum, 1)
                pe.wait_ge(ohT_ready, g + 1)
                for c in range(TPC):
                    n = g * TPC + c
                    if n >= 2:
                        pe.wait_ge(picked_ready, n - 1)
                    mm(bank[n % 2], wfcT[:, c, :], hT[:, g * C:(g + 1) * C], start=True, stop=True).then_inc(fc_psum, 1)
                    mm(bank[2 + n % 2], expert_sel[:, c, :, :].rearrange("p u h -> p (u h)"), ohT[:, g % 2, :],
                       start=True, stop=True).then_inc(mask_psum, 1)
                pe.wait_ge(act_ready, (g + 1) * TPC)
                if g >= 1:
                    pe.wait_ge(out_ready, g)
                for t in range(TPC):
                    for c in range(TPC):
                        last = mm(bank[4][:, t * P:(t + 1) * P], act2[:, g % 2, c, t * P:(t + 1) * P], wpr[:, c, :],
                                  start=(c == 0), stop=(c == TPC - 1))
                last.then_inc(moe_psum, 1)


_INS = ['L0_attn_x', 'L0_attn_Wq', 'L0_attn_bq', 'L0_attn_Wk', 'L0_attn_bk', 'L0_attn_Wv', 'L0_attn_bv',
        'L0_ffn_cn_w1', 'L0_ffn_cn_b1', 'L0_ffn_cn_w2', 'L0_ffn_cn_b2', 'L0_ffn_cn_w3', 'L0_ffn_cn_b3',
        'L0_ffn_cn_w4', 'L0_ffn_cn_b4', 'L0_ffn_gc_w1', 'L0_ffn_gc_b1', 'L0_ffn_gc_w2', 'L0_ffn_gc_b2',
        'L0_ffn_gc_w3', 'L0_ffn_gc_b3', 'L0_ffn_adaptive_range', 'L0_c', 'L0_wmod', 'L1_attn_W_qkv',
        'L1_attn_b_qkv', 'L1_attn_W_proj', 'L1_attn_b_proj', 'L1_ffn_w_router', 'L1_ffn_w_fc', 'L1_ffn_w_proj',
        'L1_c', 'L1_wmod']


def kernel(**inputs):
    import numpy as np
    import concourse.bacc as bacc
    from concourse.bass_utils import run_bass_kernel_spmd

    nc = bacc.Bacc("TRN2", target_bir_lowering=False, num_devices=1)
    arrays, args = {}, []
    for name in _INS:
        a = np.ascontiguousarray(inputs[name])
        arrays[f"in_{name}"] = a
        args.append(nc.dram_tensor(f"in_{name}", a.shape, mybir.dt.from_np(a.dtype), kind="ExternalInput").ap())
    shape = inputs['L0_attn_x'].shape
    args.append(nc.dram_tensor("out", shape, F32, kind="ExternalOutput").ap())
    build(nc, *args)
    r = run_bass_kernel_spmd(nc, [arrays], core_ids=[0])
    return r.results[0]["out"]
```

```python
from contextlib import ExitStack

import concourse.bass as bass
from concourse import mybir

P = 128
C = 512
TPC = C // P

ALU = mybir.AluOpType
ACT = mybir.ActivationFunctionType
AX = mybir.AxisListType
F32 = mybir.dt.float32
BF16 = mybir.dt.bfloat16

LN_EPS = 1e-5
GATE_FLOOR = 0.25
MASKED = -1e30
CYCLES = 3
HEAD_DIM_L1 = 8
EXPERTS = 8

BAND_EDGES = (-2.1972245773362196, -1.0986122886681098, 1.7346010553881064, 2.9444389791664403)
BAND_STEPS = (2.0, 7.0, 2.5)
BAND_BASE = 6.0
BAND_UNIT = 0.1


def build(nc, x, Wq, bq, Wk, bk, Wv, bv, cn_w1, cn_b1, cn_w2, cn_b2, cn_w3, cn_b3, cn_w4, cn_b4,
          gc_w1, gc_b1, gc_w2, gc_b2, gc_w3, gc_b3, adaptive_range, c0, wmod0,
          W_qkv, b_qkv, W_proj, b_proj, w_router, w_fc, w_proj, c1, wmod1, out):
    _, S, D = x.shape
    T = S // P
    G = S // C
    H2, H3 = cn_w2.shape[1], cn_w3.shape[1]
    assert D == P and H2 == 64 and H3 == 32 and T == 16
    SCALE0 = float(D) ** -0.5
    SCALE1 = float(HEAD_DIM_L1) ** -0.5

    with ExitStack() as ctx:
        def sb(name, shape, dt=F32):
            return ctx.enter_context(nc.sbuf_tensor(name, shape, dt))

        def sem(name):
            return ctx.enter_context(nc.semaphore(name))

        xres = sb("xres", [P, T, D])
        yT = sb("yT", [P, S])
        hT = sb("hT", [P, S])
        qT = sb("qT", [P, S])
        kT = sb("kT", [P, S])
        v = sb("v", [P, T, D])
        ident = sb("ident", [P, P])
        identb = sb("identb", [P, P], BF16)
        causal = sb("causal", [P, P], BF16)
        twist = sb("twist", [P, P])
        ones = sb("ones", [P, P])
        neghalf = sb("neghalf", [P, TPC])
        epsilon = sb("epsilon", [P, TPC])
        expert_sel = sb("expert_sel", [EXPERTS, TPC, 2, 64], BF16)
        tie_rank = sb("tie_rank", [P, T, EXPERTS])
        wqkv0_raw = sb("wqkv0_raw", [P, 3, P])
        wqkvT0 = sb("wqkvT0", [P, 3, P])
        bqk0 = sb("bqk0", [P, 2])
        bq0_scaled = sb("bq0_scaled", [P, 1])
        wvT0_raw = sb("wvT0_raw", [P, P])
        bv_row = sb("bv_row", [P, P])
        c_col = sb("c_col", [P, 2])
        tanh_c = sb("tanh_c", [P, 2])
        silu_col = sb("silu_col", [P, 2])
        silu_b = sb("silu_b", [P, 2, P])
        wmod = sb("wmod", [P, 2, 6 * P])
        mod_raw = sb("mod_raw", [P, 3, P])
        modc = sb("modc", [P, 2, 6])
        modp = sb("modp", [P, 2, 6])
        gate_sign = sb("gate_sign", [P, 3, P])
        gate_mag = sb("gate_mag", [P, 3, P])
        gate_row = sb("gate_row", [P, 3, P])
        gcol_sign = sb("gcol_sign", [P, 1])
        gcol_mag = sb("gcol_mag", [P, 1])
        gb0_col = sb("gb0_col", [P, 1])
        gb0_diag = sb("gb0_diag", [P, P])
        w1s = sb("w1s", [P, P])
        w2s = sb("w2s", [P, H2])
        w3s = sb("w3s", [P, 2 * H3])
        w4s = sb("w4s", [2 * H3, 1])
        w4b = sb("w4b", [2 * H3, P])
        g1s = sb("g1s", [P, H2])
        g2s = sb("g2s", [H2, H3])
        g3s = sb("g3s", [H3, 1])
        g3b = sb("g3b", [H3, P])
        cb1 = sb("cb1", [P, 1])
        cb2 = sb("cb2", [P, 1])
        cb3 = sb("cb3", [2 * H3, 1])
        cb4 = sb("cb4", [P, 1])
        cb4h = sb("cb4h", [P, 1])
        gb1s = sb("gb1s", [H2, 1])
        gb2s = sb("gb2s", [H3, 1])
        gb3s = sb("gb3s", [P, 1])
        gb3h = sb("gb3h", [P, 1])
        arange = sb("arange", [P, 1])
        ctx_parts = sb("ctx_parts", [P, G])
        ctx_sum = sb("ctx_sum", [P, 1])
        ctx_mean = sb("ctx_mean", [P, 1])
        g_a1 = sb("g_a1", [H2, 1])
        g_a2 = sb("g_a2", [H3, 1])
        g_th = sb("g_th", [P, 1])
        cpl_a0 = sb("cpl_a0", [P, 1])
        cpl_a1 = sb("cpl_a1", [P, 1])
        cpl_a = sb("cpl_a", [P, 1])
        cpl_b = sb("cpl_b", [P, 1])
        wqkv1 = sb("wqkv1", [P, 3, P])
        bqkv1 = sb("bqkv1", [P, 3])
        bv1_b = sb("bv1_b", [P, P])
        wproj1 = sb("wproj1", [P, P])
        bproj_row = sb("bproj_row", [P, P])
        wvT1 = sb("wvT1", [P, P])
        wvp1 = sb("wvp1", [P, P])
        add0_row = sb("add0_row", [P, P])
        add1_pre = sb("add1_pre", [P, P])
        add1_row = sb("add1_row", [P, P])
        wr_raw = sb("wr_raw", [EXPERTS, P])
        wrT = sb("wrT", [P, EXPERTS])
        wfc_raw = sb("wfc_raw", [P, TPC, P])
        wfcT = sb("wfcT", [P, TPC, P])
        wpr_raw = sb("wpr_raw", [P, EXPERTS, 64])
        wpr = sb("wpr", [P, TPC, P])
        st = sb("st", [P, 4 * T, 6])
        mv = sb("mv", [P, 4 * T, 2])
        veps = sb("veps", [P, 4 * T])
        rstd = sb("rstd", [P, 4 * T])
        nrm = sb("nrm", [P, G, TPC, P])
        probs = sb("probs", [P, 2, S])
        pT = sb("pT", [P, 4, TPC, P])
        mx = sb("mx", [P, T, G])
        negmax = sb("negmax", [P, T])
        rs = sb("rs", [P, T, G])
        rsum = sb("rsum", [P, T])
        rinv = sb("rinv", [P, T])
        scores = sb("scores", [P, 2, S])
        band = sb("band", [P, 4, S], BF16)
        band_sum = sb("band_sum", [P, 2, S], BF16)
        sign = sb("sign", [P, 2, 2, S], BF16)
        mult = sb("mult", [P, S], BF16)
        edge_bias = sb("edge_bias", [P, 2])
        qbuf = sb("qbuf", [P, 2, P])
        max1 = sb("max1", [P, 2])
        negmax1 = sb("negmax1", [P, 2])
        rsum1 = sb("rsum1", [P, 2])
        rinv1 = sb("rinv1", [P, 2])
        attended = sb("attended", [P, TPC, D])
        vT = qT
        q1T = qT
        a1 = scores[:, 0, :].rearrange("p (r u t) -> p r u t", r=2, u=2)
        th = scores[:, 1, :].rearrange("p (r u t) -> p r u t", r=2, u=2)
        cpl = band[:, 0:2, :].rearrange("p b t -> p (b t)").bitcast(F32).rearrange("p (r u t) -> p r u t", r=2, u=2)
        gain = band[:, 2:4, :].rearrange("p b t -> p (b t)").bitcast(F32).rearrange("p (r u t) -> p r u t", r=2, u=2)
        loss = sign[:, 0, :, :].rearrange("p b t -> p (b t)").bitcast(F32).rearrange("p (r u t) -> p r u t", r=2, u=2)
        a2 = sb("a2", [P, 2, C])
        a3 = sb("a3", [2 * H3, 2, C])
        warm = sb("warm", [P, 1])
        lg = sb("lg", [P, T, EXPERTS])
        lgmax = sb("lgmax", [P, T])
        ranked = sb("ranked", [P, T, EXPERTS])
        best = sb("best", [P, T])
        onehot = sb("onehot", [P, T, EXPERTS], BF16)
        ohT = sb("ohT", [EXPERTS, S], BF16)
        relu_h = scores[:, 0, 0:2 * C].rearrange("p (r t) -> p r t", r=2)
        lrelu2 = scores[:, 0, 2 * C:4 * C].rearrange("p (r t) -> p r t", r=2)
        picked = scores[:, 1, 0:2 * C].rearrange("p (r t) -> p r t", r=2)
        probs0 = [probs[:, 0, :], probs[:, 1, :], scores[:, 0, :]]
        act2 = probs[:, :, :].rearrange("p b (c t) -> p b c t", c=TPC)

        sc4 = ctx.enter_context(nc.psum_tensor("sc4", [P, 4, C], F32))
        b4 = ctx.enter_context(nc.psum_tensor("b4", [P, C], F32))
        b5 = ctx.enter_context(nc.psum_tensor("b5", [P, C], F32))
        b6 = ctx.enter_context(nc.psum_tensor("b6", [P, C], F32))
        b7 = ctx.enter_context(nc.psum_tensor("b7", [P, C], F32))
        bank = [sc4[:, i, :] for i in range(4)] + [b[:, :] for b in (b4, b5, b6, b7)]
        oh_ps = [bank[0].bitcast(BF16), b6[:, :].bitcast(BF16)]

        ld_x = [sem(f"ld_x{g}") for g in range(G)]
        ld_attn0 = sem("ld_attn0")
        ld_bias0 = sem("ld_bias0")
        ld_c = sem("ld_c")
        ld_wmod = [sem(f"ld_wmod{n}") for n in range(3)]
        ld_ffn0 = sem("ld_ffn0")
        ld_l1 = sem("ld_l1")
        ld_moe = sem("ld_moe")
        pool_chain = sem("pool_chain")
        ident_ready = sem("ident_ready")
        causal_ready = sem("causal_ready")
        consts_ready = sem("consts_ready")
        tanh_c_ready = sem("tanh_c_ready")
        silu_ready = sem("silu_ready")
        w0T_psum = sem("w0T_psum")
        w0T_ready = sem("w0T_ready")
        mod_psum = sem("mod_psum")
        mod_fetched = sem("mod_fetched")
        mod_ready = sem("mod_ready")
        w1T_psum = sem("w1T_psum")
        wv1T_ready = sem("wv1T_ready")
        wmoe_ready = sem("wmoe_ready")
        wvp_psum = sem("wvp_psum")
        wvp_ready = sem("wvp_ready")
        dve_chain = sem("dve_chain")
        act_chain = sem("act_chain")
        ffn_w_ready = sem("ffn_w_ready")
        bias_row_ready = sem("bias_row_ready")
        stats_ready = sem("stats_ready")
        rstd_ready = sem("rstd_ready")
        norm_ready = sem("norm_ready")
        side_psum = sem("side_psum")
        side_ready = sem("side_ready")
        lnT_psum = sem("lnT_psum")
        lnT_ready = sem("lnT_ready")
        kv_psum = sem("kv_psum")
        kv_ready = sem("kv_ready")
        res_biased = sem("res_biased")
        score_psum = sem("score_psum")
        negmax_ready = sem("negmax_ready")
        exp_done = sem("exp_done")
        pT_psum = sem("pT_psum")
        pT_ready = sem("pT_ready")
        attn_psum = sem("attn_psum")
        attn_added = sem("attn_added")
        h1_psum = [sem(f"h1_psum{r}") for r in range(2)]
        h1_ready = [sem(f"h1_ready{r}") for r in range(2)]
        h2_psum = [sem(f"h2_psum{r}") for r in range(2)]
        h2_ready = [sem(f"h2_ready{r}") for r in range(2)]
        h3_psum = [sem(f"h3_psum{r}") for r in range(2)]
        h3_ready = [sem(f"h3_ready{r}") for r in range(2)]
        z_psum = [sem(f"z_psum{r}") for r in range(2)]
        th_ready = [sem(f"th_ready{r}") for r in range(2)]
        y_ready = [sem(f"y_ready{r}") for r in range(2)]
        tw_psum = sem("tw_psum")
        tw_ready = sem("tw_ready")
        ctx_ready = sem("ctx_ready")
        gc_psum = sem("gc_psum")
        gc_ready = sem("gc_ready")
        gain_ready = sem("gain_ready")
        ffnT_psum = sem("ffnT_psum")
        q1_ready = sem("q1_ready")
        bn_done = sem("bn_done")
        s1_psum = sem("s1_psum")
        s1_ready = sem("s1_ready")
        signs_ready = sem("signs_ready")
        bands_done = sem("bands_done")
        exp1_done = sem("exp1_done")
        p1T_psum = sem("p1T_psum")
        p1T_ready = sem("p1T_ready")
        attn1_psum = sem("attn1_psum")
        attn1_added = sem("attn1_added")
        lg_psum = sem("lg_psum")
        onehot_ready = sem("onehot_ready")
        ohT_psum = sem("ohT_psum")
        ohT_ready = sem("ohT_ready")
        fc_psum = sem("fc_psum")
        mask_psum = sem("mask_psum")
        relu_ready = sem("relu_ready")
        picked_ready = sem("picked_ready")
        act_ready = sem("act_ready")
        moe_psum = sem("moe_psum")
        out_ready = sem("out_ready")
        stored = sem("stored")

        def nchunks(i):
            return (i + TPC) // TPC

        def first_chunk(i):
            return sum(nchunks(j) for j in range(i))

        def width(i, c):
            return min(C, (i + 1) * P - c * C)

        SRING = 4
        REST = ((0, 3), (0, 4), (0, 5), (1, 0), (1, 1), (1, 3), (1, 4))
        KV_RING = (2, 3, 0, 1)
        KV_JOBS = 2 * G + 1
        TWIST_BANK = (6, 0, 1, 7)
        FFN_OUT_BANK = (0, 1, 4, 5)
        TURN_BANK = (4, 5, 7, 4)
        LAST_LN_BANK = [bank[b] for b in (5, 7, 0, 7)]
        LOGIT_BANK = 1
        FC_BANK = (2, 3)
        PICK_BANK = (5, 0)
        ONEHOT_PARTS = ((0, 8), (8, 12), (12, 16))

        def onehot_psum(h):
            a, b = ONEHOT_PARTS[h]
            at = (0, 0, 4 * P)[h]
            return oh_ps[min(h, 1)][0:EXPERTS, at:at + (b - a) * P]
        QKV_JOBS = 4 * G

        def chunk_of(r, u):
            return 2 * (1 - r) + u

        def tiles_ahead(i):
            if i + 2 < 2 * TPC:
                return [i + 2]
            return [i + 1] if 2 * TPC <= i + 1 < T else []

        SIDE_STEPS = QKV_JOBS + G - 1 - 5
        def side_bank(j):
            return bank[4 + j] if j < 4 else bank[4]
        x_t = x.rearrange("a (t p) d -> p (a t) d", p=P)
        out_t = out.rearrange("a (t p) d -> p (a t) d", p=P)

        def col(w):
            return w.rearrange("(p a) -> p a", a=1)

        block = ctx.enter_context(nc.Block())

        @block.sync
        def _(sp):
            sp.dma_start(xres[:, 0:TPC, :], x_t[:, 0:TPC, :]).then_inc(ld_x[0], 16)
            sp.dma_start(wmod[:, 0, 0:3 * P], wmod0[:, 0:3 * P]).then_inc(ld_wmod[0], 16)
            for n, w in enumerate((Wq, Wk, Wv)):
                sp.dma_start(wqkv0_raw[:, n, :], w).then_inc(ld_attn0, 16)
            for g in range(1, G):
                sp.dma_start(xres[:, g * TPC:(g + 1) * TPC, :],
                             x_t[:, g * TPC:(g + 1) * TPC, :]).then_inc(ld_x[g], 16)
                if g == 1:
                    sp.dma_start(wmod[:, 0, 3 * P:6 * P], wmod0[:, 3 * P:6 * P]).then_inc(ld_wmod[1], 16)
                    sp.dma_start(wmod[:, 1, :], wmod1).then_inc(ld_wmod[2], 16)
            sp.dma_start(wqkv1[:, :, :], W_qkv.rearrange("d (n e) -> d n e", n=3)).then_inc(ld_l1, 16)
            sp.dma_start(wproj1[:, :], W_proj).then_inc(ld_l1, 16)
            sp.dma_start(bproj_row[:, :], b_proj.partition_broadcast(P)).then_inc(ld_l1, 16)
            for n in range(3):
                sp.dma_start(bqkv1[:, n:n + 1], col(b_qkv[n * P:(n + 1) * P])).then_inc(ld_l1, 16)
            sp.dma_start(wr_raw[:, :], w_router).then_inc(ld_moe, 16)
            for c in range(TPC):
                sp.dma_start(wfc_raw[:, c, :],
                             w_fc[2 * c:2 * c + 2, :, :].rearrange("u h d -> (u h) d")).then_inc(ld_moe, 16)
            sp.dma_start(wpr_raw[:, :, :], w_proj.rearrange("e d h -> d e h")).then_inc(ld_moe, 16)
            for dst, src in ((w1s[:, :], cn_w1), (w2s[:, :], cn_w2), (g1s[:, :], gc_w1), (g2s[:, :], gc_w2),
                             (g3s[:, :], gc_w3), (w4s[0:H3, :], cn_w4), (w4s[H3:2 * H3, :], cn_w4),
                             (cb1[:, :], col(cn_b1)), (cb2[0:H2, :], col(cn_b2)), (cb2[H2:P, :], col(cn_b2)),
                             (cb3[0:H3, :], col(cn_b3)), (cb3[H3:2 * H3, :], col(cn_b3)),
                             (cb4[:, :], cn_b4.partition_broadcast(P)), (gb1s[:, :], col(gc_b1)),
                             (gb2s[:, :], col(gc_b2)), (gb3s[:, :], gc_b3.partition_broadcast(P)),
                             (arange[:, :], adaptive_range.partition_broadcast(P))):
                sp.dma_start(dst, src).then_inc(ld_ffn0, 16)
            sp.wait_ge(consts_ready, 1)
            for u in range(2):
                sp.dma_start(w3s[u * H2:(u + 1) * H2, u * H3:(u + 1) * H3], cn_w3).then_inc(ld_ffn0, 16)
            for g in range(G):
                sp.wait_ge(out_ready, g + 1)
                sp.dma_start(out_t[:, g * TPC:(g + 1) * TPC, :],
                             xres[:, g * TPC:(g + 1) * TPC, :]).then_inc(stored, 16)
            sp.wait_ge(stored, 16 * G)
        FFN_LOADS = 19

        @block.gpsimd
        def _(pool):
            pool.memset(ident[:, :], 0.0)
            pool.memset(ones[:, :], 1.0)
            pool.memset(edge_bias[:, 0:1], -BAND_EDGES[2])
            pool.memset(edge_bias[:, 1:2], -BAND_EDGES[3])
            pool.memset(epsilon[:, :], LN_EPS)
            pool.memset(neghalf[:, :], -0.5).then_inc(pool_chain, 1)
            pool.wait_ge(pool_chain, 1)
            pool.affine_select(out=ident[:, :], in_=ident[:, :], compare_op=ALU.not_equal, fill=1.0,
                               base=0, pattern=[[-1, P]], channel_multiplier=1).then_inc(ident_ready, 1)
            pool.memset(causal[:, :], 0.0)
            pool.memset(identb[:, :], 0.0).then_inc(pool_chain, 1)
            pool.wait_ge(pool_chain, 2)
            pool.affine_select(out=identb[:, :], in_=identb[:, :], compare_op=ALU.not_equal, fill=1.0,
                               base=0, pattern=[[-1, P]], channel_multiplier=1)
            pool.affine_select(out=causal[:, :], in_=causal[:, :], compare_op=ALU.is_ge, fill=MASKED,
                               base=0, pattern=[[-1, P]], channel_multiplier=1).then_inc(causal_ready, 1)

            def ln_rstd(ph, g):
                n = ph * G + g
                s = slice(n * TPC, (n + 1) * TPC)
                pool.wait_ge(stats_ready, n + 1)
                pool.tensor_scalar(veps[:, s], mv[:, s, 1], LN_EPS, None, ALU.add).then_inc(pool_chain, 1)
                pool.wait_ge(pool_chain, n + (3 if ph == 0 else 4))
                pool.tensor_tensor(rstd[:, s], veps[:, s], neghalf[:, :], ALU.pow).then_inc(rstd_ready, 1)

            for g in range(G):
                ln_rstd(0, g)
            pool.memset(w3s[:, :], 0.0)
            pool.memset(twist[:, :], 0.0)
            for e in range(EXPERTS):
                pool.memset(tie_rank[:, :, e:e + 1], float(EXPERTS - e))
            pool.memset(expert_sel[:, :, :, :], 0.0).then_inc(pool_chain, 1)
            pool.wait_ge(pool_chain, 3 + G)
            for j0, src, sgn in ((0, 64, 1.0), (32, 96, -1.0), (64, 0, -1.0), (96, 32, 1.0)):
                pool.affine_select(out=twist[:, j0:j0 + 32], in_=twist[:, j0:j0 + 32],
                                   compare_op=ALU.not_equal, fill=sgn, base=-src,
                                   pattern=[[-1, 32]], channel_multiplier=1)
            pool.affine_select(out=expert_sel[:, :, :, :], in_=expert_sel[:, :, :, :],
                               compare_op=ALU.not_equal, fill=1.0, base=0,
                               pattern=[[-2, TPC], [-1, 2], [0, 64]],
                               channel_multiplier=1).then_inc(consts_ready, 1)
            pool.wait_ge(bias_row_ready, 1)
            for g in range(G):
                pool.wait_ge(norm_ready, g + 1)
                pool.tensor_tensor(xres[:, g * TPC:(g + 1) * TPC, :], xres[:, g * TPC:(g + 1) * TPC, :],
                                   add0_row[:, :].unsqueeze(1).to_broadcast([P, TPC, P]),
                                   ALU.add).then_inc(res_biased, 1)
            for g in range(G):
                ln_rstd(1, g)
            for g in range(G):
                ln_rstd(2, g)
            pool.wait_ge(wvp_ready, 1)
            for g in range(G):
                pool.wait_ge(norm_ready, 2 * G + g + 1)
                pool.tensor_tensor(xres[:, g * TPC:(g + 1) * TPC, :], xres[:, g * TPC:(g + 1) * TPC, :],
                                   add1_row[:, :].unsqueeze(1).to_broadcast([P, TPC, P]),
                                   ALU.add).then_inc(res_biased, 1)

            def place_query(j, u):
                pool.tensor_copy(qbuf[:, u, :], q1T[:, bass.ds(j * P, P)]).then_inc(q1_ready, 1)

            def next_query(j, u):
                pool.wait_ge(s1_psum, (j - 1) * G)
                place_query(j, u)

            def last_rstd(g):
                s = slice(3 * T, 3 * T + TPC)
                pool.wait_ge(stats_ready, g + (3 * G + 1))
                pool.tensor_tensor(veps[:, s], mv[:, s, 1], epsilon[:, :], ALU.add).then_inc(pool_chain, 1)
                pool.wait_ge(pool_chain, g + (3 * G + 4))
                pool.tensor_tensor(rstd[:, s], veps[:, s], neghalf[:, :], ALU.pow).then_inc(rstd_ready, 1)
                pool.tensor_copy(xres[:, bass.ds(g * TPC, TPC), :], attended[:, :, :]).then_inc(res_biased, 1)

            pool.wait_ge(kv_ready, 3)
            place_query(0, 0)
            place_query(1, 1)
            next_query(2, 0)
            next_query(3, 1)
            pool.wait_ge(kv_ready, KV_JOBS + G - 1)
            next_query(4, 0)
            with pool.Fori(0, G - 2) as g:
                for t in range(TPC):
                    next_query(g * TPC + (t + 5), (t + 1) % 2)
                last_rstd(g)
            for j in range(T - 3, T):
                next_query(j, j % 2)
            last_rstd(G - 2)
            last_rstd(G - 1)

        @block.scalar
        def _(act):
            act.dma_start(c_col[:, 0:1], c0.rearrange("a p -> p a")).then_inc(ld_c, 16)
            act.dma_start(c_col[:, 1:2], c1.rearrange("a p -> p a")).then_inc(ld_c, 16)
            act.dma_start(bqk0[:, 0:1], col(bq)).then_inc(ld_bias0, 16)
            act.dma_start(bqk0[:, 1:2], col(bk)).then_inc(ld_bias0, 16)
            act.dma_start(bv_row[:, :], bv.partition_broadcast(P)).then_inc(ld_bias0, 16)

            act.wait_ge(ident_ready, 1)
            nc.scalar.activation(warm[:, :], ones[:, 0:1], ACT.Tanh)
            act.wait_ge(ld_c, 32)
            nc.scalar.activation(tanh_c[:, :], c_col[:, :], ACT.Tanh, scale=0.5).then_inc(tanh_c_ready, 1)
            act.wait_ge(w0T_psum, 1)
            nc.scalar.activation(wqkvT0[:, 0:2, :], bank[0].rearrange("p (n e) -> p n e", n=4)[:, 0:2, :],
                                 ACT.Copy).then_inc(w0T_ready, 1)

            def affine(dst, g, src, layer, shift, scale):
                return nc.scalar.activation(dst[:, g * C:(g + 1) * C], src, ACT.Identity,
                                            bias=modc[:, layer, shift:shift + 1],
                                            scale=modp[:, layer, scale:scale + 1])

            def fetch_side(j):
                act.wait_ge(side_psum, j + 1)
                g, what, src = j // 4, j % 4, side_bank(j)
                if j >= QKV_JOBS:
                    ins = affine(yT, j - QKV_JOBS, src, 0, 3, 4)
                elif what == 0:
                    ins = affine(hT, g, src, 0, 0, 1)
                elif what == 3:
                    ins = nc.scalar.activation(v[:, g * TPC:(g + 1) * TPC, :],
                                               src.rearrange("p (t e) -> p t e", t=TPC), ACT.Copy)
                elif what == 1:
                    ins = nc.scalar.activation(qT[:, g * C:(g + 1) * C], src, ACT.Identity,
                                               bias=bq0_scaled[:, :], scale=SCALE0)
                else:
                    ins = nc.scalar.activation(kT[:, g * C:(g + 1) * C], src, ACT.Identity, bias=bqk0[:, 1:2])
                ins.then_inc(side_ready, 1)

            act.wait_ge(mod_ready, 1)
            for j in range(4):
                fetch_side(j)

            def exp_tile(i):
                act.wait_ge(negmax_ready, i + 1)
                if i >= 3:
                    act.wait_ge(attn_psum, i - 2)
                for c in range(nchunks(i)):
                    w = width(i, c)
                    nc.scalar.activation(probs0[i % 3][:, c * C:c * C + w],
                                         bank[(first_chunk(i) + c) % SRING][:, 0:w], ACT.Exp,
                                         bias=negmax[:, i:i + 1],
                                         accum_out=rs[:, i, c:c + 1]).then_inc(exp_done, 1)

            exp_tile(0)
            exp_tile(1)
            fetch_side(4)
            act.wait_ge(mod_psum, 2)
            nc.scalar.activation(mod_raw[:, :, :], bank[7][:, 0:3 * P].rearrange("p (n e) -> p n e", n=3), ACT.Copy)\
              .then_inc(mod_fetched, 1)
            for i in range(T - 1):
                if i == 2:
                    act.wait_ge(mod_ready, 3)
                if i < SIDE_STEPS:
                    fetch_side(5 + i)
                for j in tiles_ahead(i):
                    exp_tile(j)
            def fetch_twisted(k):
                act.wait_ge(tw_psum, k + 1)
                nc.scalar.activation(vT[:, k * C:(k + 1) * C], bank[TWIST_BANK[k]], ACT.Copy).then_inc(tw_ready, 1)

            def gelu1(r, cyc):
                for u in range(2):
                    act.wait_ge(h1_psum[r], cyc * 2 + (u + 1))
                    nc.scalar.activation(a1[:, r, u, :], bank[2 * r + u], ACT.Gelu, bias=cb1[:, :])\
                  .then_inc(h1_ready[r], 1)

            def gelu2(r, cyc):
                act.wait_ge(h2_psum[r], cyc + 1)
                nc.scalar.activation(a2[:, r, :], bank[4 + r], ACT.Gelu, bias=cb2[:, :]).then_inc(h2_ready[r], 1)

            def gelu3(r, cyc):
                act.wait_ge(h3_psum[r], cyc + 1)
                nc.scalar.activation(a3[:, r, :], bank[4 + r][0:2 * H3, :], ACT.Gelu, bias=cb3[:, :])\
                  .then_inc(h3_ready[r], 1)

            def tanh_z(r, cyc):
                for u in range(2):
                    act.wait_ge(z_psum[r], cyc * 2 + (u + 1))
                    nc.scalar.activation(th[:, r, u, :], bank[(6, 2)[r] + u], ACT.Tanh, bias=cb4h[:, :], scale=0.5)\
                  .then_inc(th_ready[r], 1)

            for k in range(G - 1):
                fetch_twisted(k)
            gelu1(1, 0)
            fetch_side(T + 3)
            fetch_twisted(G - 1)
            act.wait_ge(gc_psum, 1)
            nc.scalar.activation(g_a1[:, :], bank[5][0:H2, 0:1], ACT.Gelu, bias=gb1s[:, :]).then_inc(gc_ready, 1)
            act.wait_ge(gc_psum, 2)
            nc.scalar.activation(g_a2[:, :], bank[5][0:H3, 0:1], ACT.Gelu, bias=gb2s[:, :]).then_inc(gc_ready, 1)
            act.wait_ge(gc_psum, 3)
            nc.scalar.activation(g_th[:, :], bank[5][:, 0:1], ACT.Tanh, bias=gb3h[:, :], scale=0.5)\
                  .then_inc(gc_ready, 1)
            gelu2(1, 0)

            def cycle_act(cyc, more):
                gelu1(0, cyc)
                gelu3(1, cyc)
                gelu2(0, cyc)
                tanh_z(1, cyc)
                gelu3(0, cyc)
                tanh_z(0, cyc)
                if more:
                    gelu1(1, cyc + 1)
                    gelu2(1, cyc + 1)

            with act.Fori(0, CYCLES - 1) as cyc:
                cycle_act(cyc, True)
            cycle_act(CYCLES - 1, False)

            nc.scalar.activation(warm[:, :], ones[:, 0:1], ACT.Exp)

            def fetch_feature_major(dst, g, src, n):
                nc.scalar.activation(dst[:, g * C:(g + 1) * C], src, ACT.Identity,
                                     bias=bqkv1[:, n:n + 1]).then_inc(kv_ready, 1)

            job = 0
            for g in range(G):
                act.wait_ge(lnT_psum, g + 1)
                affine(hT, g, bank[6 + g % 2], 1, 0, 1).then_inc(lnT_ready, 1)
                for what in range(3 if g == 0 else 2):
                    src = bank[KV_RING[job % 4]]
                    job += 1
                    act.wait_ge(kv_psum, job)
                    if what == 0:
                        fetch_feature_major(kT, g, src, 1)
                    elif what == 1:
                        nc.scalar.activation(v[:, g * TPC:(g + 1) * TPC, :],
                                             src.rearrange("p (t e) -> p t e", t=TPC), ACT.Copy).then_inc(kv_ready, 1)
                    else:
                        fetch_feature_major(q1T, g, src, 0)

            def later_queries(g):
                act.wait_ge(kv_psum, KV_JOBS + g)
                fetch_feature_major(q1T, g, bank[(4, 5, 7)[g - 1]], 0)

            def fetch_scores(j, u, c):
                act.wait_ge(s1_psum, j * G + (c + 1))
                nc.scalar.activation(scores[:, u, c * C:(c + 1) * C], bank[c], ACT.Copy).then_inc(s1_ready, 1)

            def sign_scores(j, u):
                act.wait_ge(s1_ready, j * G + G)
                nc.scalar.activation(sign[:, u, 0, :], scores[:, u, :], ACT.Sign, bias=edge_bias[:, 0:1],
                                     scale=SCALE1)
                nc.scalar.activation(sign[:, u, 1, :], scores[:, u, :], ACT.Sign, bias=edge_bias[:, 1:2],
                                     scale=SCALE1).then_inc(signs_ready, 1)

            def attend_act(j, u, scores_too):
                act.wait_ge(bands_done, j + 1)
                nc.scalar.activation(probs[:, u, :], probs[:, u, :], ACT.Exp, bias=negmax1[:, u:u + 1],
                                     scale=BAND_UNIT * SCALE1, accum_out=rsum1[:, u:u + 1]).then_inc(exp1_done, 1)
                for c in range(G):
                    if scores_too and c in (0, 2):
                        fetch_scores(j + 2, u, c // 2)
                    if scores_too and c == G - 1:
                        fetch_scores(j + 2, u, 2)
                    act.wait_ge(p1T_psum, j * G + (c + 1))
                    nc.scalar.activation(pT[:, c, :, :], bank[TURN_BANK[c]].rearrange("p (t q) -> p t q", t=TPC),
                                         ACT.Copy).then_inc(p1T_ready, 1)
                if scores_too:
                    fetch_scores(j + 2, u, G - 1)
                    sign_scores(j + 2, u)

            for j in range(2):
                for c in range(G):
                    fetch_scores(j, j, c)
                    if j == 1 and c < G - 1:
                        later_queries(c + 1)
                sign_scores(j, j)
            with act.Fori(0, T // 2 - 2) as pair:
                for u in range(2):
                    attend_act(pair * 2 + u, u, True)

            def last_affine(g):
                act.wait_ge(lnT_psum, G + g + 1)
                affine(hT, g, LAST_LN_BANK[g], 1, 3, 4).then_inc(lnT_ready, 1)

            for j in range(T - 4, T):
                attend_act(j, j % 2, j + 2 < T)
                if j > T - 4:
                    last_affine(j - (T - 3))

            def square(n):
                act.wait_ge(picked_ready, n + 1)
                if n >= 2 * TPC:
                    act.wait_ge(moe_psum, n // TPC - 1)
                nc.scalar.activation(act2[:, n // TPC % 2, n % TPC, :], picked[:, n % 2, :], ACT.Square, scale=0.5)\
                  .then_inc(act_ready, 1)

            def fetch_onehot(h):
                a, b = ONEHOT_PARTS[h]
                act.wait_ge(ohT_psum, h + 1)
                nc.scalar.activation(ohT[:, a * P:b * P], onehot_psum(h), ACT.Copy).then_inc(ohT_ready, 1)

            for n in range(G * TPC):
                act.wait_ge(fc_psum, n + 1)
                nc.scalar.activation(relu_h[:, n % 2, :], bank[FC_BANK[n % 2]], ACT.Relu).then_inc(relu_ready, 1)
                if n == 1:
                    fetch_onehot(0)
                    fetch_onehot(1)
                if n == 3:
                    last_affine(G - 1)
                if n == 9:
                    fetch_onehot(2)
                if n >= 1:
                    square(n - 1)
            square(G * TPC - 1)

        @block.vector
        def _(dve):
            links = [0]

            def link(ins):
                links[0] += 1
                ins.then_inc(dve_chain, 1)
                dve.wait_ge(dve_chain, links[0])

            def nrm_free(n):
                if n < G:
                    dve.wait_ge(side_psum, 4 * n + 1)
                elif n < 2 * G:
                    dve.wait_ge(side_psum, QKV_JOBS + n - G + 1)
                else:
                    dve.wait_ge(lnT_psum, n - 2 * G + 1)

            def ln_stats(n, g):
                for t in range(TPC):
                    last = nc.vector.bn_stats(st[:, n * TPC + t, :], xres[:, g * TPC + t, :])
                link(last)
                for t in range(TPC):
                    last = nc.vector.bn_aggr(mv[:, n * TPC + t, :], st[:, n * TPC + t, :])
                last.then_inc(stats_ready, 1)

            def ln_norm(n, g):
                dve.wait_ge(rstd_ready, n + 1)
                if n >= G:
                    nrm_free(n - G)
                for t in range(TPC):
                    k = n * TPC + t
                    last = nc.vector.tensor_scalar(nrm[:, n % G, t, :], xres[:, g * TPC + t, :],
                                                   mv[:, k, 0:1], rstd[:, k:k + 1], ALU.subtract, ALU.mult)
                last.then_inc(norm_ready, 1)

            dve.wait_ge(ld_x[0], 16)
            ln_stats(0, 0)
            ln_norm(0, 0)
            dve.wait_ge(tanh_c_ready, 1)
            dve.wait_ge(ident_ready, 1)
            link(nc.vector.scalar_tensor_tensor(out=silu_col[:, :], in0=tanh_c[:, :], scalar=1.0,
                                                in1=c_col[:, :], op0=ALU.add, op1=ALU.mult))
            for n in range(2):
                last = nc.vector.tensor_scalar(silu_b[:, n, :], ones[:, :], silu_col[:, n:n + 1], 0.5,
                                               ALU.mult, ALU.mult)
            last.then_inc(silu_ready, 1)

            def gate(out, sgn, mag, src, done=None):
                link(nc.vector.tensor_scalar(sgn, src, 0.0, 2.0, ALU.is_ge, ALU.mult))
                link(nc.vector.scalar_tensor_tensor(out=mag, in0=sgn, scalar=-1.0, in1=src,
                                                    op0=ALU.add, op1=ALU.mult))
                link(nc.vector.tensor_scalar(mag, mag, GATE_FLOOR, None, ALU.max))
                last = nc.vector.scalar_tensor_tensor(out=out, in0=sgn, scalar=-1.0, in1=mag,
                                                      op0=ALU.add, op1=ALU.mult)
                if done is None:
                    link(last)
                else:
                    last.then_inc(done, 1)

            dve.wait_ge(ld_bias0, 48)
            nc.vector.tensor_scalar(bq0_scaled[:, :], bqk0[:, 0:1], SCALE0, None, ALU.mult)
            dve.wait_ge(mod_psum, 1)
            nc.vector.tensor_copy(modc[:, 0, 0:2], bank[1][:, 0:2])
            nc.vector.tensor_scalar(modp[:, 0, 0:2], bank[1][:, 0:2], 1.0, None, ALU.add).then_inc(mod_ready, 1)
            dve.wait_ge(w0T_ready, 1)
            link(nc.vector.tensor_copy(wvT0_raw[:, :], bank[0][:, 2 * P:3 * P]))
            gate(gate_row[:, 0, :], gate_sign[:, 0, :], gate_mag[:, 0, :], bank[2][:, 0:P])
            nc.vector.tensor_tensor(wqkvT0[:, 2, :], wvT0_raw[:, :], gate_row[:, 0, :], ALU.mult)\
              .then_inc(mod_ready, 1)
            for g in range(1, G):
                dve.wait_ge(ld_x[g], 16)
                ln_stats(g, g)
            nc.vector.tensor_tensor(add0_row[:, :], bv_row[:, :], gate_row[:, 0, :], ALU.mult)\
              .then_inc(bias_row_ready, 1)
            for g in range(1, G):
                ln_norm(g, g)

            def other_modulation():
                dve.wait_ge(mod_fetched, 1)
                for dst, one in ((modc, 0.0), (modp, 1.0)):
                    nc.vector.tensor_scalar(dst[:, 0, 3:6], mod_raw[:, 0, 0:3], one, None, ALU.add)
                    nc.vector.tensor_scalar(dst[:, 1, 0:2], mod_raw[:, 0, 3:5], one, None, ALU.add)
                    nc.vector.tensor_scalar(dst[:, 1, 3:5], mod_raw[:, 0, 5:7], one, None, ALU.add)
                gate(gb0_col[:, :], gcol_sign[:, :], gcol_mag[:, :], mod_raw[:, 0, 2:3])
                nc.vector.tensor_scalar(gb0_diag[:, :], ident[:, :], gb0_col[:, :], None, ALU.mult)
                gate(gate_row[:, 1:3, :], gate_sign[:, 1:3, :], gate_mag[:, 1:3, :],
                     mod_raw[:, 1:3, :], mod_ready)

            def net_weights():
                dve.wait_ge(ld_ffn0, 16 * FFN_LOADS)
                nc.vector.tensor_scalar(w4b[:, :], ones[0:2 * H3, :], w4s[:, :], None, ALU.mult)
                nc.vector.tensor_scalar(g3b[:, :], ones[0:H3, :], g3s[:, :], None, ALU.mult)
                nc.vector.tensor_scalar(cb4h[:, :], cb4[:, :], 0.5, None, ALU.mult)
                nc.vector.tensor_scalar(gb3h[:, :], gb3s[:, :], 0.5, None, ALU.mult)
                nc.vector.tensor_scalar(cpl_b[:, :], arange[:, :], 0.3, None, ALU.mult)
                dve.wait_ge(ld_l1, 96)
                nc.vector.tensor_scalar(bv1_b[:, :], ones[:, :], bqkv1[:, 2:3], None, ALU.mult)\
                  .then_inc(ffn_w_ready, 1)

            def later_weights():
                dve.wait_ge(w1T_psum, 1)
                nc.vector.tensor_copy(wvT1[:, :], bank[2][:, 0:P]).then_inc(wv1T_ready, 1)
                nc.vector.tensor_copy(wrT[:, :], bank[2][:, P:P + EXPERTS])
                nc.vector.tensor_copy(wfcT[:, :, :], bank[0].rearrange("p (c e) -> p c e", c=TPC))
                nc.vector.tensor_tensor(wpr[:, :, :], bank[1].rearrange("p (c e) -> p c e", c=TPC),
                                        gate_row[:, 2, :].unsqueeze(1).to_broadcast([P, TPC, P]), ALU.mult)\
                  .then_inc(wmoe_ready, 1)

            def row_max(i):
                n = nchunks(i)
                for c in range(n):
                    q = first_chunk(i) + c
                    dve.wait_ge(score_psum, q + 1)
                    last = nc.vector.tensor_reduce((negmax[:, i:i + 1] if n == 1 else mx[:, i, c:c + 1]),
                                                   bank[q % SRING][:, 0:width(i, c)], AX.X, ALU.max, negate=(n == 1))
                if n > 1:
                    link(last)
                    last = nc.vector.tensor_reduce(negmax[:, i:i + 1], mx[:, i, 0:n], AX.X, ALU.max, negate=True)
                last.then_inc(negmax_ready, 1)

            def fetch_pT(i, c):
                q = first_chunk(i) + c
                n = width(i, c) // P
                dve.wait_ge(pT_psum, q + 1)
                nc.vector.tensor_copy(pT[:, q % 2, 0:n, :],
                                      bank[5 + q % 2][:, 0:n * P].rearrange("p (t q) -> p t q", t=n))\
                  .then_inc(pT_ready, 1)

            def context_part(k):
                dve.wait_ge(side_ready, QKV_JOBS + k + 1)
                nc.vector.reduce_sum(ctx_parts[:, k:k + 1], yT[:, k * C:(k + 1) * C], AX.X)\
                  .then_inc(y_ready[1 - k // 2], 1)

            row_max(0)
            row_max(1)
            for i in range(T):
                n = nchunks(i)
                for c in range(min(2, n)):
                    fetch_pT(i, c)
                for j in tiles_ahead(i):
                    row_max(j)
                for c in range(2, n):
                    fetch_pT(i, c)
                if i == 0:
                    other_modulation()
                if i == 3:
                    net_weights()
                if i == T - 1:
                    later_weights()
                    for k in range(G - 1):
                        context_part(k)
                if i >= TPC and i % TPC == 0:
                    ln_norm(G + i // TPC - 1, i // TPC - 1)
                dve.wait_ge(exp_done, first_chunk(i + 1))
                if n > 1:
                    link(nc.vector.reduce_sum(rsum[:, i:i + 1], rs[:, i, 0:n], AX.X))
                link(nc.vector.reciprocal(rinv[:, i:i + 1], rsum[:, i:i + 1] if n > 1 else rs[:, i, 0:1]))
                dve.wait_ge(attn_psum, i + 1)
                dve.wait_ge(res_biased, i // TPC + 1)
                nc.vector.scalar_tensor_tensor(out=xres[:, i, :], in0=bank[7][:, 0:P], scalar=rinv[:, i:i + 1],
                                               in1=xres[:, i, :], op0=ALU.mult, op1=ALU.add).then_inc(attn_added, 1)
                if i % TPC == TPC - 1:
                    dve.wait_ge(attn_added, i + 1)
                    ln_stats(G + i // TPC, i // TPC)

            ln_norm(2 * G - 1, G - 1)
            context_part(G - 1)
            for r in range(2):
                dve.wait_ge(y_ready[r], 2)
            link(nc.vector.reduce_sum(ctx_sum[:, :], ctx_parts[:, :], AX.X))
            nc.vector.tensor_scalar(ctx_mean[:, :], ctx_sum[:, :], 1.0 / S, None, ALU.mult).then_inc(ctx_ready, 1)
            dve.wait_ge(wvp_psum, 1)
            nc.vector.tensor_tensor(wvp1[:, :], bank[4][:, 0:P], gate_row[:, 1, :], ALU.mult)
            link(nc.vector.tensor_tensor(add1_pre[:, :], bank[4][:, P:2 * P], bproj_row[:, :], ALU.add))
            nc.vector.tensor_tensor(add1_row[:, :], add1_pre[:, :], gate_row[:, 1, :], ALU.mult)\
              .then_inc(wvp_ready, 1)
            dve.wait_ge(gc_ready, 3)
            link(nc.vector.tensor_scalar(cpl_a0[:, :], g_th[:, :], 0.7, None, ALU.mult))
            link(nc.vector.tensor_scalar(cpl_a1[:, :], cpl_a0[:, :], arange[:, :], None, ALU.mult))
            link(nc.vector.tensor_scalar(cpl_a[:, :], cpl_a1[:, :], 0.1, None, ALU.add))
            base = links[0]
            dve.wait_ge(tw_ready, G)

            def coupling(r, u, cyc):
                dve.wait_ge(th_ready[r], cyc * 2 + (u + 1))
                nc.vector.tensor_scalar(cpl[:, r, u, :], th[:, r, u, :], cpl_b[:, :], cpl_a[:, :],
                                        ALU.mult, ALU.add).then_inc(dve_chain, 1)

            def couple(r, cyc, at):
                for u in range(2):
                    k = chunk_of(r, u)
                    ys, vs = yT[:, k * C:(k + 1) * C], vT[:, k * C:(k + 1) * C]
                    coupling(r, u, cyc)
                    dve.wait_ge(dve_chain, at + (2 * u + 1))
                    nc.vector.tensor_tensor(gain[:, r, u, :], cpl[:, r, u, :], vs, ALU.mult)
                    nc.vector.tensor_tensor(loss[:, r, u, :], cpl[:, r, u, :], ys, ALU.mult).then_inc(dve_chain, 1)
                    dve.wait_ge(dve_chain, at + (2 * u + 2))
                    nc.vector.tensor_tensor(ys, ys, gain[:, r, u, :], ALU.add).then_inc(y_ready[r], 1)
                for u in range(2):
                    k = chunk_of(r, u)
                    vs = vT[:, k * C:(k + 1) * C]
                    nc.vector.tensor_tensor(vs, vs, loss[:, r, u, :], ALU.subtract).then_inc(dve_chain, 1)

            with dve.Fori(0, CYCLES - 1) as cyc:
                couple(1, cyc, cyc * 12 + base)
                couple(0, cyc, cyc * 12 + (base + 6))
            links[0] = base + 12 * (CYCLES - 1)

            def last_gain(g):
                r, u = 1 - g // 2, g % 2
                coupling(r, u, CYCLES - 1)
                links[0] += 1
                dve.wait_ge(dve_chain, links[0])
                nc.vector.tensor_tensor(gain[:, r, u, :], cpl[:, r, u, :], vT[:, g * C:(g + 1) * C], ALU.mult)\
                  .then_inc(gain_ready, 1)

            last_gain(0)
            last_gain(1)
            for g in range(G):
                dve.wait_ge(ffnT_psum, g + 1)
                xs = xres[:, g * TPC:(g + 1) * TPC, :]
                link(nc.vector.tensor_tensor(xs, xs, bank[FFN_OUT_BANK[g]].rearrange("p (t e) -> p t e", t=TPC),
                                             ALU.add))
                ln_stats(2 * G + g, g)
                if g + 2 < G:
                    last_gain(g + 2)
                ln_norm(2 * G + g, g)
            BLINKS = 5

            def bands(j, u, at, i=None, t=None):
                s = scores[:, u, :]
                dve.wait_ge(s1_ready, j * G + G)
                nc.vector.tensor_scalar(band[:, 0, :], s, BAND_EDGES[0] / SCALE1, BAND_STEPS[0], ALU.is_ge, ALU.mult)
                nc.vector.tensor_scalar(band[:, 1, :], s, BAND_EDGES[1] / SCALE1, BAND_STEPS[1], ALU.is_ge, ALU.mult)\
                  .then_inc(dve_chain, 1)
                dve.wait_ge(signs_ready, j + 1)
                nc.vector.tensor_tensor(band[:, 2, :], sign[:, u, 0, :], sign[:, u, 1, :], ALU.add)\
                  .then_inc(dve_chain, 1)
                if i is not None:
                    add_attention(i, u, t)
                    dve.wait_ge(attn1_added, i + 1)
                dve.wait_ge(dve_chain, at + 1)
                nc.vector.tensor_tensor(band_sum[:, 0, :], band[:, 0, :], band[:, 1, :], ALU.add)
                if i is not None:
                    nc.vector.bn_stats(st[:, 3 * T + t, :], attended[:, t, :]).then_inc(bn_done, 1)
                dve.wait_ge(dve_chain, at + 2)
                nc.vector.tensor_scalar(band_sum[:, 1, :], band[:, 2, :], BAND_STEPS[2], BAND_BASE,
                                        ALU.mult, ALU.add).then_inc(dve_chain, 1)
                if i is not None:
                    dve.wait_ge(bn_done, i + 1)
                dve.wait_ge(dve_chain, at + 3)
                nc.vector.tensor_tensor(mult[:, :], band_sum[:, 0, :], band_sum[:, 1, :], ALU.add)\
                  .then_inc(dve_chain, 1)
                if i is not None:
                    last = nc.vector.bn_aggr(mv[:, 3 * T + t, :], st[:, 3 * T + t, :])
                    if t == TPC - 1:
                        last.then_inc(stats_ready, 1)
                dve.wait_ge(dve_chain, at + 4)
                if type(j) is not int or j > 0:
                    dve.wait_ge(exp1_done, j)
                    nc.vector.reciprocal(rinv1[:, 1 - u:2 - u], rsum1[:, 1 - u:2 - u])
                nc.vector.tensor_tensor_reduce(out=probs[:, u, :], in0=mult[:, :], in1=s, scale=1.0,
                                               scalar=-3.0e38, op0=ALU.mult, op1=ALU.max,
                                               accum_out=max1[:, u:u + 1]).then_inc(dve_chain, 1)
                dve.wait_ge(dve_chain, at + 5)
                nc.vector.tensor_scalar(negmax1[:, u:u + 1], max1[:, u:u + 1], -BAND_UNIT * SCALE1, None, ALU.mult)\
                  .then_inc(bands_done, 1)

            def add_attention(i, u, t):
                dve.wait_ge(attn1_psum, i + 1)
                nc.vector.scalar_tensor_tensor(out=attended[:, t, :], in0=bank[6][:, 0:P], scalar=rinv1[:, u:u + 1],
                                               in1=xres[:, bass.ds(i, 1), :].rearrange("p a d -> p (a d)"),
                                               op0=ALU.mult, op1=ALU.add).then_inc(attn1_added, 1)

            def last_norm(g):
                dve.wait_ge(rstd_ready, g + (3 * G + 1))
                for t in range(TPC):
                    k = 3 * T + t
                    last = nc.vector.tensor_scalar(nrm[:, bass.ds(g, 1), t, :].rearrange("p a d -> p (a d)"),
                                                   attended[:, t, :],
                                                   mv[:, k, 0:1], rstd[:, k:k + 1], ALU.subtract, ALU.mult)
                last.then_inc(norm_ready, 1)

            dve.wait_ge(res_biased, 2 * G)
            dve.wait_ge(lnT_psum, G)
            base = links[0]
            bands(0, 0, base)
            bands(1, 1, base + BLINKS)
            with dve.Fori(0, G - 1) as g:
                for t in range(TPC):
                    if t == 0:
                        dve.wait_ge(res_biased, g + 2 * G)
                        dve.wait_ge(norm_ready, g + 3 * G)
                    bands(g * TPC + (t + 2), t % 2, g * (TPC * BLINKS) + (base + BLINKS * (t + 2)),
                          g * TPC + t, t)
                last_norm(g)
            dve.wait_ge(res_biased, 3 * G - 1)
            dve.wait_ge(norm_ready, 4 * G - 1)
            for t in range(2):
                i = T - TPC + t
                bands(i + 2, t, base + BLINKS * (i + 2), i, t)
            links[0] = base + BLINKS * T
            add_attention(T - 2, 0, TPC - 2)
            dve.wait_ge(exp1_done, T)
            link(nc.vector.reciprocal(rinv1[:, 1:2], rsum1[:, 1:2]))
            add_attention(T - 1, 1, TPC - 1)
            dve.wait_ge(attn1_added, T)
            for t in range(TPC - 2, TPC):
                last = nc.vector.bn_stats(st[:, 3 * T + t, :], attended[:, t, :])
            last.then_inc(bn_done, 1)
            dve.wait_ge(bn_done, T - 1)
            for t in range(TPC - 2, TPC):
                last = nc.vector.bn_aggr(mv[:, 3 * T + t, :], st[:, 3 * T + t, :])
            last.then_inc(stats_ready, 1)

            def add_experts(g):
                dve.wait_ge(moe_psum, g + 1)
                dve.wait_ge(res_biased, 3 * G)
                xs = xres[:, g * TPC:(g + 1) * TPC, :]
                nc.vector.tensor_tensor(xs, xs, bank[4].rearrange("p (t e) -> p t e", t=TPC), ALU.add)\
                  .then_inc(out_ready, 1)

            def lrelu_double(n):
                dve.wait_ge(relu_ready, n + 1)
                link(nc.vector.tensor_tensor(lrelu2[:, n % 2, :], bank[FC_BANK[n % 2]], relu_h[:, n % 2, :], ALU.add))

            def choose(part, a, b):
                n = b - a
                dve.wait_ge(lg_psum, part + 1)
                link(nc.vector.tensor_copy(lg[:, a:b, :], bank[LOGIT_BANK][:, a * EXPERTS:b * EXPERTS]
                                           .rearrange("p (t e) -> p t e", t=n)))
                link(nc.vector.reduce_max(lgmax[:, a:b], lg[:, a:b, :], AX.X))
                link(nc.vector.tensor_tensor(ranked[:, a:b, :], lg[:, a:b, :],
                                             lgmax[:, a:b].unsqueeze(2).to_broadcast([P, n, EXPERTS]), ALU.is_ge))
                link(nc.vector.tensor_tensor(ranked[:, a:b, :], ranked[:, a:b, :], tie_rank[:, a:b, :], ALU.mult))
                link(nc.vector.reduce_max(best[:, a:b], ranked[:, a:b, :], AX.X))
                nc.vector.tensor_tensor(onehot[:, a:b, :], ranked[:, a:b, :],
                                        best[:, a:b].unsqueeze(2).to_broadcast([P, n, EXPERTS]), ALU.is_equal)\
                  .then_inc(onehot_ready, 1)

            choose(0, 0, T - TPC)
            last_norm(G - 1)
            for g in range(G):
                for c in range(TPC):
                    n = g * TPC + c
                    lrelu_double(n)
                    dve.wait_ge(mask_psum, n + 1)
                    if n >= 2:
                        dve.wait_ge(act_ready, n - 1)
                    nc.vector.tensor_tensor(picked[:, n % 2, :], lrelu2[:, n % 2, :], bank[PICK_BANK[n % 2]], ALU.mult)\
                      .then_inc(picked_ready, 1)
                    if n == 6:
                        choose(1, T - TPC, T)
                    if c == 3 and g >= 1:
                        add_experts(g - 1)
            add_experts(G - 1)

        @block.tensor
        def _(pe):
            mm = nc.tensor.matmul
            tr = nc.tensor.transpose

            def mod_column(dst, n, j):
                return mm(dst, wmod[:, n, j * P:(j + 1) * P], silu_b[:, n, 0:1], start=True, stop=True)

            def mod_row(dst, n, j):
                return mm(dst, silu_b[:, n, :], wmod[:, n, j * P:(j + 1) * P], start=True, stop=True)

            pe.wait_ge(silu_ready, 1)
            pe.wait_ge(ld_wmod[0], 16)
            mod_column(bank[1][:, 0:1], 0, 0)
            mod_column(bank[1][:, 1:2], 0, 1)
            mod_row(bank[2][:, 0:P], 0, 2).then_inc(mod_psum, 1)
            pe.wait_ge(ident_ready, 1)
            pe.wait_ge(ld_attn0, 48)
            for n in range(3):
                last = tr(bank[0][:, n * P:(n + 1) * P], wqkv0_raw[:, n, :], ident[:, :])
            last.then_inc(w0T_psum, 1)

            def ln_transpose(n, dst):
                pe.wait_ge(norm_ready, n + 1)
                for t in range(TPC):
                    last = tr(dst[:, t * P:(t + 1) * P], nrm[:, n % G, t, :], ident[:, :])
                return last

            def side_job(j):
                if j > 4:
                    pe.wait_ge(side_ready, j)
                g, what, dst = j // 4, j % 4, side_bank(j)
                if j >= QKV_JOBS:
                    last = ln_transpose(G + j - QKV_JOBS, dst)
                elif what == 0:
                    last = ln_transpose(g, dst)
                elif what == 3:
                    for t in range(TPC):
                        last = mm(dst[:, t * P:(t + 1) * P], hT[:, g * C + t * P:g * C + (t + 1) * P],
                                  wqkvT0[:, 2, :], start=True, stop=True)
                else:
                    last = mm(dst, wqkvT0[:, what - 1, :], hT[:, g * C:(g + 1) * C], start=True, stop=True)
                last.then_inc(side_psum, 1)

            side_job(0)
            pe.wait_ge(w0T_ready, 1)
            pe.wait_ge(side_ready, 1)
            side_job(1)
            side_job(2)
            pe.wait_ge(mod_ready, 2)
            side_job(3)

            def mod_rest():
                pe.wait_ge(ld_wmod[1], 16)
                pe.wait_ge(ld_wmod[2], 16)
                for k, (n, j) in enumerate(REST):
                    mod_column(bank[7][:, k:k + 1], n, j)
                mod_row(bank[7][:, P:2 * P], 1, 2)
                mod_row(bank[7][:, 2 * P:3 * P], 1, 5).then_inc(mod_psum, 1)

            def score_chunks(i):
                for c in range(nchunks(i)):
                    q = first_chunk(i) + c
                    w = width(i, c)
                    if q >= SRING:
                        pe.wait_ge(exp_done, q - SRING + 1)
                    diagonal = c == nchunks(i) - 1
                    last = mm(bank[q % SRING][:, 0:w], qT[:, i * P:(i + 1) * P], kT[:, c * C:c * C + w],
                              start=True, stop=not diagonal)
                    if diagonal:
                        last = mm(bank[q % SRING][:, w - P:w], identb[:, :], causal[:, :], start=False, stop=True)
                    last.then_inc(score_psum, 1)

            def transpose_probs(i, c):
                q = first_chunk(i) + c
                pe.wait_ge(exp_done, q + 1)
                if q >= 2:
                    pe.wait_ge(pT_ready, q - 1)
                for b in range(width(i, c) // P):
                    last = tr(bank[5 + q % 2][:, b * P:(b + 1) * P],
                              probs0[i % 3][:, c * C + b * P:c * C + (b + 1) * P], ident[:, :])
                last.then_inc(pT_psum, 1)

            def weigh_values(i, c):
                q = first_chunk(i) + c
                pe.wait_ge(pT_ready, q + 1)
                if c == 0 and i == 0:
                    pe.wait_ge(mod_fetched, 1)
                if c == 0 and i >= 1:
                    pe.wait_ge(attn_added, i)
                for b in range(width(i, c) // P):
                    k = c * TPC + b
                    last = mm(bank[7][:, 0:P], pT[:, q % 2, b, :], v[:, k, :], start=(k == 0), stop=(k == i))
                if c == nchunks(i) - 1:
                    last.then_inc(attn_psum, 1)

            def later_weights():
                pe.wait_ge(ld_l1, 96)
                pe.wait_ge(ld_moe, 96)
                for c in range(TPC):
                    tr(bank[0][:, c * P:(c + 1) * P], wfc_raw[:, c, :], ident[:, :])
                    tr(bank[1][:, c * P:(c + 1) * P],
                       wpr_raw[:, 2 * c:2 * c + 2, :].rearrange("p u h -> p (u h)"), ident[:, :])
                tr(bank[2][:, 0:P], wqkv1[:, 2, :], ident[:, :])
                tr(bank[2][:, P:P + EXPERTS], wr_raw[:, :], ident[0:EXPERTS, 0:EXPERTS]).then_inc(w1T_psum, 1)

            pe.wait_ge(side_ready, 4)
            pe.wait_ge(causal_ready, 1)
            score_chunks(0)
            score_chunks(1)
            side_job(4)
            mod_rest()
            for i in range(T):
                n = nchunks(i)
                for c in range(min(2, n)):
                    transpose_probs(i, c)
                if i < SIDE_STEPS:
                    side_job(5 + i)
                for j in tiles_ahead(i):
                    score_chunks(j)
                for c in range(n):
                    if i == T - 1 and c == n - 1:
                        later_weights()
                    weigh_values(i, c)
                    if c + 2 < n:
                        transpose_probs(i, c + 2)

            pe.wait_ge(consts_ready, 1)
            pe.wait_ge(ffn_w_ready, 1)
            def layer1(r, cyc):
                for u in range(2):
                    k = chunk_of(r, u)
                    pe.wait_ge(y_ready[r], cyc * 2 + (u + 1))
                    mm(bank[2 * r + u], w1s[:, :], yT[:, k * C:(k + 1) * C], start=True, stop=True).then_inc(h1_psum[r], 1)

            def twisted(k):
                mm(bank[TWIST_BANK[k]], twist[:, :], yT[:, k * C:(k + 1) * C], start=True, stop=True)\
                  .then_inc(tw_psum, 1)

            twisted(0)
            pe.wait_ge(wmoe_ready, 1)
            twisted(1)
            twisted(2)
            layer1(1, 0)
            side_job(T + 3)
            pe.wait_ge(side_ready, QKV_JOBS + G)
            pe.wait_ge(attn_added, T)
            twisted(3)
            mm(bank[4][:, 0:P], wvT1[:, :], wproj1[:, :], start=True, stop=True)
            mm(bank[4][:, P:2 * P], bv1_b[:, :], wproj1[:, :], start=True, stop=True).then_inc(wvp_psum, 1)
            pe.wait_ge(ctx_ready, 1)
            mm(bank[5][0:H2, 0:1], g1s[:, :], ctx_mean[:, :], start=True, stop=True).then_inc(gc_psum, 1)

            def layer2(r, cyc):
                for u in range(2):
                    pe.wait_ge(h1_ready[r], cyc * 2 + (u + 1))
                    last = mm(bank[4 + r][u * H2:(u + 1) * H2, :], w2s[:, :], a1[:, r, u, :], start=True, stop=True)
                last.then_inc(h2_psum[r], 1)

            def layer3(r, cyc):
                pe.wait_ge(h2_ready[r], cyc + 1)
                mm(bank[4 + r][0:2 * H3, :], w3s[:, :], a2[:, r, :], start=True, stop=True).then_inc(h3_psum[r], 1)

            def layer4(r, cyc):
                pe.wait_ge(h3_ready[r], cyc + 1)
                for u in range(2):
                    mm(bank[(6, 2)[r] + u], w4b[u * H3:(u + 1) * H3, :], a3[u * H3:(u + 1) * H3, r, :],
                       start=True, stop=True).then_inc(z_psum[r], 1)

            pe.wait_ge(gc_ready, 1)
            mm(bank[5][0:H3, 0:1], g2s[:, :], g_a1[:, :], start=True, stop=True).then_inc(gc_psum, 1)
            pe.wait_ge(gc_ready, 2)
            mm(bank[5][:, 0:1], g3b[:, :], g_a2[:, :], start=True, stop=True).then_inc(gc_psum, 1)
            pe.wait_ge(gc_ready, 3)
            layer2(1, 0)
            pe.wait_ge(wvp_ready, 1)
            pe.wait_ge(tw_ready, G)

            with pe.Fori(0, CYCLES - 1) as cyc:
                layer1(0, cyc)
                layer3(1, cyc)
                layer2(0, cyc)
                layer4(1, cyc)
                layer3(0, cyc)
                layer4(0, cyc)
                layer1(1, cyc + 1)
                layer2(1, cyc + 1)

            def output(g):
                r, u = 1 - g // 2, g % 2
                pe.wait_ge(gain_ready, g + 1)
                for t in range(TPC):
                    dst = bank[FFN_OUT_BANK[g]][:, t * P:(t + 1) * P]
                    mm(dst, yT[:, g * C + t * P:g * C + (t + 1) * P], gb0_diag[:, :], start=True, stop=False)
                    last = mm(dst, gain[:, r, u, t * P:(t + 1) * P], gb0_diag[:, :], start=False, stop=True)
                last.then_inc(ffnT_psum, 1)

            layer1(0, CYCLES - 1)
            layer3(1, CYCLES - 1)
            layer2(0, CYCLES - 1)
            layer4(1, CYCLES - 1)
            layer3(0, CYCLES - 1)
            layer4(0, CYCLES - 1)
            output(0)
            output(1)

            def features(dst, g, n):
                return mm(dst, wqkv1[:, n, :], hT[:, g * C:(g + 1) * C], start=True, stop=True)

            job = 0
            for g in range(G):
                if g == 0:
                    pe.wait_ge(th_ready[0], 2 * CYCLES)
                    pe.wait_ge(th_ready[1], 2 * CYCLES)
                if g >= 2:
                    pe.wait_ge(lnT_ready, g - 1)
                ln_transpose(2 * G + g, bank[6 + g % 2]).then_inc(lnT_psum, 1)
                if g < 2:
                    output(g + 2)
                pe.wait_ge(lnT_ready, g + 1)
                for what in range(3 if g == 0 else 2):
                    dst = bank[KV_RING[job % 4]]
                    if job >= 4:
                        pe.wait_ge(kv_ready, job - 3)
                    job += 1
                    if what == 1:
                        for t in range(TPC):
                            last = mm(dst[:, t * P:(t + 1) * P], hT[:, g * C + t * P:g * C + (t + 1) * P],
                                      wvp1[:, :], start=True, stop=True)
                    else:
                        last = features(dst, g, 1 if what == 0 else 0)
                    last.then_inc(kv_psum, 1)

            def score_tile(j, u, first=False):
                pe.wait_ge(q1_ready, j + 1)
                for c in range(G):
                    if not first:
                        pe.wait_ge(s1_ready, (j - 1) * G + (c + 1))
                    mm(bank[c], qbuf[:, u, :], kT[:, c * C:(c + 1) * C], start=True, stop=True).then_inc(s1_psum, 1)

            def attend(j, u, first=False):
                pe.wait_ge(exp1_done, j + 1)

                def turn(c):
                    if c == 0 and not first:
                        pe.wait_ge(p1T_ready, j * G)
                    if c == G - 1:
                        pe.wait_ge(p1T_ready, j * G + 1)
                    for b in range(TPC):
                        last = tr(bank[TURN_BANK[c]][:, b * P:(b + 1) * P],
                                  probs[:, u, c * C + b * P:c * C + (b + 1) * P], ident[:, :])
                    last.then_inc(p1T_psum, 1)

                for c in range(G - 1):
                    turn(c)
                for c in range(G):
                    pe.wait_ge(p1T_ready, j * G + (c + 1))
                    if c == 0 and not first:
                        pe.wait_ge(attn1_added, j)
                    for b in range(TPC):
                        k = c * TPC + b
                        last = mm(bank[6][:, 0:P], pT[:, c, b, :], v[:, k, :], start=(k == 0), stop=(k == T - 1))
                    if c == 0:
                        turn(G - 1)
                last.then_inc(attn1_psum, 1)

            pe.wait_ge(kv_ready, KV_JOBS)
            score_tile(0, 0, first=True)
            for g in range(1, G):
                features(bank[(4, 5, 7)[g - 1]], g, 0).then_inc(kv_psum, 1)
            score_tile(1, 1)
            for u in range(2):
                score_tile(2 + u, u)
                attend(u, u, first=(u == 0))
            with pe.Fori(1, T // 2 - 2) as pair:
                for u in range(2):
                    score_tile(pair * 2 + (2 + u), u)
                    attend(pair * 2 + u, u)
            for j in range(T - 4, T - 1):
                if j + 2 < T:
                    score_tile(j + 2, j % 2)
                attend(j, j % 2)
                if j > T - 4:
                    ln_transpose(3 * G + j - (T - 3), LAST_LN_BANK[j - (T - 3)]).then_inc(lnT_psum, 1)

            def logits(g):
                pe.wait_ge(lnT_ready, G + g + 1)
                for t in range(TPC):
                    k = g * TPC + t
                    last = mm(bank[LOGIT_BANK][:, k * EXPERTS:(k + 1) * EXPERTS], hT[:, k * P:(k + 1) * P], wrT[:, :],
                              start=True, stop=True)
                return last

            def expand(n):
                g, c = n // TPC, n % TPC
                mm(bank[FC_BANK[n % 2]], wfcT[:, c, :], hT[:, g * C:(g + 1) * C], start=True, stop=True).then_inc(fc_psum, 1)

            def pick(n):
                g, c = n // TPC, n % TPC
                mm(bank[PICK_BANK[n % 2]], expert_sel[:, c, :, :].rearrange("p u h -> p (u h)"),
                   ohT[:, g * C:(g + 1) * C], start=True, stop=True).then_inc(mask_psum, 1)

            def contract(g):
                pe.wait_ge(act_ready, (g + 1) * TPC)
                if g >= 1:
                    pe.wait_ge(out_ready, g)
                for t in range(TPC):
                    for c in range(TPC):
                        last = mm(bank[4][:, t * P:(t + 1) * P], act2[:, g % 2, c, t * P:(t + 1) * P], wpr[:, c, :],
                                  start=(c == 0), stop=(c == TPC - 1))
                last.then_inc(moe_psum, 1)

            def turn_onehot(h):
                a, b = ONEHOT_PARTS[h]
                pe.wait_ge(onehot_ready, 1 if h < 2 else 2)
                for t in range(a, b):
                    last = tr(onehot_psum(h)[:, (t - a) * P:(t - a + 1) * P], onehot[:, t, :], identb[:, :])
                last.then_inc(ohT_psum, 1)

            pe.wait_ge(s1_ready, G * T)
            ln_transpose(4 * G - 2, LAST_LN_BANK[2]).then_inc(lnT_psum, 1)
            logits(0)
            logits(1)
            attend(T - 1, 1)
            logits(2).then_inc(lg_psum, 1)
            expand(0)
            expand(1)
            pe.wait_ge(attn1_added, T)
            turn_onehot(0)
            turn_onehot(1)
            pe.wait_ge(ohT_ready, 2)
            pe.wait_ge(p1T_ready, G * T)
            for n in range(G * TPC):
                if n == 9:
                    turn_onehot(2)
                if n == 12:
                    pe.wait_ge(ohT_ready, 3)
                if n >= 2:
                    pe.wait_ge(picked_ready, n - 1)
                    expand(n)
                pick(n)
                if n == 2:
                    ln_transpose(4 * G - 1, LAST_LN_BANK[3]).then_inc(lnT_psum, 1)
                if n == 5:
                    logits(3).then_inc(lg_psum, 1)
                if n % TPC == 2 and n > TPC:
                    contract(n // TPC - 1)
            contract(G - 1)


_INS = ['L0_attn_x', 'L0_attn_Wq', 'L0_attn_bq', 'L0_attn_Wk', 'L0_attn_bk', 'L0_attn_Wv', 'L0_attn_bv',
        'L0_ffn_cn_w1', 'L0_ffn_cn_b1', 'L0_ffn_cn_w2', 'L0_ffn_cn_b2', 'L0_ffn_cn_w3', 'L0_ffn_cn_b3',
        'L0_ffn_cn_w4', 'L0_ffn_cn_b4', 'L0_ffn_gc_w1', 'L0_ffn_gc_b1', 'L0_ffn_gc_w2', 'L0_ffn_gc_b2',
        'L0_ffn_gc_w3', 'L0_ffn_gc_b3', 'L0_ffn_adaptive_range', 'L0_c', 'L0_wmod', 'L1_attn_W_qkv',
        'L1_attn_b_qkv', 'L1_attn_W_proj', 'L1_attn_b_proj', 'L1_ffn_w_router', 'L1_ffn_w_fc', 'L1_ffn_w_proj',
        'L1_c', 'L1_wmod']


def kernel(**inputs):
    import numpy as np
    import concourse.bacc as bacc
    from concourse.bass_utils import run_bass_kernel_spmd

    nc = bacc.Bacc("TRN2", target_bir_lowering=False, num_devices=1)
    arrays, args = {}, []
    for name in _INS:
        a = np.ascontiguousarray(inputs[name])
        arrays[f"in_{name}"] = a
        args.append(nc.dram_tensor(f"in_{name}", a.shape, mybir.dt.from_np(a.dtype), kind="ExternalInput").ap())
    shape = inputs['L0_attn_x'].shape
    args.append(nc.dram_tensor("out", shape, F32, kind="ExternalOutput").ap())
    build(nc, *args)
    r = run_bass_kernel_spmd(nc, [arrays], core_ids=[0])
    return r.results[0]["out"]
```

```python
from contextlib import ExitStack

import concourse.bass as bass
from concourse import mybir

P = 128
C = 512
TPC = C // P

ALU = mybir.AluOpType
ACT = mybir.ActivationFunctionType
AX = mybir.AxisListType
F32 = mybir.dt.float32
BF16 = mybir.dt.bfloat16

LN_EPS = 1e-5
GATE_FLOOR = 0.25
MASKED = -1e30
CYCLES = 3
HEAD_DIM_L1 = 8
EXPERTS = 8

BAND_EDGES = (-2.1972245773362196, -1.0986122886681098, 1.7346010553881064, 2.9444389791664403)
BAND_STEPS = (2.0, 7.0, 2.5)
BAND_BASE = 6.0
BAND_UNIT = 0.1


def build(nc, x, Wq, bq, Wk, bk, Wv, bv, cn_w1, cn_b1, cn_w2, cn_b2, cn_w3, cn_b3, cn_w4, cn_b4,
          gc_w1, gc_b1, gc_w2, gc_b2, gc_w3, gc_b3, adaptive_range, c0, wmod0,
          W_qkv, b_qkv, W_proj, b_proj, w_router, w_fc, w_proj, c1, wmod1, out):
    _, S, D = x.shape
    T = S // P
    G = S // C
    H2, H3 = cn_w2.shape[1], cn_w3.shape[1]
    assert D == P and H2 == 64 and H3 == 32 and T == 16
    SCALE0 = float(D) ** -0.5
    SCALE1 = float(HEAD_DIM_L1) ** -0.5

    with ExitStack() as ctx:
        def sb(name, shape, dt=F32):
            return ctx.enter_context(nc.sbuf_tensor(name, shape, dt))

        def sem(name):
            return ctx.enter_context(nc.semaphore(name))

        xres = sb("xres", [P, T, D])
        ybuf = sb("ybuf", [P, 3, S])
        yT = ybuf[:, 0, :]
        yT_last = ybuf[:, 2, :]
        hT = ybuf[:, 1, :]
        kT = ybuf[:, 2, :]
        qT = sb("qT", [P, S])
        v = sb("v", [P, T, D])
        ident = sb("ident", [P, P])
        identb = sb("identb", [P, P], BF16)
        causal = sb("causal", [P, P], BF16)
        twist = sb("twist", [P, P])
        ones = sb("ones", [P, P])
        neghalf = sb("neghalf", [P, TPC])
        epsilon = sb("epsilon", [P, TPC])
        expert_sel = sb("expert_sel", [EXPERTS, TPC, 2, 64], BF16)
        tie_rank = sb("tie_rank", [P, T, EXPERTS])
        wqkv0_raw = sb("wqkv0_raw", [P, 3, P])
        wqkvT0 = sb("wqkvT0", [P, 3, P])
        bqk0 = sb("bqk0", [P, 2])
        bq0_scaled = sb("bq0_scaled", [P, 1])
        wvT0_raw = sb("wvT0_raw", [P, P])
        bv_row = sb("bv_row", [P, P])
        c_col = sb("c_col", [P, 2])
        tanh_c = sb("tanh_c", [P, 2])
        silu_col = sb("silu_col", [P, 2])
        silu_b = sb("silu_b", [P, 2, P])
        wmod = sb("wmod", [P, 2, 6 * P])
        mod_raw = sb("mod_raw", [P, 3, P])
        modc = sb("modc", [P, 2, 6])
        modp = sb("modp", [P, 2, 6])
        gate_sign = sb("gate_sign", [P, 3, P])
        gate_mag = sb("gate_mag", [P, 3, P])
        gate_row = sb("gate_row", [P, 3, P])
        gcol_sign = sb("gcol_sign", [P, 1])
        gcol_mag = sb("gcol_mag", [P, 1])
        gb0_col = sb("gb0_col", [P, 1])
        gb0_diag = sb("gb0_diag", [P, P])
        w1s = sb("w1s", [P, P])
        w2s = sb("w2s", [P, H2])
        w3s = sb("w3s", [P, 2 * H3])
        w4s = sb("w4s", [2 * H3, 1])
        w4b = sb("w4b", [2 * H3, P])
        g1s = sb("g1s", [P, H2])
        g2s = sb("g2s", [H2, H3])
        g3s = sb("g3s", [H3, 1])
        g3b = sb("g3b", [H3, P])
        cb1 = sb("cb1", [P, 1])
        cb2 = sb("cb2", [P, 1])
        cb3 = sb("cb3", [2 * H3, 1])
        cb4 = sb("cb4", [P, 1])
        cb4h = sb("cb4h", [P, 1])
        gb1s = sb("gb1s", [H2, 1])
        gb2s = sb("gb2s", [H3, 1])
        gb3s = sb("gb3s", [P, 1])
        gb3h = sb("gb3h", [P, 1])
        arange = sb("arange", [P, 1])
        ctx_parts = sb("ctx_parts", [P, G])
        ctx_sum = sb("ctx_sum", [P, 1])
        ctx_mean = sb("ctx_mean", [P, 1])
        g_a1 = sb("g_a1", [H2, 1])
        g_a2 = sb("g_a2", [H3, 1])
        g_th = sb("g_th", [P, 1])
        cpl_a0 = sb("cpl_a0", [P, 1])
        cpl_a1 = sb("cpl_a1", [P, 1])
        cpl_a = sb("cpl_a", [P, 1])
        cpl_b = sb("cpl_b", [P, 1])
        wqkv1 = sb("wqkv1", [P, 3, P])
        bqkv1 = sb("bqkv1", [P, 3])
        bv1_b = sb("bv1_b", [P, P])
        wproj1 = sb("wproj1", [P, P])
        bproj_row = sb("bproj_row", [P, P])
        wvT1 = sb("wvT1", [P, P])
        wvp1 = sb("wvp1", [P, P])
        add0_row = sb("add0_row", [P, P])
        add1_pre = sb("add1_pre", [P, P])
        add1_row = sb("add1_row", [P, P])
        wr_raw = sb("wr_raw", [EXPERTS, P])
        wrT = sb("wrT", [P, EXPERTS])
        wfc_raw = sb("wfc_raw", [P, TPC, P])
        wfcT = sb("wfcT", [P, TPC, P])
        wpr_raw = sb("wpr_raw", [P, EXPERTS, 64])
        wpr = sb("wpr", [P, TPC, P])
        st = sb("st", [P, 4 * T, 6])
        mv = sb("mv", [P, 4 * T, 2])
        veps = sb("veps", [P, 4 * T])
        rstd = sb("rstd", [P, 4 * T])
        nrm = sb("nrm", [P, G, TPC, P])
        probs = sb("probs", [P, 2, S])
        pT = sb("pT", [P, 4, TPC, P])
        mx = sb("mx", [P, T, G])
        negmax = sb("negmax", [P, T])
        rs = sb("rs", [P, T, G])
        rsum = sb("rsum", [P, T])
        rinv = sb("rinv", [P, T])
        scores = sb("scores", [P, 2, S])
        band = sb("band", [P, 4, S], BF16)
        band_sum = sb("band_sum", [P, 2, S], BF16)
        sign = sb("sign", [P, 2, 2, S], BF16)
        mult = sb("mult", [P, S], BF16)
        edge_bias = sb("edge_bias", [P, 2])
        qbuf = sb("qbuf", [P, 2, P])
        max1 = sb("max1", [P, 2])
        minus_unit = sb("minus_unit", [P, 1])
        negmax1 = sb("negmax1", [P, 2])
        rsum1 = sb("rsum1", [P, 2])
        rinv1 = sb("rinv1", [P, TPC])
        attended = sb("attended", [P, TPC, D])
        vT = qT
        q1T = qT
        a1 = scores[:, 0, :].rearrange("p (r u t) -> p r u t", r=2, u=2)
        th = scores[:, 1, :].rearrange("p (r u t) -> p r u t", r=2, u=2)
        cpl = band[:, 0:2, :].rearrange("p b t -> p (b t)").bitcast(F32).rearrange("p (r u t) -> p r u t", r=2, u=2)
        gain = band[:, 2:4, :].rearrange("p b t -> p (b t)").bitcast(F32).rearrange("p (r u t) -> p r u t", r=2, u=2)
        loss = sign[:, 0, :, :].rearrange("p b t -> p (b t)").bitcast(F32).rearrange("p (r u t) -> p r u t", r=2, u=2)
        a2 = sb("a2", [P, 2, C])
        a3 = sb("a3", [2 * H3, 2, C])
        warm = sb("warm", [P, 1])
        lg = sb("lg", [P, T, EXPERTS])
        lgmax = sb("lgmax", [P, T])
        ranked = sb("ranked", [P, T, EXPERTS])
        best = sb("best", [P, T])
        onehot = sb("onehot", [P, T, EXPERTS], BF16)
        ohT = sb("ohT", [EXPERTS, S], BF16)
        relu_h = [scores[:, 0, i * C:(i + 1) * C] for i in range(3)]
        lrelu2 = [scores[:, 0, 3 * C:4 * C], scores[:, 1, 0:C]]
        picked = [scores[:, 1, i * C:(i + 1) * C] for i in range(1, 4)]
        probs0 = [probs[:, 0, :], probs[:, 1, :], scores[:, 0, :]]
        act2 = probs[:, :, :].rearrange("p b (c t) -> p b c t", c=TPC)

        sc4 = ctx.enter_context(nc.psum_tensor("sc4", [P, 4, C], F32))
        turn2 = ctx.enter_context(nc.psum_tensor("turn2", [P, 2, C], F32))
        b6 = ctx.enter_context(nc.psum_tensor("b6", [P, C], F32))
        b7 = ctx.enter_context(nc.psum_tensor("b7", [P, C], F32))
        bank = [sc4[:, i, :] for i in range(4)] + [turn2[:, i, :] for i in range(2)] + [b6[:, :], b7[:, :]]
        oh_ps = [bank[0].bitcast(BF16), bank[1].bitcast(BF16)]

        ld_x = [sem(f"ld_x{g}") for g in range(G)]
        ld_attn0 = sem("ld_attn0")
        ld_bias0 = sem("ld_bias0")
        ld_c = sem("ld_c")
        ld_wmod = [sem(f"ld_wmod{n}") for n in range(3)]
        ld_ffn0 = sem("ld_ffn0")
        ld_l1 = sem("ld_l1")
        ld_moe = sem("ld_moe")
        pool_chain = sem("pool_chain")
        ident_ready = sem("ident_ready")
        causal_ready = sem("causal_ready")
        consts_ready = sem("consts_ready")
        tanh_c_ready = sem("tanh_c_ready")
        silu_ready = sem("silu_ready")
        w0T_psum = sem("w0T_psum")
        w0T_ready = sem("w0T_ready")
        mod_psum = sem("mod_psum")
        mod_fetched = sem("mod_fetched")
        mod_ready = sem("mod_ready")
        w1T_psum = sem("w1T_psum")
        wv1T_ready = sem("wv1T_ready")
        wmoe_ready = sem("wmoe_ready")
        wvp_psum = sem("wvp_psum")
        wvp_ready = sem("wvp_ready")
        dve_chain = sem("dve_chain")
        act_chain = sem("act_chain")
        ffn_w_ready = sem("ffn_w_ready")
        bias_row_ready = sem("bias_row_ready")
        stats_ready = sem("stats_ready")
        rstd_ready = sem("rstd_ready")
        norm_ready = sem("norm_ready")
        side_psum = sem("side_psum")
        side_ready = sem("side_ready")
        lnT_psum = sem("lnT_psum")
        lnT_ready = sem("lnT_ready")
        kv_psum = sem("kv_psum")
        kv_ready = sem("kv_ready")
        res_biased = sem("res_biased")
        score_psum = sem("score_psum")
        negmax_ready = sem("negmax_ready")
        exp_done = sem("exp_done")
        pT_psum = sem("pT_psum")
        pT_ready = sem("pT_ready")
        attn_psum = sem("attn_psum")
        attn_added = sem("attn_added")
        h1_psum = [sem(f"h1_psum{r}") for r in range(2)]
        h1_ready = [sem(f"h1_ready{r}") for r in range(2)]
        h2_psum = [sem(f"h2_psum{r}") for r in range(2)]
        h2_ready = [sem(f"h2_ready{r}") for r in range(2)]
        h3_psum = [sem(f"h3_psum{r}") for r in range(2)]
        h3_ready = [sem(f"h3_ready{r}") for r in range(2)]
        z_psum = [sem(f"z_psum{r}") for r in range(2)]
        th_ready = [sem(f"th_ready{r}") for r in range(2)]
        y_ready = [sem(f"y_ready{r}") for r in range(2)]
        tw_psum = sem("tw_psum")
        tw_ready = sem("tw_ready")
        ctx_ready = sem("ctx_ready")
        gc_psum = sem("gc_psum")
        gc_ready = sem("gc_ready")
        gain_ready = sem("gain_ready")
        ffnT_psum = sem("ffnT_psum")
        q1_ready = sem("q1_ready")
        bn_done = sem("bn_done")
        s1_psum = sem("s1_psum")
        s1_ready = sem("s1_ready")
        signs_ready = sem("signs_ready")
        max1_ready = sem("max1_ready")
        bands_done = sem("bands_done")
        exp1_done = sem("exp1_done")
        p1T_psum = sem("p1T_psum")
        p1T_ready = sem("p1T_ready")
        attn1_psum = sem("attn1_psum")
        attn1_added = sem("attn1_added")
        lg_psum = sem("lg_psum")
        onehot_ready = sem("onehot_ready")
        ohT_psum = sem("ohT_psum")
        ohT_ready = sem("ohT_ready")
        fc_psum = sem("fc_psum")
        mask_psum = sem("mask_psum")
        relu_ready = sem("relu_ready")
        picked_ready = sem("picked_ready")
        act_ready = sem("act_ready")
        moe_psum = sem("moe_psum")
        out_ready = sem("out_ready")
        stored = sem("stored")

        def nchunks(i):
            return (i + TPC) // TPC

        def first_chunk(i):
            return sum(nchunks(j) for j in range(i))

        def width(i, c):
            return min(C, (i + 1) * P - c * C)

        SRING = 4
        REST = ((0, 3), (0, 4), (0, 5), (1, 0), (1, 1), (1, 3), (1, 4))
        KV_JOBS = (("k", 0, 2), ("v", 0, 3), ("q", 0, 0), ("k", 1, 1), ("v", 1, 2), ("k", 2, 3), ("k", 3, 4),
                   ("v", 2, 5), ("v", 3, 4), ("q", 1, 7), ("q", 2, 6), ("q", 3, 7))
        HALF = 2 * C
        HALVES = S // HALF
        TWIST_BANK = (6, 5, 7, 1)
        CONTEXT_BANK = 7
        FFN_OUT_BANK = (0, 1, 4, 5)
        LAST_LN_BANK = [bank[b] for b in (0, 2, 3, 7)]
        LOGIT_BANK = 1
        FC_BANK = (2, 3, 6)
        OUT_BANK = (4, 7)
        PICK_BANK = (5, 0)
        ONEHOT_PARTS = ((0, 8), (8, 12), (12, 16))

        def onehot_psum(h):
            a, b = ONEHOT_PARTS[h]
            at = (0, 2 * P, 2 * P)[h]
            return oh_ps[min(h, 1)][0:EXPERTS, at:at + (b - a) * P]
        QKV_JOBS = 4 * G

        def chunk_of(r, u):
            return 2 * (1 - r) + u

        def tiles_ahead(i):
            if i + 2 < 2 * TPC:
                return [i + 2]
            return [i + 1] if 2 * TPC <= i + 1 < T else []

        SIDE_STEPS = QKV_JOBS + G - 1 - 5
        def side_bank(j):
            return bank[4 + j] if j < 4 else bank[4]
        x_t = x.rearrange("a (t p) d -> p (a t) d", p=P)
        out_t = out.rearrange("a (t p) d -> p (a t) d", p=P)

        def col(w):
            return w.rearrange("(p a) -> p a", a=1)

        block = ctx.enter_context(nc.Block())

        @block.sync
        def _(sp):
            sp.dma_start(xres[:, 0:TPC, :], x_t[:, 0:TPC, :]).then_inc(ld_x[0], 16)
            sp.dma_start(wmod[:, 0, 0:3 * P], wmod0[:, 0:3 * P]).then_inc(ld_wmod[0], 16)
            for n, w in enumerate((Wq, Wk, Wv)):
                sp.dma_start(wqkv0_raw[:, n, :], w).then_inc(ld_attn0, 16)
            for g in range(1, G):
                sp.dma_start(xres[:, g * TPC:(g + 1) * TPC, :],
                             x_t[:, g * TPC:(g + 1) * TPC, :]).then_inc(ld_x[g], 16)
                if g == 1:
                    sp.dma_start(wmod[:, 0, 3 * P:6 * P], wmod0[:, 3 * P:6 * P]).then_inc(ld_wmod[1], 16)
                    sp.dma_start(wmod[:, 1, :], wmod1).then_inc(ld_wmod[2], 16)
            sp.dma_start(wqkv1[:, :, :], W_qkv.rearrange("d (n e) -> d n e", n=3)).then_inc(ld_l1, 16)
            sp.dma_start(wproj1[:, :], W_proj).then_inc(ld_l1, 16)
            sp.dma_start(bproj_row[:, :], b_proj.partition_broadcast(P)).then_inc(ld_l1, 16)
            for n in range(3):
                sp.dma_start(bqkv1[:, n:n + 1], col(b_qkv[n * P:(n + 1) * P])).then_inc(ld_l1, 16)
            sp.dma_start(wr_raw[:, :], w_router).then_inc(ld_moe, 16)
            for c in range(TPC):
                sp.dma_start(wfc_raw[:, c, :],
                             w_fc[2 * c:2 * c + 2, :, :].rearrange("u h d -> (u h) d")).then_inc(ld_moe, 16)
            sp.dma_start(wpr_raw[:, :, :], w_proj.rearrange("e d h -> d e h")).then_inc(ld_moe, 16)
            for dst, src in ((w1s[:, :], cn_w1), (w2s[:, :], cn_w2), (g1s[:, :], gc_w1), (g2s[:, :], gc_w2),
                             (g3s[:, :], gc_w3), (w4s[0:H3, :], cn_w4), (w4s[H3:2 * H3, :], cn_w4),
                             (cb1[:, :], col(cn_b1)), (cb2[0:H2, :], col(cn_b2)), (cb2[H2:P, :], col(cn_b2)),
                             (cb3[0:H3, :], col(cn_b3)), (cb3[H3:2 * H3, :], col(cn_b3)),
                             (cb4[:, :], cn_b4.partition_broadcast(P)), (gb1s[:, :], col(gc_b1)),
                             (gb2s[:, :], col(gc_b2)), (gb3s[:, :], gc_b3.partition_broadcast(P)),
                             (arange[:, :], adaptive_range.partition_broadcast(P))):
                sp.dma_start(dst, src).then_inc(ld_ffn0, 16)
            sp.wait_ge(consts_ready, 1)
            for u in range(2):
                sp.dma_start(w3s[u * H2:(u + 1) * H2, u * H3:(u + 1) * H3], cn_w3).then_inc(ld_ffn0, 16)
            for g in range(G):
                sp.wait_ge(out_ready, g + 1)
                sp.dma_start(out_t[:, g * TPC:(g + 1) * TPC, :],
                             xres[:, g * TPC:(g + 1) * TPC, :]).then_inc(stored, 16)
            sp.wait_ge(stored, 16 * G)
        FFN_LOADS = 19

        @block.gpsimd
        def _(pool):
            pool.memset(ident[:, :], 0.0)
            pool.memset(ones[:, :], 1.0)
            pool.memset(edge_bias[:, 0:1], -BAND_EDGES[2])
            pool.memset(edge_bias[:, 1:2], -BAND_EDGES[3])
            pool.memset(epsilon[:, :], LN_EPS)
            pool.memset(minus_unit[:, :], -BAND_UNIT * SCALE1)
            pool.memset(neghalf[:, :], -0.5).then_inc(pool_chain, 1)
            pool.wait_ge(pool_chain, 1)
            pool.affine_select(out=ident[:, :], in_=ident[:, :], compare_op=ALU.not_equal, fill=1.0,
                               base=0, pattern=[[-1, P]], channel_multiplier=1).then_inc(ident_ready, 1)
            pool.memset(causal[:, :], 0.0)
            pool.memset(identb[:, :], 0.0).then_inc(pool_chain, 1)
            pool.wait_ge(pool_chain, 2)
            pool.affine_select(out=identb[:, :], in_=identb[:, :], compare_op=ALU.not_equal, fill=1.0,
                               base=0, pattern=[[-1, P]], channel_multiplier=1)
            pool.affine_select(out=causal[:, :], in_=causal[:, :], compare_op=ALU.is_ge, fill=MASKED,
                               base=0, pattern=[[-1, P]], channel_multiplier=1).then_inc(causal_ready, 1)

            def ln_rstd(ph, g):
                n = ph * G + g
                s = slice(n * TPC, (n + 1) * TPC)
                pool.wait_ge(stats_ready, n + 1)
                pool.tensor_scalar(veps[:, s], mv[:, s, 1], LN_EPS, None, ALU.add).then_inc(pool_chain, 1)
                pool.wait_ge(pool_chain, n + (3 if ph == 0 else 4))
                pool.tensor_tensor(rstd[:, s], veps[:, s], neghalf[:, :], ALU.pow).then_inc(rstd_ready, 1)

            for g in range(G):
                ln_rstd(0, g)
            pool.memset(w3s[:, :], 0.0)
            pool.memset(twist[:, :], 0.0)
            for e in range(EXPERTS):
                pool.memset(tie_rank[:, :, e:e + 1], float(EXPERTS - e))
            pool.memset(expert_sel[:, :, :, :], 0.0).then_inc(pool_chain, 1)
            pool.wait_ge(pool_chain, 3 + G)
            for j0, src, sgn in ((0, 64, 1.0), (32, 96, -1.0), (64, 0, -1.0), (96, 32, 1.0)):
                pool.affine_select(out=twist[:, j0:j0 + 32], in_=twist[:, j0:j0 + 32],
                                   compare_op=ALU.not_equal, fill=sgn, base=-src,
                                   pattern=[[-1, 32]], channel_multiplier=1)
            pool.affine_select(out=expert_sel[:, :, :, :], in_=expert_sel[:, :, :, :],
                               compare_op=ALU.not_equal, fill=1.0, base=0,
                               pattern=[[-2, TPC], [-1, 2], [0, 64]],
                               channel_multiplier=1).then_inc(consts_ready, 1)
            pool.wait_ge(bias_row_ready, 1)
            for g in range(G):
                pool.wait_ge(norm_ready, g + 1)
                pool.tensor_tensor(xres[:, g * TPC:(g + 1) * TPC, :], xres[:, g * TPC:(g + 1) * TPC, :],
                                   add0_row[:, :].unsqueeze(1).to_broadcast([P, TPC, P]),
                                   ALU.add).then_inc(res_biased, 1)
            for g in range(G):
                ln_rstd(1, g)
            for g in range(G):
                ln_rstd(2, g)
            def place_query(j, u):
                pool.tensor_copy(qbuf[:, u, :], q1T[:, bass.ds(j * P, P)]).then_inc(q1_ready, 1)

            def next_query(j, u):
                pool.wait_ge(s1_psum, (j - 1) * HALVES)
                place_query(j, u)

            def last_rstd(g):
                s = slice(3 * T, 3 * T + TPC)
                pool.wait_ge(stats_ready, g + (3 * G + 1))
                pool.tensor_tensor(veps[:, s], mv[:, s, 1], epsilon[:, :], ALU.add).then_inc(pool_chain, 1)
                pool.wait_ge(pool_chain, g + (3 * G + 4))
                pool.tensor_tensor(rstd[:, s], veps[:, s], neghalf[:, :], ALU.pow).then_inc(rstd_ready, 1)
                pool.tensor_copy(xres[:, bass.ds(g * TPC, TPC), :], attended[:, :, :]).then_inc(res_biased, 1)

            pool.wait_ge(kv_ready, 3)
            place_query(0, 0)
            place_query(1, 1)
            pool.wait_ge(wvp_ready, 1)
            for g in range(G):
                pool.wait_ge(norm_ready, 2 * G + g + 1)
                pool.tensor_tensor(xres[:, g * TPC:(g + 1) * TPC, :], xres[:, g * TPC:(g + 1) * TPC, :],
                                   add1_row[:, :].unsqueeze(1).to_broadcast([P, TPC, P]),
                                   ALU.add).then_inc(res_biased, 1)
            def negate_max(j, u):
                pool.wait_ge(max1_ready, j + 1)
                pool.tensor_tensor(negmax1[:, u:u + 1], max1[:, u:u + 1], minus_unit[:, :], ALU.mult)\
                  .then_inc(bands_done, 1)

            next_query(2, 0)
            negate_max(0, 0)
            next_query(3, 1)
            negate_max(1, 1)
            pool.wait_ge(kv_ready, len(KV_JOBS))
            next_query(4, 0)
            negate_max(2, 0)
            with pool.Fori(0, G - 2) as g:
                for t in range(TPC):
                    next_query(g * TPC + (t + 5), (t + 1) % 2)
                    if t == TPC - 1:
                        last_rstd(g)
                    negate_max(g * TPC + (t + 3), (t + 1) % 2)
            for j in range(T - 5, T):
                if j + 2 < T:
                    next_query(j + 2, j % 2)
                if j == T - 2:
                    last_rstd(G - 2)
                negate_max(j, j % 2)
            last_rstd(G - 1)

        @block.scalar
        def _(act):
            act.dma_start(c_col[:, 0:1], c0.rearrange("a p -> p a")).then_inc(ld_c, 16)
            act.dma_start(c_col[:, 1:2], c1.rearrange("a p -> p a")).then_inc(ld_c, 16)
            act.dma_start(bqk0[:, 0:1], col(bq)).then_inc(ld_bias0, 16)
            act.dma_start(bqk0[:, 1:2], col(bk)).then_inc(ld_bias0, 16)
            act.dma_start(bv_row[:, :], bv.partition_broadcast(P)).then_inc(ld_bias0, 16)

            act.wait_ge(ident_ready, 1)
            nc.scalar.activation(warm[:, :], ones[:, 0:1], ACT.Tanh)
            act.wait_ge(ld_c, 32)
            nc.scalar.activation(tanh_c[:, :], c_col[:, :], ACT.Tanh, scale=0.5).then_inc(tanh_c_ready, 1)
            act.wait_ge(w0T_psum, 1)
            nc.scalar.activation(wqkvT0[:, 0:2, :], bank[0].rearrange("p (n e) -> p n e", n=4)[:, 0:2, :],
                                 ACT.Copy).then_inc(w0T_ready, 1)

            def affine(dst, g, src, layer, shift, scale):
                return nc.scalar.activation(dst[:, g * C:(g + 1) * C], src, ACT.Identity,
                                            bias=modc[:, layer, shift:shift + 1],
                                            scale=modp[:, layer, scale:scale + 1])

            def fetch_side(j):
                act.wait_ge(side_psum, j + 1)
                g, what, src = j // 4, j % 4, side_bank(j)
                if j >= QKV_JOBS:
                    ins = affine(yT, j - QKV_JOBS, src, 0, 3, 4)
                elif what == 0:
                    ins = affine(hT, g, src, 0, 0, 1)
                elif what == 3:
                    ins = nc.scalar.activation(v[:, g * TPC:(g + 1) * TPC, :],
                                               src.rearrange("p (t e) -> p t e", t=TPC), ACT.Copy)
                elif what == 1:
                    ins = nc.scalar.activation(qT[:, g * C:(g + 1) * C], src, ACT.Identity,
                                               bias=bq0_scaled[:, :], scale=SCALE0)
                else:
                    ins = nc.scalar.activation(kT[:, g * C:(g + 1) * C], src, ACT.Identity, bias=bqk0[:, 1:2])
                ins.then_inc(side_ready, 1)

            act.wait_ge(mod_ready, 1)
            for j in range(4):
                fetch_side(j)

            def exp_tile(i):
                act.wait_ge(negmax_ready, i + 1)
                if i >= 3:
                    act.wait_ge(attn_psum, i - 2)
                for c in range(nchunks(i)):
                    w = width(i, c)
                    nc.scalar.activation(probs0[i % 3][:, c * C:c * C + w],
                                         bank[(first_chunk(i) + c) % SRING][:, 0:w], ACT.Exp,
                                         bias=negmax[:, i:i + 1],
                                         accum_out=rs[:, i, c:c + 1]).then_inc(exp_done, 1)

            exp_tile(0)
            exp_tile(1)
            fetch_side(4)
            act.wait_ge(mod_psum, 2)
            nc.scalar.activation(mod_raw[:, :, :], bank[7][:, 0:3 * P].rearrange("p (n e) -> p n e", n=3), ACT.Copy)\
              .then_inc(mod_fetched, 1)
            for i in range(T - 1):
                if i == 2:
                    act.wait_ge(mod_ready, 3)
                if i < SIDE_STEPS:
                    fetch_side(5 + i)
                for j in tiles_ahead(i):
                    exp_tile(j)
            def fetch_twisted(k):
                act.wait_ge(tw_psum, k + 1)
                nc.scalar.activation(vT[:, k * C:(k + 1) * C], bank[TWIST_BANK[k]], ACT.Copy).then_inc(tw_ready, 1)

            def gelu1(r, u, cyc):
                act.wait_ge(h1_psum[r], cyc * 2 + (u + 1))
                nc.scalar.activation(a1[:, r, u, :], bank[2 * r + u], ACT.Gelu, bias=cb1[:, :])\
                  .then_inc(h1_ready[r], 1)

            def gelu2(r, cyc):
                act.wait_ge(h2_psum[r], cyc + 1)
                nc.scalar.activation(a2[:, r, :], bank[4 + r], ACT.Gelu, bias=cb2[:, :]).then_inc(h2_ready[r], 1)

            def gelu3(r, cyc):
                act.wait_ge(h3_psum[r], cyc + 1)
                nc.scalar.activation(a3[:, r, :], bank[4 + r][0:2 * H3, :], ACT.Gelu, bias=cb3[:, :])\
                  .then_inc(h3_ready[r], 1)

            def tanh_z(r, cyc):
                for u in range(2):
                    act.wait_ge(z_psum[r], cyc * 2 + (u + 1))
                    nc.scalar.activation(th[:, r, u, :], bank[(6, 2)[r] + u], ACT.Tanh, bias=cb4h[:, :], scale=0.5)\
                  .then_inc(th_ready[r], 1)

            fetch_twisted(0)
            fetch_twisted(1)
            gelu1(1, 0, 0)
            gelu1(1, 1, 0)
            fetch_twisted(2)
            fetch_side(T + 3)
            fetch_twisted(3)
            gelu1(0, 0, 0)
            gelu2(1, 0)
            act.wait_ge(gc_psum, 1)
            nc.scalar.activation(g_a1[:, :], bank[CONTEXT_BANK][0:H2, 0:1], ACT.Gelu, bias=gb1s[:, :])\
              .then_inc(gc_ready, 1)
            gelu1(0, 1, 0)
            act.wait_ge(gc_psum, 2)
            nc.scalar.activation(g_a2[:, :], bank[CONTEXT_BANK][0:H3, 0:1], ACT.Gelu, bias=gb2s[:, :])\
              .then_inc(gc_ready, 1)
            act.wait_ge(gc_psum, 3)
            nc.scalar.activation(g_th[:, :], bank[CONTEXT_BANK][:, 0:1], ACT.Tanh, bias=gb3h[:, :], scale=0.5)\
              .then_inc(gc_ready, 1)

            def cycle_act(cyc):
                gelu3(1, cyc)
                gelu2(0, cyc)
                tanh_z(1, cyc)
                gelu3(0, cyc)
                tanh_z(0, cyc)

            with act.Fori(0, CYCLES - 1) as cyc:
                cycle_act(cyc)
                for r, u in ((1, 0), (1, 1), (0, 0)):
                    gelu1(r, u, cyc + 1)
                gelu2(1, cyc + 1)
                gelu1(0, 1, cyc + 1)
            cycle_act(CYCLES - 1)

            nc.scalar.activation(warm[:, :], ones[:, 0:1], ACT.Exp)

            def fetch_scores(j, u, h):
                act.wait_ge(s1_psum, j * HALVES + (h + 1))
                nc.scalar.activation(scores[:, u, h * HALF:(h + 1) * HALF], sc4[:, 2 * h:2 * h + 2, :]
                                     .rearrange("p b t -> p (b t)"), ACT.Copy).then_inc(s1_ready, 1)

            def sign_part(u, edge, a, b):
                return nc.scalar.activation(sign[:, u, edge, a:b], scores[:, u, a:b], ACT.Sign,
                                            bias=edge_bias[:, edge:edge + 1], scale=SCALE1)

            def first_norm_affine(g):
                act.wait_ge(lnT_psum, g + 1)
                affine(hT, g, bank[6 + g % 2], 1, 0, 1).then_inc(lnT_ready, 1)

            def fetch_kv(n):
                what, g, b = KV_JOBS[n]
                act.wait_ge(kv_psum, n + 1)
                if what == "v":
                    ins = nc.scalar.activation(v[:, g * TPC:(g + 1) * TPC, :],
                                               bank[b].rearrange("p (t e) -> p t e", t=TPC), ACT.Copy)
                else:
                    ins = nc.scalar.activation((q1T if what == "q" else kT)[:, g * C:(g + 1) * C], bank[b],
                                               ACT.Identity, bias=bqkv1[:, "qk".index(what):"qk".index(what) + 1])
                ins.then_inc(kv_ready, 1)

            first_norm_affine(0)
            for n in range(3):
                fetch_kv(n)
            first_norm_affine(1)
            fetch_kv(3)
            fetch_kv(4)
            first_norm_affine(2)
            fetch_kv(5)
            first_norm_affine(3)
            fetch_scores(0, 0, 0)
            fetch_kv(6)
            act.wait_ge(s1_ready, 1)
            sign_part(0, 0, 0, HALF)
            fetch_scores(0, 0, 1)
            sign_part(0, 1, 0, HALF)
            act.wait_ge(s1_ready, HALVES)
            sign_part(0, 0, HALF, S)
            sign_part(0, 1, HALF, S).then_inc(signs_ready, 1)

            def attend_act(j, u, scores_too=True, meanwhile=((), ())):
                act.wait_ge(bands_done, j + 1)
                nc.scalar.activation(probs[:, u, :], probs[:, u, :], ACT.Exp, bias=negmax1[:, u:u + 1],
                                     scale=BAND_UNIT * SCALE1, accum_out=rsum1[:, u:u + 1]).then_inc(exp1_done, 1)
                if scores_too:
                    for h in range(HALVES):
                        fetch_scores(j + 2, u, h)
                for h in range(HALVES):
                    act.wait_ge(p1T_psum, j * HALVES + (h + 1))
                    nc.scalar.activation(pT[:, 2 * h:2 * h + 2, :, :].rearrange("p c t q -> p (c t q)"),
                                         turn2[:, :, :].rearrange("p b t -> p (b t)"), ACT.Copy)\
                      .then_inc(p1T_ready, 1)
                    if scores_too:
                        act.wait_ge(s1_ready, j * HALVES + 3 * HALVES)
                        ins = sign_part(u, h, 0, S)
                    for step, n in meanwhile[h]:
                        step(n)
                if scores_too:
                    ins.then_inc(signs_ready, 1)

            for h in range(HALVES):
                fetch_scores(1, 1, h)
            act.wait_ge(s1_ready, 2 * HALVES)
            sign_part(1, 0, 0, S)
            sign_part(1, 1, 0, S).then_inc(signs_ready, 1)
            for n in range(7, len(KV_JOBS)):
                fetch_kv(n)
            with act.Fori(0, T // 2 - 2) as pair:
                for u in range(2):
                    attend_act(pair * 2 + u, u)

            def last_affine(g):
                act.wait_ge(lnT_psum, G + g + 1)
                affine(hT, g, LAST_LN_BANK[g], 1, 3, 4).then_inc(lnT_ready, 1)

            def relu(n):
                act.wait_ge(fc_psum, n + 1)
                nc.scalar.activation(relu_h[n % 3], bank[FC_BANK[n % 3]], ACT.Relu).then_inc(relu_ready, 1)

            def fetch_onehot(h):
                a, b = ONEHOT_PARTS[h]
                act.wait_ge(ohT_psum, h + 1)
                nc.scalar.activation(ohT[:, a * P:b * P], onehot_psum(h), ACT.Copy).then_inc(ohT_ready, 1)

            attend_act(T - 4, 0)
            attend_act(T - 3, 1)
            attend_act(T - 2, 0, False, (((last_affine, 0), (last_affine, 1)), ((last_affine, 2),)))
            attend_act(T - 1, 1, False, (((relu, 0), (relu, 1), (fetch_onehot, 0)), ((fetch_onehot, 1),)))

            def square(n):
                act.wait_ge(picked_ready, n + 1)
                if n >= 2 * TPC:
                    act.wait_ge(moe_psum, n - 2 * TPC + 1)
                nc.scalar.activation(act2[:, n // TPC % 2, n % TPC, :], picked[n % 3], ACT.Square, scale=0.5)\
                  .then_inc(act_ready, 1)

            for n in range(G * TPC):
                if n >= 2:
                    relu(n)
                if n == 5:
                    last_affine(G - 1)
                if n == 10:
                    fetch_onehot(2)
                if n >= 1:
                    square(n - 1)
            square(G * TPC - 1)

        @block.vector
        def _(dve):
            links = [0]

            def link(ins):
                links[0] += 1
                ins.then_inc(dve_chain, 1)
                dve.wait_ge(dve_chain, links[0])

            def nrm_free(n):
                if n < G:
                    dve.wait_ge(side_psum, 4 * n + 1)
                elif n < 2 * G:
                    dve.wait_ge(side_psum, QKV_JOBS + n - G + 1)
                else:
                    dve.wait_ge(lnT_psum, n - 2 * G + 1)

            def ln_stats(n, g):
                for t in range(TPC):
                    last = nc.vector.bn_stats(st[:, n * TPC + t, :], xres[:, g * TPC + t, :])
                link(last)
                for t in range(TPC):
                    last = nc.vector.bn_aggr(mv[:, n * TPC + t, :], st[:, n * TPC + t, :])
                last.then_inc(stats_ready, 1)

            def ln_norm(n, g):
                dve.wait_ge(rstd_ready, n + 1)
                if n >= G:
                    nrm_free(n - G)
                for t in range(TPC):
                    k = n * TPC + t
                    last = nc.vector.tensor_scalar(nrm[:, n % G, t, :], xres[:, g * TPC + t, :],
                                                   mv[:, k, 0:1], rstd[:, k:k + 1], ALU.subtract, ALU.mult)
                last.then_inc(norm_ready, 1)

            dve.wait_ge(ld_x[0], 16)
            ln_stats(0, 0)
            ln_norm(0, 0)
            dve.wait_ge(tanh_c_ready, 1)
            dve.wait_ge(ident_ready, 1)
            link(nc.vector.scalar_tensor_tensor(out=silu_col[:, :], in0=tanh_c[:, :], scalar=1.0,
                                                in1=c_col[:, :], op0=ALU.add, op1=ALU.mult))
            for n in range(2):
                last = nc.vector.tensor_scalar(silu_b[:, n, :], ones[:, :], silu_col[:, n:n + 1], 0.5,
                                               ALU.mult, ALU.mult)
            last.then_inc(silu_ready, 1)

            def gate(out, sgn, mag, src, done=None):
                link(nc.vector.tensor_scalar(sgn, src, 0.0, 2.0, ALU.is_ge, ALU.mult))
                link(nc.vector.scalar_tensor_tensor(out=mag, in0=sgn, scalar=-1.0, in1=src,
                                                    op0=ALU.add, op1=ALU.mult))
                link(nc.vector.tensor_scalar(mag, mag, GATE_FLOOR, None, ALU.max))
                last = nc.vector.scalar_tensor_tensor(out=out, in0=sgn, scalar=-1.0, in1=mag,
                                                      op0=ALU.add, op1=ALU.mult)
                if done is None:
                    link(last)
                else:
                    last.then_inc(done, 1)

            dve.wait_ge(ld_bias0, 48)
            nc.vector.tensor_scalar(bq0_scaled[:, :], bqk0[:, 0:1], SCALE0, None, ALU.mult)
            dve.wait_ge(mod_psum, 1)
            nc.vector.tensor_copy(modc[:, 0, 0:2], bank[1][:, 0:2])
            nc.vector.tensor_scalar(modp[:, 0, 0:2], bank[1][:, 0:2], 1.0, None, ALU.add).then_inc(mod_ready, 1)
            dve.wait_ge(w0T_ready, 1)
            link(nc.vector.tensor_copy(wvT0_raw[:, :], bank[0][:, 2 * P:3 * P]))
            gate(gate_row[:, 0, :], gate_sign[:, 0, :], gate_mag[:, 0, :], bank[2][:, 0:P])
            nc.vector.tensor_tensor(wqkvT0[:, 2, :], wvT0_raw[:, :], gate_row[:, 0, :], ALU.mult)\
              .then_inc(mod_ready, 1)
            for g in range(1, G):
                dve.wait_ge(ld_x[g], 16)
                ln_stats(g, g)
            nc.vector.tensor_tensor(add0_row[:, :], bv_row[:, :], gate_row[:, 0, :], ALU.mult)\
              .then_inc(bias_row_ready, 1)
            for g in range(1, G):
                ln_norm(g, g)

            def other_modulation():
                dve.wait_ge(mod_fetched, 1)
                for dst, one in ((modc, 0.0), (modp, 1.0)):
                    nc.vector.tensor_scalar(dst[:, 0, 3:6], mod_raw[:, 0, 0:3], one, None, ALU.add)
                    nc.vector.tensor_scalar(dst[:, 1, 0:2], mod_raw[:, 0, 3:5], one, None, ALU.add)
                    nc.vector.tensor_scalar(dst[:, 1, 3:5], mod_raw[:, 0, 5:7], one, None, ALU.add)
                gate(gb0_col[:, :], gcol_sign[:, :], gcol_mag[:, :], mod_raw[:, 0, 2:3])
                nc.vector.tensor_scalar(gb0_diag[:, :], ident[:, :], gb0_col[:, :], None, ALU.mult)
                gate(gate_row[:, 1:3, :], gate_sign[:, 1:3, :], gate_mag[:, 1:3, :],
                     mod_raw[:, 1:3, :], mod_ready)

            def net_weights():
                dve.wait_ge(ld_ffn0, 16 * FFN_LOADS)
                nc.vector.tensor_scalar(w4b[:, :], ones[0:2 * H3, :], w4s[:, :], None, ALU.mult)
                nc.vector.tensor_scalar(g3b[:, :], ones[0:H3, :], g3s[:, :], None, ALU.mult)
                nc.vector.tensor_scalar(cb4h[:, :], cb4[:, :], 0.5, None, ALU.mult)
                nc.vector.tensor_scalar(gb3h[:, :], gb3s[:, :], 0.5, None, ALU.mult)
                nc.vector.tensor_scalar(cpl_b[:, :], arange[:, :], 0.3, None, ALU.mult)
                dve.wait_ge(ld_l1, 96)
                nc.vector.tensor_scalar(bv1_b[:, :], ones[:, :], bqkv1[:, 2:3], None, ALU.mult)\
                  .then_inc(ffn_w_ready, 1)

            def later_weights():
                nc.vector.tensor_copy(wfcT[:, :, :], bank[0].rearrange("p (c e) -> p c e", c=TPC))
                nc.vector.tensor_tensor(wpr[:, :, :], bank[1].rearrange("p (c e) -> p c e", c=TPC),
                                        gate_row[:, 2, :].unsqueeze(1).to_broadcast([P, TPC, P]), ALU.mult)\
                  .then_inc(wmoe_ready, 1)

            def row_max(i):
                n = nchunks(i)
                for c in range(n):
                    q = first_chunk(i) + c
                    dve.wait_ge(score_psum, q + 1)
                    last = nc.vector.tensor_reduce((negmax[:, i:i + 1] if n == 1 else mx[:, i, c:c + 1]),
                                                   bank[q % SRING][:, 0:width(i, c)], AX.X, ALU.max, negate=(n == 1))
                if n > 1:
                    link(last)
                    last = nc.vector.tensor_reduce(negmax[:, i:i + 1], mx[:, i, 0:n], AX.X, ALU.max, negate=True)
                last.then_inc(negmax_ready, 1)

            def fetch_pT(i, c):
                q = first_chunk(i) + c
                n = width(i, c) // P
                dve.wait_ge(pT_psum, q + 1)
                nc.vector.tensor_copy(pT[:, q % 2, 0:n, :],
                                      bank[5 + q % 2][:, 0:n * P].rearrange("p (t q) -> p t q", t=n))\
                  .then_inc(pT_ready, 1)

            def context_part(k):
                dve.wait_ge(side_ready, QKV_JOBS + k + 1)
                nc.vector.reduce_sum(ctx_parts[:, k:k + 1], yT[:, k * C:(k + 1) * C], AX.X)\
                  .then_inc(y_ready[1 - k // 2], 1)

            row_max(0)
            row_max(1)
            for i in range(T):
                n = nchunks(i)
                for c in range(min(2, n)):
                    fetch_pT(i, c)
                for j in tiles_ahead(i):
                    row_max(j)
                for c in range(2, n):
                    fetch_pT(i, c)
                if i == 0:
                    other_modulation()
                if i == 3:
                    net_weights()
                if i == T - 3:
                    context_part(0)
                    context_part(1)
                if i == T - 2:
                    context_part(2)
                if i == T - 1:
                    dve.wait_ge(w1T_psum, 1)
                    nc.vector.tensor_copy(wvT1[:, :], bank[2][:, 0:P])
                    nc.vector.tensor_copy(wrT[:, :], bank[2][:, P:P + EXPERTS]).then_inc(wv1T_ready, 1)
                if i >= TPC and i % TPC == 0:
                    ln_norm(G + i // TPC - 1, i // TPC - 1)
                dve.wait_ge(exp_done, first_chunk(i + 1))
                if n > 1:
                    link(nc.vector.reduce_sum(rsum[:, i:i + 1], rs[:, i, 0:n], AX.X))
                link(nc.vector.reciprocal(rinv[:, i:i + 1], rsum[:, i:i + 1] if n > 1 else rs[:, i, 0:1]))
                dve.wait_ge(attn_psum, i + 1)
                dve.wait_ge(res_biased, i // TPC + 1)
                nc.vector.scalar_tensor_tensor(out=xres[:, i, :], in0=bank[7][:, 0:P], scalar=rinv[:, i:i + 1],
                                               in1=xres[:, i, :], op0=ALU.mult, op1=ALU.add).then_inc(attn_added, 1)
                if i % TPC == TPC - 1:
                    dve.wait_ge(attn_added, i + 1)
                    ln_stats(G + i // TPC, i // TPC)

            later_weights()
            ln_norm(2 * G - 1, G - 1)
            context_part(G - 1)
            for r in range(2):
                dve.wait_ge(y_ready[r], 2)
            link(nc.vector.reduce_sum(ctx_sum[:, :], ctx_parts[:, :], AX.X))
            nc.vector.tensor_scalar(ctx_mean[:, :], ctx_sum[:, :], 1.0 / S, None, ALU.mult).then_inc(ctx_ready, 1)
            dve.wait_ge(wvp_psum, 1)
            nc.vector.tensor_tensor(wvp1[:, :], bank[4][:, 0:P], gate_row[:, 1, :], ALU.mult)
            link(nc.vector.tensor_tensor(add1_pre[:, :], bank[4][:, P:2 * P], bproj_row[:, :], ALU.add))
            nc.vector.tensor_tensor(add1_row[:, :], add1_pre[:, :], gate_row[:, 1, :], ALU.mult)\
              .then_inc(wvp_ready, 1)
            dve.wait_ge(gc_ready, 3)
            link(nc.vector.tensor_scalar(cpl_a0[:, :], g_th[:, :], 0.7, None, ALU.mult))
            link(nc.vector.tensor_scalar(cpl_a1[:, :], cpl_a0[:, :], arange[:, :], None, ALU.mult))
            link(nc.vector.tensor_scalar(cpl_a[:, :], cpl_a1[:, :], 0.1, None, ALU.add))
            base = links[0]
            dve.wait_ge(tw_ready, G)

            def coupling(r, u, cyc):
                dve.wait_ge(th_ready[r], cyc * 2 + (u + 1))
                nc.vector.tensor_scalar(cpl[:, r, u, :], th[:, r, u, :], cpl_b[:, :], cpl_a[:, :],
                                        ALU.mult, ALU.add).then_inc(dve_chain, 1)

            def state(i, k):
                return ybuf[:, bass.ds(i, 1), k * C:(k + 1) * C].rearrange("p a t -> p (a t)")

            def couple(r, cyc, at):
                for u in range(2):
                    k = chunk_of(r, u)
                    coupling(r, u, cyc)
                    dve.wait_ge(dve_chain, at + (2 * u + 1))
                    nc.vector.tensor_tensor(gain[:, r, u, :], cpl[:, r, u, :], vT[:, k * C:(k + 1) * C], ALU.mult)\
                      .then_inc(dve_chain, 1)
                    dve.wait_ge(dve_chain, at + (2 * u + 2))
                    nc.vector.tensor_tensor(state(cyc + 1, k), state(cyc, k), gain[:, r, u, :], ALU.add)\
                      .then_inc(y_ready[r], 1)

            def lose(r, cyc, at):
                for u in range(2):
                    ins = nc.vector.tensor_tensor(loss[:, r, u, :], cpl[:, r, u, :], state(cyc, chunk_of(r, u)),
                                                  ALU.mult)
                ins.then_inc(dve_chain, 1)
                dve.wait_ge(dve_chain, at)
                for u in range(2):
                    k = chunk_of(r, u)
                    vs = vT[:, k * C:(k + 1) * C]
                    ins = nc.vector.tensor_tensor(vs, vs, loss[:, r, u, :], ALU.subtract)
                ins.then_inc(dve_chain, 1)

            with dve.Fori(0, CYCLES - 1) as cyc:
                couple(1, cyc, cyc * 12 + base)
                couple(0, cyc, cyc * 12 + (base + 4))
                lose(1, cyc, cyc * 12 + (base + 9))
                lose(0, cyc, cyc * 12 + (base + 11))
            links[0] = base + 12 * (CYCLES - 1)

            def last_gain(g):
                r, u = 1 - g // 2, g % 2
                coupling(r, u, CYCLES - 1)
                links[0] += 1
                dve.wait_ge(dve_chain, links[0])
                ins = nc.vector.tensor_tensor(gain[:, r, u, :], cpl[:, r, u, :], vT[:, g * C:(g + 1) * C], ALU.mult)
                if g < 2:
                    link(ins)
                    ys = yT_last[:, g * C:(g + 1) * C]
                    ins = nc.vector.tensor_tensor(ys, ys, gain[:, r, u, :], ALU.add)
                ins.then_inc(gain_ready, 1)

            def add_ffn(g):
                dve.wait_ge(ffnT_psum, g + 1)
                xs = xres[:, g * TPC:(g + 1) * TPC, :]
                link(nc.vector.tensor_tensor(xs, xs, bank[FFN_OUT_BANK[g]].rearrange("p (t e) -> p t e", t=TPC),
                                             ALU.add))
                ln_stats(2 * G + g, g)

            last_gain(0)
            last_gain(1)
            add_ffn(0)
            for g in range(1, G):
                if g + 1 < G:
                    last_gain(g + 1)
                add_ffn(g)
                ln_norm(2 * G + g - 1, g - 1)
            ln_norm(3 * G - 1, G - 1)
            BLINKS = 4

            def lower_bands(u, a, b):
                for k in range(2):
                    last = nc.vector.tensor_scalar(band[:, k, a:b], scores[:, u, a:b], BAND_EDGES[k] / SCALE1,
                                                   BAND_STEPS[k], ALU.is_ge, ALU.mult)
                return last

            def bands(j, slot, at, i=None, t=None):
                u = slot % 2
                s = scores[:, u, :]
                if type(j) is int and j == 0:
                    dve.wait_ge(s1_ready, 1)
                    lower_bands(u, 0, HALF)
                    dve.wait_ge(s1_ready, HALVES)
                    lower_bands(u, HALF, S).then_inc(dve_chain, 1)
                else:
                    dve.wait_ge(s1_ready, j * HALVES + HALVES)
                    lower_bands(u, 0, S).then_inc(dve_chain, 1)
                if i is not None:
                    add_attention(i, t)
                    dve.wait_ge(attn1_added, i + 1)
                dve.wait_ge(dve_chain, at + 1)
                nc.vector.tensor_tensor(band_sum[:, 0, :], band[:, 0, :], band[:, 1, :], ALU.add)
                if i is not None:
                    nc.vector.bn_stats(st[:, 3 * T + t, :], attended[:, t, :]).then_inc(bn_done, 1)
                dve.wait_ge(signs_ready, j + 1)
                nc.vector.tensor_tensor(band[:, 2, :], sign[:, u, 0, :], sign[:, u, 1, :], ALU.add)\
                  .then_inc(dve_chain, 1)
                dve.wait_ge(dve_chain, at + 2)
                if i is not None:
                    dve.wait_ge(bn_done, i + 1)
                nc.vector.tensor_scalar(band_sum[:, 1, :], band[:, 2, :], BAND_STEPS[2], BAND_BASE,
                                        ALU.mult, ALU.add).then_inc(dve_chain, 1)
                if i is not None:
                    last = nc.vector.bn_aggr(mv[:, 3 * T + t, :], st[:, 3 * T + t, :])
                    if t == TPC - 1:
                        last.then_inc(stats_ready, 1)
                dve.wait_ge(dve_chain, at + 3)
                nc.vector.tensor_tensor(mult[:, :], band_sum[:, 0, :], band_sum[:, 1, :], ALU.add)\
                  .then_inc(dve_chain, 1)
                dve.wait_ge(dve_chain, at + 4)
                if type(j) is not int or j > 0:
                    dve.wait_ge(exp1_done, j)
                    before = (slot + TPC - 1) % TPC
                    nc.vector.reciprocal(rinv1[:, before:before + 1], rsum1[:, 1 - u:2 - u])
                nc.vector.tensor_tensor_reduce(out=probs[:, u, :], in0=mult[:, :], in1=s, scale=1.0,
                                               scalar=-3.0e38, op0=ALU.mult, op1=ALU.max,
                                               accum_out=max1[:, u:u + 1]).then_inc(max1_ready, 1)

            def add_attention(i, t):
                dve.wait_ge(attn1_psum, i + 1)
                nc.vector.scalar_tensor_tensor(out=attended[:, t, :], in0=bank[6 + t % 2][:, 0:P],
                                               scalar=rinv1[:, t:t + 1],
                                               in1=xres[:, bass.ds(i, 1), :].rearrange("p a d -> p (a d)"),
                                               op0=ALU.mult, op1=ALU.add).then_inc(attn1_added, 1)

            def last_norm(g):
                dve.wait_ge(rstd_ready, g + (3 * G + 1))
                for t in range(TPC):
                    k = 3 * T + t
                    last = nc.vector.tensor_scalar(nrm[:, bass.ds(g, 1), t, :].rearrange("p a d -> p (a d)"),
                                                   attended[:, t, :], mv[:, k, 0:1], rstd[:, k:k + 1],
                                                   ALU.subtract, ALU.mult)
                last.then_inc(norm_ready, 1)

            base = links[0]
            bands(0, 0, base)
            bands(1, 1, base + BLINKS)
            bands(2, 2, base + 2 * BLINKS)
            dve.wait_ge(res_biased, 2 * G)
            dve.wait_ge(lnT_psum, G)
            with dve.Fori(0, G - 1) as g:
                for t in range(TPC):
                    if t == 0:
                        dve.wait_ge(res_biased, g + 2 * G)
                        dve.wait_ge(norm_ready, g + 3 * G)
                    bands(g * TPC + (t + 3), (t + 3) % TPC, g * (TPC * BLINKS) + (base + BLINKS * (t + 3)),
                          g * TPC + t, t)
                last_norm(g)
            dve.wait_ge(res_biased, 3 * G - 1)
            dve.wait_ge(norm_ready, 4 * G - 1)
            bands(T - 1, TPC - 1, base + BLINKS * (T - 1), T - TPC, 0)
            links[0] = base + BLINKS * T

            def lrelu_double(n):
                dve.wait_ge(relu_ready, n + 1)
                link(nc.vector.tensor_tensor(lrelu2[n % 2], bank[FC_BANK[n % 3]], relu_h[n % 3], ALU.add))

            def choose(part, a, b):
                n = b - a
                dve.wait_ge(lg_psum, part + 1)
                link(nc.vector.tensor_copy(lg[:, a:b, :], bank[LOGIT_BANK][:, a * EXPERTS:b * EXPERTS]
                                           .rearrange("p (t e) -> p t e", t=n)))
                link(nc.vector.reduce_max(lgmax[:, a:b], lg[:, a:b, :], AX.X))
                link(nc.vector.tensor_tensor(ranked[:, a:b, :], lg[:, a:b, :],
                                             lgmax[:, a:b].unsqueeze(2).to_broadcast([P, n, EXPERTS]), ALU.is_ge))
                link(nc.vector.tensor_tensor(ranked[:, a:b, :], ranked[:, a:b, :], tie_rank[:, a:b, :], ALU.mult))
                link(nc.vector.reduce_max(best[:, a:b], ranked[:, a:b, :], AX.X))
                nc.vector.tensor_tensor(onehot[:, a:b, :], ranked[:, a:b, :],
                                        best[:, a:b].unsqueeze(2).to_broadcast([P, n, EXPERTS]), ALU.is_equal)\
                  .then_inc(onehot_ready, 1)

            add_attention(T - 3, 1)
            choose(0, 0, T - TPC)
            dve.wait_ge(exp1_done, T)
            link(nc.vector.reciprocal(rinv1[:, TPC - 1:TPC], rsum1[:, 1:2]))
            add_attention(T - 2, 2)
            lrelu_double(0)
            add_attention(T - 1, TPC - 1)
            dve.wait_ge(attn1_added, T)
            for t in range(1, TPC):
                last = nc.vector.bn_stats(st[:, 3 * T + t, :], attended[:, t, :])
            last.then_inc(bn_done, 1)
            dve.wait_ge(bn_done, T - 2)
            for t in range(1, TPC):
                last = nc.vector.bn_aggr(mv[:, 3 * T + t, :], st[:, 3 * T + t, :])
            last.then_inc(stats_ready, 1)

            def add_experts(g):
                dve.wait_ge(moe_psum, (g + 1) * TPC)
                dve.wait_ge(res_biased, 3 * G)
                xs = xres[:, g * TPC:(g + 1) * TPC, :]
                nc.vector.tensor_tensor(xs, xs, bank[OUT_BANK[g % 2]].rearrange("p (t e) -> p t e", t=TPC), ALU.add)\
                  .then_inc(out_ready, 1)

            for g in range(G):
                for c in range(TPC):
                    n = g * TPC + c
                    if n >= 1:
                        lrelu_double(n)
                    dve.wait_ge(mask_psum, n + 1)
                    if n >= 3:
                        dve.wait_ge(act_ready, n - 2)
                    nc.vector.tensor_tensor(picked[n % 3], lrelu2[n % 2], bank[PICK_BANK[n % 2]], ALU.mult)\
                      .then_inc(picked_ready, 1)
                    if n == 1:
                        last_norm(G - 1)
                    if n == 8:
                        choose(1, T - TPC, T)
                    if c == 3 and g >= 1:
                        add_experts(g - 1)
            add_experts(G - 1)

        @block.tensor
        def _(pe):
            mm = nc.tensor.matmul
            tr = nc.tensor.transpose

            def mod_column(dst, n, j):
                return mm(dst, wmod[:, n, j * P:(j + 1) * P], silu_b[:, n, 0:1], start=True, stop=True)

            def mod_row(dst, n, j):
                return mm(dst, silu_b[:, n, :], wmod[:, n, j * P:(j + 1) * P], start=True, stop=True)

            pe.wait_ge(silu_ready, 1)
            pe.wait_ge(ld_wmod[0], 16)
            mod_column(bank[1][:, 0:1], 0, 0)
            mod_column(bank[1][:, 1:2], 0, 1)
            mod_row(bank[2][:, 0:P], 0, 2).then_inc(mod_psum, 1)
            pe.wait_ge(ident_ready, 1)
            pe.wait_ge(ld_attn0, 48)
            for n in range(3):
                last = tr(bank[0][:, n * P:(n + 1) * P], wqkv0_raw[:, n, :], ident[:, :])
            last.then_inc(w0T_psum, 1)

            def ln_transpose(n, dst):
                pe.wait_ge(norm_ready, n + 1)
                for t in range(TPC):
                    last = tr(dst[:, t * P:(t + 1) * P], nrm[:, n % G, t, :], ident[:, :])
                return last

            def side_job(j):
                if j > 4:
                    pe.wait_ge(side_ready, j)
                g, what, dst = j // 4, j % 4, side_bank(j)
                if j >= QKV_JOBS:
                    last = ln_transpose(G + j - QKV_JOBS, dst)
                elif what == 0:
                    last = ln_transpose(g, dst)
                elif what == 3:
                    for t in range(TPC):
                        last = mm(dst[:, t * P:(t + 1) * P], hT[:, g * C + t * P:g * C + (t + 1) * P],
                                  wqkvT0[:, 2, :], start=True, stop=True)
                else:
                    last = mm(dst, wqkvT0[:, what - 1, :], hT[:, g * C:(g + 1) * C], start=True, stop=True)
                last.then_inc(side_psum, 1)

            side_job(0)
            pe.wait_ge(w0T_ready, 1)
            pe.wait_ge(side_ready, 1)
            side_job(1)
            side_job(2)
            pe.wait_ge(mod_ready, 2)
            side_job(3)

            def mod_rest():
                pe.wait_ge(ld_wmod[1], 16)
                pe.wait_ge(ld_wmod[2], 16)
                for k, (n, j) in enumerate(REST):
                    mod_column(bank[7][:, k:k + 1], n, j)
                mod_row(bank[7][:, P:2 * P], 1, 2)
                mod_row(bank[7][:, 2 * P:3 * P], 1, 5).then_inc(mod_psum, 1)

            def score_chunks(i):
                for c in range(nchunks(i)):
                    q = first_chunk(i) + c
                    w = width(i, c)
                    if q >= SRING:
                        pe.wait_ge(exp_done, q - SRING + 1)
                    diagonal = c == nchunks(i) - 1
                    last = mm(bank[q % SRING][:, 0:w], qT[:, i * P:(i + 1) * P], kT[:, c * C:c * C + w],
                              start=True, stop=not diagonal)
                    if diagonal:
                        last = mm(bank[q % SRING][:, w - P:w], identb[:, :], causal[:, :], start=False, stop=True)
                    last.then_inc(score_psum, 1)

            def transpose_probs(i, c):
                q = first_chunk(i) + c
                pe.wait_ge(exp_done, q + 1)
                if q >= 2:
                    pe.wait_ge(pT_ready, q - 1)
                for b in range(width(i, c) // P):
                    last = tr(bank[5 + q % 2][:, b * P:(b + 1) * P],
                              probs0[i % 3][:, c * C + b * P:c * C + (b + 1) * P], ident[:, :])
                last.then_inc(pT_psum, 1)

            def weigh_values(i, c):
                q = first_chunk(i) + c
                pe.wait_ge(pT_ready, q + 1)
                if c == 0 and i == 0:
                    pe.wait_ge(mod_fetched, 1)
                if c == 0 and i >= 1:
                    pe.wait_ge(attn_added, i)
                for b in range(width(i, c) // P):
                    k = c * TPC + b
                    last = mm(bank[7][:, 0:P], pT[:, q % 2, b, :], v[:, k, :], start=(k == 0), stop=(k == i))
                if c == nchunks(i) - 1:
                    last.then_inc(attn_psum, 1)

            def later_weights():
                pe.wait_ge(ld_l1, 96)
                pe.wait_ge(ld_moe, 96)
                for c in range(TPC):
                    tr(bank[0][:, c * P:(c + 1) * P], wfc_raw[:, c, :], ident[:, :])
                    tr(bank[1][:, c * P:(c + 1) * P],
                       wpr_raw[:, 2 * c:2 * c + 2, :].rearrange("p u h -> p (u h)"), ident[:, :])
                tr(bank[2][:, 0:P], wqkv1[:, 2, :], ident[:, :])
                tr(bank[2][:, P:P + EXPERTS], wr_raw[:, :], ident[0:EXPERTS, 0:EXPERTS]).then_inc(w1T_psum, 1)

            pe.wait_ge(side_ready, 4)
            pe.wait_ge(causal_ready, 1)
            score_chunks(0)
            score_chunks(1)
            side_job(4)
            mod_rest()
            for i in range(T):
                n = nchunks(i)
                for c in range(min(2, n)):
                    transpose_probs(i, c)
                if i < SIDE_STEPS:
                    side_job(5 + i)
                for j in tiles_ahead(i):
                    score_chunks(j)
                for c in range(n):
                    if i == T - 1 and c == n - 1:
                        later_weights()
                    weigh_values(i, c)
                    if c + 2 < n:
                        transpose_probs(i, c + 2)

            pe.wait_ge(consts_ready, 1)
            pe.wait_ge(ffn_w_ready, 1)
            def layer1(r, u, cyc):
                k = chunk_of(r, u)
                pe.wait_ge(y_ready[r], cyc * 2 + (u + 1))
                mm(bank[2 * r + u], w1s[:, :],
                   ybuf[:, bass.ds(cyc, 1), k * C:(k + 1) * C].rearrange("p a t -> p (a t)"),
                   start=True, stop=True).then_inc(h1_psum[r], 1)

            def twisted(k):
                mm(bank[TWIST_BANK[k]], twist[:, :], yT[:, k * C:(k + 1) * C], start=True, stop=True)\
                  .then_inc(tw_psum, 1)

            twisted(0)
            twisted(1)
            pe.wait_ge(wv1T_ready, 1)
            layer1(1, 0, 0)
            layer1(1, 1, 0)
            pe.wait_ge(attn_added, T)
            twisted(2)
            side_job(T + 3)
            pe.wait_ge(side_ready, QKV_JOBS + G)
            pe.wait_ge(wmoe_ready, 1)
            twisted(3)
            layer1(0, 0, 0)

            def layer2(r, cyc):
                for u in range(2):
                    pe.wait_ge(h1_ready[r], cyc * 2 + (u + 1))
                    last = mm(bank[4 + r][u * H2:(u + 1) * H2, :], w2s[:, :], a1[:, r, u, :], start=True, stop=True)
                last.then_inc(h2_psum[r], 1)

            def layer3(r, cyc):
                pe.wait_ge(h2_ready[r], cyc + 1)
                mm(bank[4 + r][0:2 * H3, :], w3s[:, :], a2[:, r, :], start=True, stop=True).then_inc(h3_psum[r], 1)

            def layer4(r, cyc):
                pe.wait_ge(h3_ready[r], cyc + 1)
                for u in range(2):
                    mm(bank[(6, 2)[r] + u], w4b[u * H3:(u + 1) * H3, :], a3[u * H3:(u + 1) * H3, r, :],
                       start=True, stop=True).then_inc(z_psum[r], 1)

            def context_layer(k):
                pe.wait_ge(*((ctx_ready, 1) if k == 0 else (gc_ready, k)))
                w, a, m = ((g1s, ctx_mean, H2), (g2s, g_a1, H3), (g3b, g_a2, P))[k]
                mm(bank[CONTEXT_BANK][0:m, 0:1], w[:, :], a[:, :], start=True, stop=True).then_inc(gc_psum, 1)

            pe.wait_ge(tw_ready, G - 1)
            layer2(1, 0)
            context_layer(0)
            pe.wait_ge(tw_ready, G)
            layer1(0, 1, 0)
            context_layer(1)
            mm(bank[4][:, 0:P], wvT1[:, :], wproj1[:, :], start=True, stop=True)
            mm(bank[4][:, P:2 * P], bv1_b[:, :], wproj1[:, :], start=True, stop=True).then_inc(wvp_psum, 1)
            context_layer(2)
            pe.wait_ge(wvp_ready, 1)

            with pe.Fori(0, CYCLES - 1) as cyc:
                layer3(1, cyc)
                layer2(0, cyc)
                layer4(1, cyc)
                layer3(0, cyc)
                layer4(0, cyc)
                for r, u in ((1, 0), (1, 1), (0, 0)):
                    layer1(r, u, cyc + 1)
                layer2(1, cyc + 1)
                layer1(0, 1, cyc + 1)

            def output(g):
                r, u = 1 - g // 2, g % 2
                pe.wait_ge(gain_ready, g + 1)
                for t in range(TPC):
                    dst = bank[FFN_OUT_BANK[g]][:, t * P:(t + 1) * P]
                    last = mm(dst, yT_last[:, g * C + t * P:g * C + (t + 1) * P], gb0_diag[:, :], start=True, stop=(g < 2))
                    if g >= 2:
                        last = mm(dst, gain[:, r, u, t * P:(t + 1) * P], gb0_diag[:, :], start=False, stop=True)
                last.then_inc(ffnT_psum, 1)

            layer3(1, CYCLES - 1)
            layer2(0, CYCLES - 1)
            layer4(1, CYCLES - 1)
            layer3(0, CYCLES - 1)
            layer4(0, CYCLES - 1)
            output(0)
            output(1)
            output(2)

            def features(dst, g, n):
                return mm(dst, wqkv1[:, n, :], hT[:, g * C:(g + 1) * C], start=True, stop=True)

            def kv_job(n):
                what, g, b = KV_JOBS[n]
                before = [m for m in range(n) if KV_JOBS[m][2] == b]
                if before:
                    pe.wait_ge(kv_ready, before[-1] + 1)
                pe.wait_ge(lnT_ready, g + 1)
                if what == "v":
                    for t in range(TPC):
                        last = mm(bank[b][:, t * P:(t + 1) * P], hT[:, g * C + t * P:g * C + (t + 1) * P],
                                  wvp1[:, :], start=True, stop=True)
                else:
                    last = features(bank[b], g, "qk".index(what))
                last.then_inc(kv_psum, 1)

            def first_norm(g):
                if g >= 2:
                    pe.wait_ge(lnT_ready, g - 1)
                ln_transpose(2 * G + g, bank[6 + g % 2]).then_inc(lnT_psum, 1)

            def early_scores(h, n):
                pe.wait_ge(kv_ready, n)
                for c in range(2 * h, 2 * h + 2):
                    last = mm(bank[c], qbuf[:, 0, :], kT[:, c * C:(c + 1) * C], start=True, stop=True)
                last.then_inc(s1_psum, 1)

            pe.wait_ge(th_ready[0], 2 * CYCLES)
            pe.wait_ge(th_ready[1], 2 * CYCLES)
            first_norm(0)
            output(3)
            for n in range(3):
                kv_job(n)
            first_norm(1)
            kv_job(3)
            kv_job(4)
            first_norm(2)
            kv_job(5)
            first_norm(3)
            pe.wait_ge(q1_ready, 1)
            early_scores(0, 4)
            kv_job(6)
            early_scores(1, 7)
            kv_job(7)
            kv_job(8)

            def score_tile(j, u):
                pe.wait_ge(q1_ready, j + 1)
                for h in range(HALVES):
                    pe.wait_ge(s1_ready, (j - 1) * HALVES + (h + 1))
                    for c in range(2 * h, 2 * h + 2):
                        last = mm(bank[c], qbuf[:, u, :], kT[:, c * C:(c + 1) * C], start=True, stop=True)
                    last.then_inc(s1_psum, 1)

            def turn(j, u, h, first=False):
                if h == 0:
                    pe.wait_ge(exp1_done, j + 1)
                if not (first and h == 0):
                    pe.wait_ge(p1T_ready, j * HALVES + h)
                for k in range(HALF // P):
                    last = tr(turn2[:, k // TPC, k % TPC * P:(k % TPC + 1) * P],
                              probs[:, u, h * HALF + k * P:h * HALF + (k + 1) * P], ident[:, :])
                last.then_inc(p1T_psum, 1)

            def weigh(j, u, h, early=False):
                if h == 0 and not early:
                    pe.wait_ge(attn1_added, j - 1)
                pe.wait_ge(p1T_ready, j * HALVES + (h + 1))
                for k in range(h * HALF // P, (h + 1) * HALF // P):
                    last = mm(bank[6 + u][:, 0:P], pT[:, k // TPC, k % TPC, :], v[:, k, :],
                              start=(k == 0), stop=(k == T - 1))
                if h == 1:
                    last.then_inc(attn1_psum, 1)

            def attend(j, u, start=False, early=False, meanwhile=None):
                turn(j, u, 0, first=start)
                if not start:
                    weigh(j - 1, 1 - u, 1)
                if meanwhile:
                    meanwhile()
                turn(j, u, 1)
                weigh(j, u, 0, early)

            score_tile(1, 1)
            kv_job(9)
            kv_job(10)
            score_tile(2, 0)
            kv_job(11)
            attend(0, 0, start=True, early=True)
            score_tile(3, 1)
            attend(1, 1, early=True)
            with pe.Fori(1, T // 2 - 2) as pair:
                for u in range(2):
                    score_tile(pair * 2 + (2 + u), u)
                    attend(pair * 2 + u, u)

            def logits(g):
                pe.wait_ge(lnT_ready, G + g + 1)
                for t in range(TPC):
                    k = g * TPC + t
                    last = mm(bank[LOGIT_BANK][:, k * EXPERTS:(k + 1) * EXPERTS], hT[:, k * P:(k + 1) * P], wrT[:, :],
                              start=True, stop=True)
                return last

            def expand(n):
                g, c = n // TPC, n % TPC
                if n >= 3:
                    pe.wait_ge(picked_ready, n - 2)
                mm(bank[FC_BANK[n % 3]], wfcT[:, c, :], hT[:, g * C:(g + 1) * C], start=True, stop=True).then_inc(fc_psum, 1)

            def pick(n):
                g, c = n // TPC, n % TPC
                if n >= 2:
                    pe.wait_ge(picked_ready, n - 1)
                mm(bank[PICK_BANK[n % 2]], expert_sel[:, c, :, :].rearrange("p u h -> p (u h)"),
                   ohT[:, g * C:(g + 1) * C], start=True, stop=True).then_inc(mask_psum, 1)

            def contract(n):
                g, c = n // TPC, n % TPC
                pe.wait_ge(act_ready, n + 1)
                if c == 0 and g >= 2:
                    pe.wait_ge(out_ready, g - 1)
                for t in range(TPC):
                    last = mm(bank[OUT_BANK[g % 2]][:, t * P:(t + 1) * P], act2[:, g % 2, c, t * P:(t + 1) * P],
                              wpr[:, c, :], start=(c == 0 and t == 0),
                              stop=(c == TPC - 1 and t == TPC - 1))
                last.then_inc(moe_psum, 1)

            def turn_onehot(h):
                a, b = ONEHOT_PARTS[h]
                pe.wait_ge(onehot_ready, 1 if h < 2 else 2)
                for t in range(a, b):
                    last = tr(onehot_psum(h)[:, (t - a) * P:(t - a + 1) * P], onehot[:, t, :], identb[:, :])
                last.then_inc(ohT_psum, 1)

            def turn_onehot(h):
                a, b = ONEHOT_PARTS[h]
                pe.wait_ge(onehot_ready, 1 if h < 2 else 2)
                for t in range(a, b):
                    last = tr(onehot_psum(h)[:, (t - a) * P:(t - a + 1) * P], onehot[:, t, :], identb[:, :])
                last.then_inc(ohT_psum, 1)

            for j in (T - 4, T - 3):
                score_tile(j + 2, j % 2)
                attend(j, j % 2)
            pe.wait_ge(s1_ready, HALVES * T)
            for g in range(G - 1):
                ln_transpose(3 * G + g, LAST_LN_BANK[g]).then_inc(lnT_psum, 1)
            attend(T - 2, 0)
            logits(0)
            logits(1)
            logits(2).then_inc(lg_psum, 1)
            expand(0)
            expand(1)

            def turn_first_onehots():
                turn_onehot(0)
                turn_onehot(1)

            attend(T - 1, 1, meanwhile=turn_first_onehots)
            weigh(T - 1, 1, 1)
            pe.wait_ge(attn1_added, T - 1)
            expand(2)
            pe.wait_ge(ohT_ready, 2)
            N = G * TPC
            for n in range(N):
                if n == 6:
                    logits(G - 1).then_inc(lg_psum, 1)
                if n == 10:
                    turn_onehot(2)
                if n == N - TPC:
                    pe.wait_ge(ohT_ready, 3)
                pick(n)
                if n >= 3:
                    contract(n - 3)
                if n == 3:
                    ln_transpose(4 * G - 1, LAST_LN_BANK[3]).then_inc(lnT_psum, 1)
                if 1 <= n < N - 2:
                    expand(n + 2)
            for n in range(N - 3, N):
                contract(n)


_INS = ['L0_attn_x', 'L0_attn_Wq', 'L0_attn_bq', 'L0_attn_Wk', 'L0_attn_bk', 'L0_attn_Wv', 'L0_attn_bv',
        'L0_ffn_cn_w1', 'L0_ffn_cn_b1', 'L0_ffn_cn_w2', 'L0_ffn_cn_b2', 'L0_ffn_cn_w3', 'L0_ffn_cn_b3',
        'L0_ffn_cn_w4', 'L0_ffn_cn_b4', 'L0_ffn_gc_w1', 'L0_ffn_gc_b1', 'L0_ffn_gc_w2', 'L0_ffn_gc_b2',
        'L0_ffn_gc_w3', 'L0_ffn_gc_b3', 'L0_ffn_adaptive_range', 'L0_c', 'L0_wmod', 'L1_attn_W_qkv',
        'L1_attn_b_qkv', 'L1_attn_W_proj', 'L1_attn_b_proj', 'L1_ffn_w_router', 'L1_ffn_w_fc', 'L1_ffn_w_proj',
        'L1_c', 'L1_wmod']


def kernel(**inputs):
    import numpy as np
    import concourse.bacc as bacc
    from concourse.bass_utils import run_bass_kernel_spmd

    nc = bacc.Bacc("TRN2", target_bir_lowering=False, num_devices=1)
    arrays, args = {}, []
    for name in _INS:
        a = np.ascontiguousarray(inputs[name])
        arrays[f"in_{name}"] = a
        args.append(nc.dram_tensor(f"in_{name}", a.shape, mybir.dt.from_np(a.dtype), kind="ExternalInput").ap())
    shape = inputs['L0_attn_x'].shape
    args.append(nc.dram_tensor("out", shape, F32, kind="ExternalOutput").ap())
    build(nc, *args)
    r = run_bass_kernel_spmd(nc, [arrays], core_ids=[0])
    return r.results[0]["out"]
```
